# Optimizing a Trainium2 kernel written in Bass

```python
import numpy as np
import jax
import jax.numpy as jnp

def _softmax(x, axis=-1):
    return jax.nn.softmax(x, axis=axis)

def _gelu(x):
    return jax.nn.gelu(x, approximate=True)

def _silu(x):
    return jax.nn.silu(x)

def _sigmoid(x):
    return jax.nn.sigmoid(x)

def _layernorm(x, axis=-1, eps=1e-05):
    m = jnp.mean(x, axis=axis, keepdims=True)
    v = jnp.var(x, axis=axis, keepdims=True)
    return (x - m) / jnp.sqrt(v + eps)

def _scatter_add(tgt, idx, src, axis=0):
    return tgt.at[idx].add(src)

def _segment_sum(src, seg, n):
    return jax.ops.segment_sum(src, seg, n)
kernel_name = 'mk_gps_d1_gnn_r8_b936cd'

def setup_inputs(seed: int=0):
    np.random.seed(seed)
    _w = jnp.asarray

    def _rec_inputs():
        import jax
        import jax.numpy as jnp
        _gk = jax.random.key(seed)
        x = -8.776e-05 + 1 * jax.random.normal(jax.random.fold_in(_gk, 1), (6250, 256), jnp.float32)
        src = jax.random.randint(jax.random.fold_in(_gk, 2), (200000,), 0, 6250, jnp.int32)
        dst = jax.random.randint(jax.random.fold_in(_gk, 3), (200000,), 0, 6250, jnp.int32)
        _o = jnp.argsort(dst, stable=True)
        src = src[_o]
        dst = dst[_o]
        return (x, src, dst)
    x, src, dst = _rec_inputs()

    def _L0_gnn_setup():
        import jax, jax.numpy as jnp
        import numpy as np
        N = 2500
        E = 40000
        IN_F = 256
        HEADS = 4
        OUT_F = 64
        NEG_SLOPE = 0.2

        def _leaky_relu(v):
            return jnp.where(v > 0, v, NEG_SLOPE * v)
        key = jax.random.key(seed)
        k1, k2, k3, k4 = jax.random.split(key, 4)
        x = jax.random.normal(k1, (N, IN_F), dtype=jnp.float32)
        edge_index = jax.random.randint(k2, (2, E), 0, N, dtype=jnp.int64)
        W = jax.random.normal(k3, (IN_F, HEADS * OUT_F), dtype=jnp.float32) * (1.0 / np.sqrt(IN_F))
        att = jax.random.normal(k4, (1, HEADS, 2 * OUT_F), dtype=jnp.float32) * 0.1
        b = jnp.zeros((HEADS * OUT_F,), dtype=jnp.float32)
        return {'x': x, 'W': W, 'att': att, 'b': b, 'edge_index': edge_index}
    _L0_gnn_all = _L0_gnn_setup()
    _L0_gnn_in = {k: v for k, v in _L0_gnn_all.items() if k in ('W', 'att', 'b')}
    del _L0_gnn_all

    def _L0_mix_setup():
        import jax, jax.numpy as jnp
        import numpy as np
        B, S, D = (8, 256, 256)
        H, KD = (8, 256)
        M = 256
        EPS_LN = 1e-06
        EPS_ATT = 1e-06

        def _layernorm(x, g, b):
            mu = jnp.mean(x, axis=-1, keepdims=True)
            var = jnp.mean(jnp.square(x - mu), axis=-1, keepdims=True)
            return (x - mu) * jax.lax.rsqrt(var + EPS_LN) * g + b

        def _phi(x, proj):
            u = jnp.einsum('bshd,md->bshm', x, proj)
            sq = 0.5 * jnp.sum(jnp.square(x), axis=-1, keepdims=True)
            return jnp.exp(u - sq) * (1.0 / np.sqrt(M)) + EPS_ATT
        key = jax.random.key(seed)
        ks = jax.random.split(key, 16)
        sd = lambda *s: 1.0 / np.sqrt(s[0])
        return {'inputs': jax.random.normal(ks[0], (B, S, D), dtype=jnp.float32), 'Wq': jax.random.normal(ks[1], (D, H, KD), jnp.float32) * sd(D), 'bq': jnp.zeros((H, KD), jnp.float32), 'Wk': jax.random.normal(ks[2], (D, H, KD), jnp.float32) * sd(D), 'bk': jnp.zeros((H, KD), jnp.float32), 'Wv': jax.random.normal(ks[3], (D, H, KD), jnp.float32) * sd(D), 'bv': jnp.zeros((H, KD), jnp.float32), 'Wo': jax.random.normal(ks[4], (H, KD, D), jnp.float32) * sd(H * KD), 'bo': jnp.zeros((D,), jnp.float32), 'proj': jax.random.normal(ks[5], (M, KD), jnp.float32), 'W1': jax.random.normal(ks[6], (D, D), jnp.float32) * sd(D), 'bias1': jnp.zeros((D,), jnp.float32), 'W2': jax.random.normal(ks[7], (D, D), jnp.float32) * sd(D), 'bias2': jnp.zeros((D,), jnp.float32), 'g1': jnp.ones((D,), jnp.float32), 'beta1': jnp.zeros((D,), jnp.float32), 'g2': jnp.ones((D,), jnp.float32), 'beta2': jnp.zeros((D,), jnp.float32)}
    _L0_mix_all = _L0_mix_setup()
    _L0_mix_in = {k: v for k, v in _L0_mix_all.items() if k in ('Wq', 'bq', 'Wk', 'bk', 'Wv', 'bv', 'Wo', 'bo', 'proj', 'W1', 'bias1', 'W2', 'bias2', 'g1', 'beta1', 'g2', 'beta2')}
    del _L0_mix_all

    def _L0_ffn_setup():
        import math
        import jax, jax.numpy as jnp
        import numpy as np
        CAPACITY_FACTOR = 1.25
        key = jax.random.key(seed)
        ks = jax.random.split(key, 5)
        B, L, D, F, E = (8, 1024, 256, 1024, 8)
        h = jax.random.normal(ks[0], (B, L, D), dtype=jnp.float32)
        gate_w = jax.random.normal(ks[1], (D, E), dtype=jnp.float32) * 0.02
        gate_b = jnp.zeros((E,), dtype=jnp.float32)
        w1 = jax.random.normal(ks[2], (E, D, F), dtype=jnp.float32) * (1.0 / math.sqrt(D))
        b1 = jnp.zeros((E, F), dtype=jnp.float32)
        w2 = jax.random.normal(ks[3], (E, F, D), dtype=jnp.float32) * (1.0 / math.sqrt(F))
        b2 = jnp.zeros((E, D), dtype=jnp.float32)
        return {'h': h, 'gate_w': gate_w, 'gate_b': gate_b, 'w1': w1, 'b1': b1, 'w2': w2, 'b2': b2}
    _L0_ffn_all = _L0_ffn_setup()
    _L0_ffn_in = {k: v for k, v in _L0_ffn_all.items() if k in ('gate_w', 'gate_b', 'w1', 'b1', 'w2', 'b2')}
    del _L0_ffn_all
    return {'x': x, 'src': src, 'dst': dst, 'L0_gnn_W': _L0_gnn_in['W'], 'L0_gnn_att': _L0_gnn_in['att'], 'L0_gnn_b': _L0_gnn_in['b'], 'L0_mix_Wq': _L0_mix_in['Wq'], 'L0_mix_bq': _L0_mix_in['bq'], 'L0_mix_Wk': _L0_mix_in['Wk'], 'L0_mix_bk': _L0_mix_in['bk'], 'L0_mix_Wv': _L0_mix_in['Wv'], 'L0_mix_bv': _L0_mix_in['bv'], 'L0_mix_Wo': _L0_mix_in['Wo'], 'L0_mix_bo': _L0_mix_in['bo'], 'L0_mix_proj': _L0_mix_in['proj'], 'L0_mix_W1': _L0_mix_in['W1'], 'L0_mix_bias1': _L0_mix_in['bias1'], 'L0_mix_W2': _L0_mix_in['W2'], 'L0_mix_bias2': _L0_mix_in['bias2'], 'L0_mix_g1': _L0_mix_in['g1'], 'L0_mix_beta1': _L0_mix_in['beta1'], 'L0_mix_g2': _L0_mix_in['g2'], 'L0_mix_beta2': _L0_mix_in['beta2'], 'L0_ffn_gate_w': _L0_ffn_in['gate_w'], 'L0_ffn_gate_b': _L0_ffn_in['gate_b'], 'L0_ffn_w1': _L0_ffn_in['w1'], 'L0_ffn_b1': _L0_ffn_in['b1'], 'L0_ffn_w2': _L0_ffn_in['w2'], 'L0_ffn_b2': _L0_ffn_in['b2']}

def reference(x, src, dst, L0_gnn_W, L0_gnn_att, L0_gnn_b, L0_mix_Wq, L0_mix_bq, L0_mix_Wk, L0_mix_bk, L0_mix_Wv, L0_mix_bv, L0_mix_Wo, L0_mix_bo, L0_mix_proj, L0_mix_W1, L0_mix_bias1, L0_mix_W2, L0_mix_bias2, L0_mix_g1, L0_mix_beta1, L0_mix_g2, L0_mix_beta2, L0_ffn_gate_w, L0_ffn_gate_b, L0_ffn_w1, L0_ffn_b1, L0_ffn_w2, L0_ffn_b2):
    import jax
    import jax.numpy as jnp

    def _L0_gnn_ref(x, W, att, b, edge_index):
        import jax, jax.numpy as jnp
        import numpy as np
        N = 2500
        E = 40000
        IN_F = 256
        HEADS = 4
        OUT_F = 64
        NEG_SLOPE = 0.2

        def _leaky_relu(v):
            return jnp.where(v > 0, v, NEG_SLOPE * v)
        n = x.shape[0]
        heads = att.shape[1]
        d = att.shape[2] // 2
        loops = jnp.arange(n, dtype=edge_index.dtype)
        src = jnp.concatenate([edge_index[0], loops])
        dst = jnp.concatenate([edge_index[1], loops])
        h = (x @ W).reshape(n, heads, d)
        a_src = att[0, :, :d]
        a_dst = att[0, :, d:]
        h_src = h[src]
        scores = jnp.einsum('ehd,hd->eh', _leaky_relu(h_src), a_src) + jnp.einsum('ehd,hd->eh', _leaky_relu(h[dst]), a_dst)
        w = jax.nn.softmax(scores, axis=0)
        out = jax.ops.segment_sum(h_src * w[:, :, None], dst, num_segments=n)
        return out.reshape(n, heads * d) + b

    def _L0_mix_ref(inputs, Wq, bq, Wk, bk, Wv, bv, Wo, bo, proj, W1, bias1, W2, bias2, g1, beta1, g2, beta2):
        import jax, jax.numpy as jnp
        import numpy as np
        B, S, D = (8, 256, 256)
        H, KD = (8, 256)
        M = 256
        EPS_LN = 1e-06
        EPS_ATT = 1e-06

        def _layernorm(x, g, b):
            mu = jnp.mean(x, axis=-1, keepdims=True)
            var = jnp.mean(jnp.square(x - mu), axis=-1, keepdims=True)
            return (x - mu) * jax.lax.rsqrt(var + EPS_LN) * g + b

        def _phi(x, proj):
            u = jnp.einsum('bshd,md->bshm', x, proj)
            sq = 0.5 * jnp.sum(jnp.square(x), axis=-1, keepdims=True)
            return jnp.exp(u - sq) * (1.0 / np.sqrt(M)) + EPS_ATT
        scale = KD ** (-0.25)
        q = (jnp.einsum('bsd,dhk->bshk', inputs, Wq) + bq) * scale
        k = (jnp.einsum('bsd,dhk->bshk', inputs, Wk) + bk) * scale
        v = jnp.einsum('bsd,dhk->bshk', inputs, Wv) + bv
        phi_q = _phi(q, proj)
        phi_k = _phi(k, proj)
        kv = jnp.einsum('bshm,bshk->bhmk', phi_k, v)
        z = jnp.einsum('bshm,bhm->bsh', phi_q, phi_k.sum(axis=1))
        attn = jnp.einsum('bshm,bhmk->bshk', phi_q, kv) / z[..., None]
        attn_out = jnp.einsum('bshk,hkd->bsd', attn, Wo) + bo
        out1 = _layernorm(inputs + attn_out, g1, beta1)
        h = jax.nn.relu(out1 @ W1 + bias1)
        ffn_out = h @ W2 + bias2
        return _layernorm(out1 + ffn_out, g2, beta2)

    def _L0_ffn_ref(h, gate_w, gate_b, w1, b1, w2, b2):
        import math
        import jax, jax.numpy as jnp
        import numpy as np
        CAPACITY_FACTOR = 1.25
        B, L, D = h.shape
        E = gate_w.shape[1]
        T = B * L
        C = max(1, math.ceil(CAPACITY_FACTOR * T / E))
        x = h.reshape(T, D)
        logits = x @ gate_w + gate_b
        probs = jax.nn.softmax(logits, axis=-1)
        idx = jnp.argmax(probs, axis=-1)
        prb = jnp.take_along_axis(probs, idx[:, None], axis=1)[:, 0]
        one_hot = jax.nn.one_hot(idx, E, dtype=jnp.float32)
        pos = (jnp.cumsum(one_hot, axis=0) * one_hot).sum(-1).astype(jnp.int32) - 1
        kept = pos < C
        pos_safe = jnp.where(kept, pos, C)
        buf = jnp.zeros((E, C, D), dtype=h.dtype).at[idx, pos_safe].set(x, mode='drop')
        hmid = jax.nn.relu(jnp.einsum('ecd,edf->ecf', buf, w1) + b1[:, None, :])
        ybuf = jnp.einsum('ecf,efd->ecd', hmid, w2) + b2[:, None, :]
        pos_g = jnp.minimum(pos, C - 1)
        y_tok = ybuf[idx, pos_g] * (prb * kept)[:, None]
        y = y_tok.reshape(B, L, D)
        y = jnp.nan_to_num(y, nan=0.0, posinf=10000.0, neginf=-10000.0)
        return y
    edge_index = jnp.stack([src, dst])
    xn = _layernorm(x, axis=-1)
    x = x + _L0_gnn_ref(xn, L0_gnn_W, L0_gnn_att, L0_gnn_b, edge_index) + _L0_mix_ref(xn[None], L0_mix_Wq, L0_mix_bq, L0_mix_Wk, L0_mix_bk, L0_mix_Wv, L0_mix_bv, L0_mix_Wo, L0_mix_bo, L0_mix_proj, L0_mix_W1, L0_mix_bias1, L0_mix_W2, L0_mix_bias2, L0_mix_g1, L0_mix_beta1, L0_mix_g2, L0_mix_beta2)[0]
    x = x + _L0_ffn_ref(_layernorm(x, axis=-1)[None], L0_ffn_gate_w, L0_ffn_gate_b, L0_ffn_w1, L0_ffn_b1, L0_ffn_w2, L0_ffn_b2)[0]
    return x

_drawn_inputs = setup_inputs


def setup_inputs(seed=0):
    import zlib

    import numpy as np

    out = dict(_drawn_inputs(seed))
    spreads = {'L0_gnn_b': (0.0, 0.1),
     'L0_mix_bq': (0.0, 0.1),
     'L0_mix_bk': (0.0, 0.1),
     'L0_mix_bv': (0.0, 0.1),
     'L0_mix_bo': (0.0, 0.1),
     'L0_mix_bias1': (0.0, 0.1),
     'L0_mix_bias2': (0.0, 0.1),
     'L0_mix_g1': (1.0, 0.2),
     'L0_mix_beta1': (0.0, 0.1),
     'L0_mix_g2': (1.0, 0.2),
     'L0_mix_beta2': (0.0, 0.1),
     'L0_ffn_gate_b': (0.0, 0.1),
     'L0_ffn_b1': (0.0, 0.8),
     'L0_ffn_b2': (0.0, 0.8)}
    factors = {'L0_gnn_W': 8.0, 'L0_gnn_att': 8.0}
    for name, (base, spread) in spreads.items():
        noise = np.random.default_rng([zlib.crc32(name.encode()), seed]).standard_normal(out[name].shape)
        drawn = base * np.exp(spread * noise) if base else spread * noise
        out[name] = jnp.asarray(drawn.astype(out[name].dtype))
    for name, factor in factors.items():
        out[name] = (out[name] * factor).astype(out[name].dtype)
    return out
```

```python
import math
from contextlib import ExitStack, contextmanager

import concourse.bass as bass
from concourse import mybir

F32, I32 = mybir.dt.float32, mybir.dt.int32
F16, BF16 = mybir.dt.float16, mybir.dt.bfloat16
ALU, ACT, AX = mybir.AluOpType, mybir.ActivationFunctionType, mybir.AxisListType
ds = bass.ds

N, D, E = 6250, 256, 200000
P = 125
NT = N // P
GH, GD = 4, 64
H, M = 8, 256
NE, F = 8, 1024
CAP = -(-5 * N // (4 * NE))
CT = 8
CB = CT * P
LOG16 = 2.772588722239781
LN_EPS, MIX_EPS, PHI_EPS = 1e-5, 1e-6, 1e-6
ROWW = D + GH
SR = 400
NS = E // SR
WIN, BLK = 64, 4
WB = WIN // BLK
SHIFT = 36.0
CH = 5
LCH = 10


@contextmanager
def steps(engine, n, step):
    with engine.Fori(0, n // step) as i:
        yield i * step


def gps_layer(nc, x, src, dst, gW, gatt, gb, Wq, bq, Wk, bk, Wv, bv, Wo, bo, proj, W1, bias1, W2, bias2,
              g1, beta1, g2, beta2, gate_w, gate_b, w1, b1, w2, b2, out):
    ctx = ExitStack()
    with ctx:
        def sb(name, shape, dt=F32):
            return ctx.enter_context(nc.sbuf_tensor(name, shape, dt))

        def sem(name):
            return ctx.enter_context(nc.semaphore(name))

        def scratch(name, shape, dt=F32):
            return nc.dram_tensor(name, shape, dt, kind="Internal").ap()

        table = scratch("gather_table", [N + 1, ROWW])
        srcpad = scratch("src_padded", [E + WIN], I32)
        sums = scratch("neighbour_sums", [NT, P, BLK * ROWW])
        acc = sb("acc", [P, NT, D])
        xa_full = [sb(f"xa{i}", [128, NT, D + 2], F16) for i in (0, 1)]
        xa = [full[0:P] for full in xa_full]
        xt = sb("xt", [128, NT, 4, 128], F16)
        mean = sb("mean", [P, NT])
        rstd = sb("rstd", [P, NT])
        wf = sb("wf", [P, NT, 2 * GH])
        wsum = sb("wsum", [P, NT, BLK, GH])
        ident = sb("ident", [128, 128])
        identh = sb("identh", [128, 128], F16)
        ones = sb("ones", [128, 128])
        spare = sb("spare", [P, 2])
        nones = sb("nones", [1, 128])
        bank = [ctx.enter_context(nc.psum_tensor(f"bank{i}", [128, 512], F32)) for i in range(8)]
        gacc = sb("gacc", [P, 2, BLK, ROWW])
        offi = sb("offi", [P + 1, NT], I32)
        deg = sb("deg", [P, NT])
        nblk = sb("nblk", [1, 5, NT], I32)
        woff = sb("woff", [P, 1], I32)
        wrem = sb("wrem", [P, 1])
        widx = sb("widx", [P, WIN], I32)
        wmask = sb("wmask", [P, WIN])
        wval = sb("wval", [P, WIN])
        gidx = sb("gidx", [P, WIN], I32)
        kpos = sb("kpos", [P, WIN])
        zrow = sb("zrow", [1, ROWW])
        arena = sb("arena", [128, 9720])
        a_off = [0]

        def cut(shape, dt=F32, parts=128, at=None):
            n = math.prod(shape) * (2 if dt in (F16, BF16) else 4)
            o = a_off[0] if at is None else at
            a_off[0] = o + -(-n // 4)
            assert a_off[0] <= 9720, a_off[0]
            v = arena[0:parts, o:o + -(-n // 4)]
            if dt != F32:
                v = v.bitcast(dt)
            if len(shape) == 2:
                v = v.rearrange("p (a b) -> p a b", b=shape[1])
            if len(shape) == 3:
                v = v.rearrange("p (a b c) -> p a b c", b=shape[1], c=shape[2])
            if len(shape) == 4:
                v = v.rearrange("p (a b c d) -> p a b c d", b=shape[1], c=shape[2], d=shape[3])
            return v

        a_off[0] = 0
        st6 = cut([NT, 6], F32, P)
        stt = [cut([NT], F32, P) for _ in range(9)]
        eps = cut([1], F32, P)
        shf = cut([1], F32, P)
        gwf = cut([2, D])
        gw = cut([2, 2, D], F16)
        attb = cut([2, D], F32, P)
        lk = cut([CH, D], F32, P)
        tat_at = a_off[0]
        tat = cut([CH * 2, D], F32, P)
        mx = cut([2 * GH], F32, P)
        mxa = cut([2 * GH], F32, P)
        firsts = cut([NS], F32, P + 1)
        first1 = arena[0:1, tat_at:tat_at + NS].bitcast(I32)
        first1f = arena[0:1, tat_at + NS:tat_at + 2 * NS]
        dq = cut([NT], F32, P + 1)
        cnt1 = cut([NT], F32, P + 1)
        cnt2 = cut([NT], F32, P + 1)
        offf = cut([NT], F32, P + 1)
        ri = cut([NT], I32, P + 1)
        junk = cut([2, 512], F16, P + 1)
        rslot = [cut([1], I32, P + 1) for _ in range(CH)]
        drow = cut([CH, SR], I32, P + 1)
        offT = cut([P + 1], F32, NT)
        degT = cut([P], F32, NT)
        mxd = cut([4], F32, NT)
        nrow = arena[0:1, tat_at:tat_at + 4 * NT].rearrange("p (a b) -> p a b", b=NT)
        nsum = arena[0:1, tat_at + 4 * NT:tat_at + 6 * NT].rearrange("p (a b) -> p a b", b=NT)
        mxi = cut([2], I32, NT)

        a_off[0] = 0
        wc = [cut([2, 2, 2 * D], F16) for _ in (0, 1)]
        bmat = cut([2, D])
        wbase = a_off[0]
        ex = [cut([M], F32, P) for _ in range(4)]
        sqj = [cut([M], F32, P) for _ in range(4)]
        sq = [cut([1], F32, P) for _ in range(4)]
        nsq = [cut([1], F32, P) for _ in range(4)]
        ph = [cut([2, M], BF16, P) for _ in range(4)]
        kvs = cut([2, D + 2])
        kvt = cut([2, M])
        kvo = cut([2, 2, D + 2], BF16)
        qt = [cut([2, 2, 128], BF16) for _ in range(4)]
        rz = [cut([1], F32, P) for _ in range(4)]
        fbank = {"k": [bank[j] for j in (0, 1, 6, 7)], "q": [bank[j] for j in (0, 1, 2, 3)]}
        zero = cut([128], BF16, P)
        mix_end = a_off[0]
        a_off[0] = wbase
        wraw = cut([3, 2, D])
        wo = cut([2, D])
        brow = cut([3, D], F32, 1)
        brow_bo = cut([D], F32, P)
        wt = cut([3, 2, D])
        projr = cut([2, D])
        projt = cut([2, M])
        wcat = scratch("mix_weights", [H, 2, 128, 2 * 2 * 2 * D], F16)
        bdram = scratch("mix_wv_wo", [H, 128, 2 * D])

        a_off[0] = 0
        tst = cut([NT, 6], F32, P)
        tln = [cut([NT], F32, P) for _ in range(8)]
        slot_out = cut([NT], I32, P)
        slot_in = cut([NT], I32, P)
        pk = cut([NT], F32, P)
        b1t = cut([NE, F // 128])
        tail = a_off[0]
        g1b, beta1b, g2b, beta2b, bias2b, gnnb = (cut([D], F32, P) for _ in range(6))
        W1s, W2s = (cut([2, D]) for _ in (0, 1))
        b1r = cut([128], F32, 2)
        bias1t = cut([2])
        gate = cut([2, NE])
        gateb = cut([NE], F32, P)
        xc = [cut([CH, D], F32, P) for _ in (0, 1)]
        fbase = a_off[0]
        ot = [cut([2, 2 * P]) for _ in (0, 1)]
        ht = [cut([2, 2 * P]) for _ in (0, 1)]
        a_off[0] = fbase
        nsum_in = [cut([BLK * ROWW], F32, P) for _ in (0, 1)]
        gn = [cut([D], F32, P) for _ in (0, 1)]
        fz = cut([NT, GH], F32, P)
        zpart = cut([GH], F32, P)
        zall = cut([GH], F32, P)
        wfs = arena[0:P, fbase:fbase + NT * BLK * GH].rearrange("p (t b h) -> p t b h", b=BLK, h=GH)
        lg = cut([NT, NE], F32, P)
        xft = [arena[:, fbase + k * 250:fbase + k * 250 + 250].rearrange("p (a b) -> p a b", a=2) for k in (0, 1)]
        o1 = [xc[k][:, 0:2, :] for k in (0, 1)]
        xfs = [xc[k][:, 0, :] for k in (0, 1)]
        a_off[0] = tail
        rmax, rsum, rinv, ridx, rpos, rkept, rdump, rslot_o, rtmp = (cut([NT], F32, P) for _ in range(9))
        rex, roh, rtot, rscan, rall = (cut([NT, NE], F32, P) for _ in range(5))
        tri = cut([P], F32, P)
        down = cut([NE], F32, P)
        downi = cut([NE], I32, P)
        node = cut([NT], I32, P)
        xs = [cut([D], F32, P) for _ in range(CH)]
        oslot = [cut([1], I32, P) for _ in range(CH)]
        assert a_off[0] < fbase
        a_off[0] = tail
        xe = [cut([4, D], F32, P) for _ in (0, 1)]
        xet = [cut([2, 4 * P]) for _ in (0, 1)]
        hid = cut([F // 128, 4 * P])
        b1rows = arena[0:NE * F // 128, a_off[0] - 4 * P:a_off[0] - 4 * P + 128]
        gflat = gacc[:, :, :, :].rearrange("p a b c -> p (a b c)")
        ye = gflat[:, 0:4 * D].rearrange("p (a b) -> p a b", b=D)
        b2b = [gflat[:, (4 + k) * D:(5 + k) * D] for k in (0, 1)]
        we = []
        for full in xa_full:
            w = full[:, :, :].rearrange("p t d -> p (t d)").bitcast(F32)
            we.append((w[:, 0:2 * F].rearrange("p (a f) -> p a f", a=2), w[:, 2 * F:2 * F + F // 128 * D].rearrange("p (a d) -> p a d", d=D)))
        a_off[0] = tail
        yg = [cut([CH, D], F32, P) for _ in (0, 1)]
        msk = [cut([CH, D], I32, P) for _ in (0, 1)]
        fill = [cut([D], F32, P) for _ in range(3)]
        islot = [cut([1], I32, P) for _ in range(2 * CH)]
        ebuf = scratch("expert_rows", [NE * CB + N, D])
        ybuf = scratch("expert_out", [NE * CB, D])

        S, kept = {}, {}
        def s(name):
            if name in kept:
                return kept[name]
            if name not in S:
                S[name] = nc.alloc_semaphore(name)
            return S[name]

        for name in [f"row_in{k}" for k in range(CH)] + ["widx_in"] + [f"added{j}" for j in range(BLK)] + [f"scattered{k}" for k in range(CH)] + ["yg_in0", "yg_in1"]:
            kept[name] = sem(name)

        def next_part():
            for handle in S.values():
                nc.gpsimd.sem_clear(handle)
                nc.release_semaphore(handle)
            S.clear()
            nc.all_engine_barrier()

        def hold(e, name, value, who="pool"):
            e.wait_ge(s(name), value)
            e.sem_inc(s(who + "_passed"), 1)

        xv = x.rearrange("(t p) d -> p t d", p=P)

        def less(t, n):
            return max(t - n, 0) if isinstance(t, int) else t + -n

        def pipeline(e, stages, n=NT, un=2):
            lag = max(a for a, _ in stages)
            ramp = lag + un - 1
            rounds = (n - ramp) // un
            for t in range(ramp):
                for a, step in stages:
                    if t >= a:
                        step((t - a) % un, (t - a) // un, t - a)
            with e.Fori(0, rounds) as i:
                for u in range(un):
                    for a, step in stages:
                        o = ramp + u - a
                        step(o % un, i + o // un, i * un + o)
            for t in range(ramp + un * rounds, n + lag):
                for a, step in stages:
                    if t - a < n:
                        step((t - a) % un, (t - a) // un, t - a)


        with nc.Block() as block:
            @block.sync
            def _(sp):
                sp.dma_start(first1, dst.rearrange("(a b) -> a b", b=SR)[:, 0:1].rearrange("a b -> b a"), allow_slow_non_contiguous=True).then_inc(s("firsts_in"), 16)
                for c in range(NT // LCH):
                    sp.dma_start(acc[:, c * LCH:(c + 1) * LCH, :], xv[:, c * LCH:(c + 1) * LCH, :]).then_inc(s(f"x_in{c}"), 16)
                sp.dma_start(gwf, gW.rearrange("(a p) n -> p a n", p=128)).then_inc(s("gw_in"), 16)
                av = gatt.rearrange("o h (s d) -> o s h d", s=2)
                for k in (0, 1):
                    sp.dma_start(attb[:, k, :].rearrange("p (h d) -> p h d", d=GD),
                                 av[:, k].broadcast_to([P, GH, GD])).then_inc(s("att_in"), 16)
                sp.dma_start(srcpad[0:E].rearrange("(a b) -> a b", a=16), src.rearrange("(a b) -> a b", a=16)).then_inc(s("src_in"), 16)
                sp.wait_ge(s("zeros_ready"), 1)
                sp.dma_start(srcpad[E:E + WIN].rearrange("(o n) -> o n", o=1), zrow[0:1, 0:WIN].bitcast(I32)).then_inc(s("src_in"), 16)
                sp.dma_start(table[N:N + 1, :], zrow[:, :]).then_inc(s("table_in"), 16)
                tv = table[0:N, :].rearrange("(t p) d -> p t d", p=P)
                sp.wait_ge(s("w_ready"), 1)
                sp.dma_start(tv[:, :, D:D + GH], wf[:, :, 0:GH]).then_inc(s("table_in"), 16)
                with steps(sp, NT, CH) as t:
                    sp.wait_ge(s("g_ready"), t + CH)
                    sp.dma_start(tv[:, ds(t, CH), 0:D], acc[:, ds(t, CH), :]).then_inc(s("table_in"), 16)
                sp.wait_ge(s("gacc_zero"), 1)
                for c in range(NE * CB * D // (P * 8 * D)):
                    sp.dma_start(ebuf[0:NE * CB, :].rearrange("(c p r) d -> c p (r d)", p=P, r=8)[c], gacc[:, :, :, :].rearrange("p a b c -> p (a b c)")[:, 0:8 * D]).then_inc(s("ebuf_zero"), 16)
                sp.wait_ge(s("ebuf_zero"), 16 * (NE * CB // (P * 8)))
                sp.wait_ge(s("table_in"), 16 * (2 + NT // CH))

            @block.gpsimd
            def _(pool):
                pool.memset(zrow[:, :], 0.0).then_inc(s("zeros_ready"), 1)
                pool.memset(gacc[:, :, :, :].rearrange("p a b c -> p (a b c)")[:, 0:8 * D], 0.0).then_inc(s("gacc_zero"), 1)
                pool.memset(ones[:, :], 1.0).then_inc(s("ones_ready"), 1)
                pool.memset(nones[:, :], -1.0).then_inc(s("ones_ready"), 1)
                pool.memset(ident[:, :], 0.0).then_inc(s("id0"), 1)
                pool.wait_ge(s("id0"), 1)
                pool.affine_select(out=ident[:, :], in_=ident[:, :], compare_op=ALU.not_equal, fill=1.0, base=0,
                                   pattern=[[-1, 128]], channel_multiplier=1).then_inc(s("ident_ready"), 1)
                pool.wait_ge(s("ident_ready"), 1)
                pool.tensor_copy(identh[:, :], ident[:, :]).then_inc(s("identh_ready"), 1)
                pool.iota(ri, pattern=[[P, NT]], base=0, channel_multiplier=1).then_inc(s("iotas"), 1)
                pool.iota(gidx[:, :], pattern=[[1, WIN]], base=0, channel_multiplier=0).then_inc(s("iotas"), 1)
                pool.memset(eps, LN_EPS).then_inc(s("eps_ready"), 1)
                pool.memset(shf, SHIFT).then_inc(s("eps_ready"), 1)
                pool.wait_ge(s("iotas"), 2)
                pool.tensor_copy(dq, ri).then_inc(s("dq_ready"), 1)
                pool.tensor_copy(kpos[:, :], gidx[:, :]).then_inc(s("kpos_ready"), 1)
                for k in (0, 1):
                    pool.memset(xa[k][:, :, D:D + 2], 1.0 - k).then_inc(s("xa_ones"), 1)
                pool.wait_ge(s("ri_ready"), 1)
                with steps(pool, NT, CH) as t:
                    for k in range(CH):
                        pool.wait_ge(s("rows_counted"), t)
                        pool.tensor_copy(rslot[k], ri[:, ds(t + k, 1)]).then_inc(s("rslot_ready"), 1)
                        hold(pool, "rslot_ready", t + (k + 1))
                        pool.indirect_dma_start(out=drow[:, k, :], out_offset=None, in_=dst.rearrange("(a b) -> a b", b=SR),
                                                in_offset=bass.IndirectOffsetOnAxis(ap=rslot[k], axis=0)).then_inc(s(f"row_in{k}"), 16)
                pool.wait_ge(s("mx_ready"), 1)
                pool.partition_all_reduce(mxa, mx, P, bass.bass_isa.ReduceOp.max).then_inc(s("mxa_ready"), 1)

                pool.wait_ge(s("nblk_ready"), 1)
                pool.wait_ge(s("deg_ready"), 1)
                pool.wait_ge(s("src_in"), 32)

            @block.vector
            def _(v):
                v.wait_ge(s("firsts_in"), 16)
                v.tensor_copy(first1f, first1).then_inc(s("first1f_ready"), 1)
                v.wait_ge(s("firsts_bcast"), 1)
                v.tensor_copy(firsts, bank[7][0:P + 1, 0:NS]).then_inc(s("firsts_ready"), 1)
                v.wait_ge(s("firsts_ready"), 1)
                v.wait_ge(s("dq_ready"), 1)
                with steps(v, NT, 2) as t:
                    for k in (0, 1):
                        v.wait_ge(s("cnt1"), t + (k - 1) if k else t)
                        v.tensor_scalar(junk[:, k, 0:NS], firsts, dq[:, ds(t + k, 1)], 0.0, ALU.is_lt, ALU.add,
                                        accum_out=cnt1[:, ds(t + k, 1)]).then_inc(s("cnt1"), 1)
                v.wait_ge(s("cnt1"), NT)
                v.tensor_scalar(ri, cnt1, -1.0, 0.0, ALU.add, ALU.max).then_inc(s("ri_ready"), 1)

                for c in range(NT // LCH):
                    v.wait_ge(s(f"x_in{c}"), 16)
                    with v.Fori(c * LCH, (c + 1) * LCH) as t:
                        v.bn_stats(st6[:, ds(t, 1), :].rearrange("p t a -> p (t a)"), acc[:, ds(t, 1), :].rearrange("p t d -> p (t d)")).then_inc(s("stats"), 1)
                v.wait_ge(s("stats"), NT)
                me, ve, mo, vo = st6[:, :, 1], st6[:, :, 2], st6[:, :, 4], st6[:, :, 5]
                q, dm, vs, ve_, va, r0, r2, r3 = stt[0:8]
                v.tensor_tensor(q, me, mo, ALU.add).then_inc(s("ln"), 1)
                v.tensor_tensor(dm, me, mo, ALU.subtract).then_inc(s("ln"), 1)
                v.tensor_tensor(vs, ve, vo, ALU.add).then_inc(s("ln"), 1)
                v.wait_ge(s("ln"), 3)
                v.tensor_scalar(mean[:, :], q, 0.5, None, ALU.mult).then_inc(s("ln"), 1)
                v.scalar_tensor_tensor(r0, dm, 0.25, dm, ALU.mult, ALU.mult).then_inc(s("ln"), 1)
                v.wait_ge(s("ln"), 5)
                v.scalar_tensor_tensor(va, vs, 1.0 / D, r0, ALU.mult, ALU.add).then_inc(s("ln"), 1)
                v.wait_ge(s("ln"), 6)
                v.tensor_scalar(ve_, va, LN_EPS, None, ALU.add).then_inc(s("var_ready"), 1)
                v.wait_ge(s("sqrt_ready"), 1)
                v.reciprocal(r2, r3).then_inc(s("ln"), 1)
                v.wait_ge(s("ln"), 7)
                v.tensor_tensor(q, r2, r2, ALU.mult).then_inc(s("ln"), 1)
                v.wait_ge(s("ln"), 8)
                v.scalar_tensor_tensor(dm, q, -0.5, ve_, ALU.mult, ALU.mult).then_inc(s("ln"), 1)
                v.wait_ge(s("ln"), 9)
                v.scalar_tensor_tensor(rstd[:, :], dm, 1.5, r2, ALU.add, ALU.mult).then_inc(s("ln"), 1)
                v.wait_ge(s("ln"), 10)
                v.wait_ge(s("colsum"), 1)
                v.scalar_tensor_tensor(gwf, bank[6][:, None, 0:D].broadcast_to([128, 2, D]), -1.0 / D, gwf, ALU.mult, ALU.add).then_inc(s("gwc"), 1)
                v.wait_ge(s("gwc"), 1)
                v.tensor_copy(gw[:, 0], gwf).then_inc(s("gwh"), 1)
                v.wait_ge(s("gwh"), 1)
                v.tensor_tensor(gw[:, 1], gwf, gw[:, 0], ALU.subtract).then_inc(s("gw_ready"), 1)
                with steps(v, NT, CH) as t:
                    for k in range(CH):
                        xn = acc[:, ds(t + k, 1), :]
                        v.tensor_scalar(xn, xn, mean[:, ds(t + k, 1)], rstd[:, ds(t + k, 1)], ALU.subtract, ALU.mult).then_inc(s("xn"), 1)
                    v.wait_ge(s("xn"), t + CH)
                    xn = acc[:, ds(t, CH), :]
                    hi, lo = (xa[k][:, ds(t, CH), 0:D] for k in (0, 1))
                    v.tensor_scalar(hi, xn, 1.0, None, ALU.add).then_inc(s("xa_hi"), CH)
                    v.wait_ge(s("xa_hi"), t + CH)
                    v.scalar_tensor_tensor(lo, xn, 1.0, hi, ALU.add, ALU.subtract).then_inc(s("xa_ready"), CH)
                v.wait_ge(s("att_in"), 32)
                with v.Fori(0, NT // CH) as i:
                    t = i * CH
                    for k in range(CH):
                        v.wait_ge(s(f"row_in{k}"), i * 16 + 16)
                        if k >= 2:
                            v.wait_ge(s("cnt2"), t + (k - 1))
                        else:
                            v.wait_ge(s("cnt2"), t)
                        v.tensor_scalar(junk[:, k % 2, 0:SR], drow[:, k, :], dq[:, ds(t + k, 1)], 0.0, ALU.is_lt, ALU.add,
                                        accum_out=cnt2[:, ds(t + k, 1)]).then_inc(s("cnt2"), 1)
                    v.wait_ge(s("cnt2"), t + CH)
                    v.sem_inc(s("rows_counted"), CH)
                    v.wait_ge(s("h_ready"), t + CH)
                    v.wait_ge(s("scored"), t)
                    ht = acc[:, ds(t, CH), :]
                    v.scalar_tensor_tensor(lk, ht, 0.2, ht, ALU.mult, ALU.max).then_inc(s("leaky"), CH)
                    v.wait_ge(s("leaky"), t + CH)
                    t4 = tat.rearrange("p (c s) d -> p c s d", s=2)
                    v.tensor_tensor(t4, lk[:, :, None, :].broadcast_to([P, CH, 2, D]), attb[:, None, :, :].broadcast_to([P, CH, 2, D]), ALU.mult).then_inc(s("tat_ready"), CH)
                    v.wait_ge(s("tat_ready"), t + CH)
                    v.tensor_reduce(wf[:, ds(t, CH), :].rearrange("p t h -> p (t h)"), tat.rearrange("p c (h d) -> p (c h) d", d=GD), AX.X, ALU.add).then_inc(s("scored"), CH)
                v.scalar_tensor_tensor(offf, ri, float(SR), cnt2, ALU.mult, ALU.add).then_inc(s("off_ready"), 1)
                v.wait_ge(s("off_ready"), 1)
                v.tensor_copy(offi[:, :], offf).then_inc(s("offi_ready"), 1)
                v.wait_ge(s("off_t"), 1)
                v.tensor_copy(offT, bank[7][0:NT, 0:P + 1]).then_inc(s("offT"), 1)
                v.wait_ge(s("offT"), 1)
                v.tensor_tensor(degT, offT[:, 1:P + 1], offT[:, 0:P], ALU.subtract).then_inc(s("degT"), 1)
                v.wait_ge(s("degT"), 1)
                v.tensor_reduce(mxd[:, 0:1], degT, AX.X, ALU.max).then_inc(s("mxd"), 1)
                v.wait_ge(s("mxd"), 1)
                v.tensor_scalar(mxi[:, 0:1], mxd[:, 0:1], 1.0, float(BLK - 1), ALU.max, ALU.add).then_inc(s("mxd"), 1)
                v.tensor_scalar(mxi[:, 1:2], mxd[:, 0:1], 1.0, float(WIN - 1), ALU.max, ALU.add).then_inc(s("mxd"), 1)
                v.wait_ge(s("mxd"), 3)
                v.tensor_scalar(mxi[:, 0:1], mxi[:, 0:1], 2, None, ALU.arith_shift_right).then_inc(s("mxd"), 1)
                v.tensor_scalar(mxi[:, 1:2], mxi[:, 1:2], 6, None, ALU.arith_shift_right).then_inc(s("mxd"), 1)
                v.wait_ge(s("mxd"), 5)
                v.tensor_scalar(mxd[:, 0:1], mxi[:, 0:1], float(WB), None, ALU.min).then_inc(s("mxd"), 1)
                v.tensor_copy(mxd[:, 1:2], mxi[:, 1:2]).then_inc(s("mxd"), 1)
                v.wait_ge(s("mxd"), 7)
                v.tensor_scalar(mxd[:, 3:4], mxd[:, 1:2], -1.0, float(WB), ALU.add, ALU.mult).then_inc(s("mxd"), 1)
                v.wait_ge(s("mxd"), 8)
                v.tensor_tensor(mxd[:, 2:3], mxd[:, 3:4], mxd[:, 0:1], ALU.add).then_inc(s("mxd"), 1)
                v.wait_ge(s("deg_t"), 1)
                v.tensor_copy(deg[:, :], bank[6][0:P, 0:NT]).then_inc(s("deg_ready"), 1)
                v.wait_ge(s("nblk_t"), 1)
                v.tensor_copy(nrow, bank[5][0:1, 0:4 * NT].rearrange("p (a b) -> p a b", b=NT)).then_inc(s("nrow"), 1)
                v.wait_ge(s("nrow"), 1)
                for k, what in ((0, 2), (1, 1)):
                    v.tensor_tensor_scan(nsum[:, k, :], nrow[:, what, :], nrow[:, what, :], 0.0, ALU.add, ALU.bypass).then_inc(s("nrow"), 1)
                v.wait_ge(s("nrow"), 3)
                for k, what in ((0, 2), (1, 1)):
                    v.tensor_tensor(nblk[:, 2 + k, :], nsum[:, k, :], nrow[:, what, :], ALU.subtract).then_inc(s("nrow"), 1)
                v.tensor_copy(nblk[:, 4, :], nsum[:, 0, :]).then_inc(s("nrow"), 1)
                v.tensor_copy(nblk[:, 0:2, :], nrow[:, 0:2, :]).then_inc(s("nrow"), 1)
                v.wait_ge(s("nrow"), 7)
                v.engine_nop().then_inc(s("nblk_ready"), 1)
                v.wait_ge(s("scored"), NT)
                v.tensor_reduce(mx, wf[:, :, :].rearrange("p t h -> p h t"), AX.X, ALU.max).then_inc(s("mx_ready"), 1)
                v.wait_ge(s("mxa_ready"), 1)
                v.tensor_tensor(wf[:, :, :], wf[:, :, :], mxa[:, None, :].broadcast_to([P, NT, 2 * GH]), ALU.subtract).then_inc(s("score_shifted"), 1)
                v.wait_ge(s("w_ready"), 1)
                with steps(v, NT, CH) as t:
                    g4 = acc[:, ds(t, CH), :].rearrange("p t (h d) -> p t h d", d=GD)
                    v.tensor_tensor(g4, g4, wf[:, ds(t, CH), 0:GH].rearrange("p t (h o) -> p t h o", o=1).broadcast_to([P, CH, GH, GD]), ALU.mult).then_inc(s("g_ready"), CH)

            @block.scalar
            def _(a):
                a.wait_ge(s("var_ready"), 1)
                a.activation(stt[7], stt[3], ACT.Sqrt).then_inc(s("sqrt_ready"), 1)
                a.wait_ge(s("eps_ready"), 2)
                a.activation(stt[8][:, 0:1], shf, ACT.Exp, scale=0.0).then_inc(s("exp_table"), 1)
                with steps(a, NT, 2) as t:
                    for k in (0, 1):
                        a.wait_ge(s("xt_ps"), t + (k + 1))
                        a.activation(xt[:, ds(t + k, 1), :, 0:P].rearrange("p t j n -> p (t j) n"),
                                     bank[k][:, 0:256].bitcast(F16).rearrange("p (j n) -> p j n", j=4)[:, :, 0:P], ACT.Copy).then_inc(s("xt_ready"), 1)
                        a.wait_ge(s("h_ps"), t + (k + 1))
                        a.activation(acc[:, ds(t + k, 1), :].rearrange("p t d -> p (t d)"), bank[2 + k][0:P, 0:D], ACT.Copy).then_inc(s("h_ready"), 1)
                a.wait_ge(s("score_shifted"), 1)
                a.activation(wf[:, :, :], wf[:, :, :], ACT.Exp, bias=shf).then_inc(s("w_ready"), 1)

            @block.tensor
            def _(pe):
                pe.wait_ge(s("first1f_ready"), 1)
                pe.wait_ge(s("ones_ready"), 2)
                pe.matmul(bank[7][0:P + 1, 0:NS], ones[0:1, 0:P + 1], first1f, start=True, stop=True).then_inc(s("firsts_bcast"), 1)
                pe.wait_ge(s("gw_in"), 16)
                for k in (0, 1):
                    mm = pe.matmul(bank[6][:, 0:D], ones[:, :], gwf[:, k, :], start=(k == 0), stop=(k == 1))
                mm.then_inc(s("colsum"), 1)
                pe.wait_ge(s("identh_ready"), 1)
                pe.wait_ge(s("gw_ready"), 1)

                def transpose_x(t, k, wait_bank):
                    for j in range(4):
                        mm = pe.transpose(bank[k][:, 0:256].bitcast(F16).rearrange("p (j n) -> p j n", j=4)[:, j, 0:P],
                                          xa[j // 2][:, ds(t, 1), 128 * (j % 2):128 * (j % 2) + 128].rearrange("p t d -> p (t d)"), identh[0:P, 0:P])
                    mm.then_inc(s("xt_ps"), 1)

                with steps(pe, NT, 2) as t:
                    for k in (0, 1):
                        pe.wait_ge(s("xa_ready"), t + (k + 1))
                        pe.wait_ge(s("xt_ready"), t)
                        transpose_x(t + k, k, None)
                    for k in (0, 1):
                        pe.wait_ge(s("xt_ready"), t + (k + 1))
                        pe.wait_ge(s("h_ready"), t)
                        n = 0
                        for xh, wh in ((0, 0), (0, 1), (1, 0)):
                            for dh in (0, 1):
                                mm = pe.matmul(bank[2 + k][0:P, 0:D], xt[:, ds(t + k, 1), 2 * xh + dh, 0:P].rearrange("p t n -> p (t n)"), gw[:, wh, dh, :],
                                               start=(n == 0), stop=(n == 5))
                                n += 1
                        mm.then_inc(s("h_ps"), 1)
                pe.wait_ge(s("off_ready"), 1)
                pe.wait_ge(s("ident_ready"), 1)
                pe.wait_ge(s("firsts_ready"), 1)
                pe.transpose(bank[7][0:NT, 0:P + 1], offf, ident[0:P + 1, 0:P + 1]).then_inc(s("off_t"), 1)
                pe.wait_ge(s("degT"), 1)
                pe.wait_ge(s("gwc"), 1)
                pe.transpose(bank[6][0:P, 0:NT], degT, ident[0:NT, 0:NT]).then_inc(s("deg_t"), 1)
                pe.wait_ge(s("mxd"), 9)
                for k in range(4):
                    mm = pe.transpose(bank[5][0:1, k * NT:(k + 1) * NT], mxd[:, k:k + 1], ident[0:NT, 0:NT])
                mm.then_inc(s("nblk_t"), 1)


        next_part()

        with nc.Block() as block:
            @block.sync
            def _(sp):
                def start_sums(t, k):
                    sp.dma_start(gacc[:, k, 0, :], table[0:N, :].rearrange("(t p) d -> t p d", p=P)[ds(t, 1)].rearrange("t p d -> p (t d)")).then_inc(s(f"sum_start{k}"), 16)
                    sp.dma_start(gacc[:, k, 1:BLK, :].rearrange("p a b -> p (a b)"),
                                 table[N:N + 1, 0:ROWW].rearrange("o (a b) -> o a b", a=1).broadcast_to([P, BLK - 1, ROWW])).then_inc(s(f"sum_start{k}"), 16)
                for k in (0, 1):
                    start_sums(k, k)

                def store_sums(t, k, n):
                    sp.wait_ge(s("sum_ready"), t + 1)
                    sp.dma_start(sums[ds(t, 1)].rearrange("t p d -> p (t d)"), gacc[:, k].rearrange("p a b -> p (a b)")).then_inc(s(f"sum_stored{k}"), 16)
                    sp.wait_ge(s(f"sum_stored{k}"), n * 16 + 16)
                with sp.Fori(0, NT // 2 - 1) as i:
                    for k in (0, 1):
                        store_sums(i * 2 + k, k, i)
                        start_sums(i * 2 + (k + 2), k)
                for k in (0, 1):
                    store_sums(NT - 2 + k, k, NT // 2 - 1)
                for k in (0, 1):
                    sp.wait_ge(s(f"sum_stored{k}"), 16 * (NT // 2))
                sp.wait_ge(s("fz_ready"), 1)

                def load_sums(k, i, t):
                    sp.wait_ge(s("gn_red"), less(t, 1))
                    sp.dma_start(nsum_in[k], sums[ds(t, 1)].rearrange("t p d -> p (t d)")).then_inc(s(f"sums_in{k}"), 16)
                pipeline(sp, [(0, load_sums)])

            @block.gpsimd
            def _(pool):
                def window(n):
                    pool.indirect_dma_start(out=widx[:, :], out_offset=None, in_=srcpad.rearrange("(n o) -> n o", o=1),
                                            in_offset=bass.IndirectOffsetOnAxis(ap=woff[:, 0:1], axis=0)).then_inc(s("widx_in"), 16)
                    pool.tensor_scalar(wmask[:, :], kpos[:, :], wrem[:, 0:1], None, ALU.is_lt).then_inc(s("wmask"), 1)
                    hold(pool, "widx_in", n * 16 + 16)
                    pool.tensor_scalar(wval[:, :], widx[:, :], float(-N), None, ALU.add).then_inc(s("wmask"), 1)
                    hold(pool, "wmask", n * 4 + 2)
                    pool.tensor_tensor(wval[:, :], wval[:, :], wmask[:, :], ALU.mult).then_inc(s("wmask"), 1)
                    hold(pool, "wmask", n * 4 + 3)
                    pool.tensor_scalar(gidx[:, :], wval[:, :], float(N), None, ALU.add).then_inc(s("wmask"), 1)
                    hold(pool, "wmask", n * 4 + 4)

                def gathers(k, b, n):
                    for j in range(BLK):
                        hold(pool, f"added{j}", n * 16)
                        pool.indirect_dma_start(out=gacc[:, k, j, :], out_offset=None, in_=table,
                                                in_offset=bass.IndirectOffsetOnAxis(ap=gidx[:, BLK * b + j:BLK * b + j + 1], axis=0),
                                                compute_op=ALU.add).then_inc(s(f"added{j}"), 16)

                with pool.Fori(0, NT // 2) as i:
                    for k in (0, 1):
                        t = i * 2 + k
                        nb = pool.value_load(nblk[0:1, 0, ds(t, 1)], min_val=1, max_val=WB)
                        nw = pool.value_load(nblk[0:1, 1, ds(t, 1)], min_val=1, max_val=E // WIN + 1)
                        bsum = pool.value_load(nblk[0:1, 2, ds(t, 1)], min_val=0, max_val=E)
                        wsumr = pool.value_load(nblk[0:1, 3, ds(t, 1)], min_val=0, max_val=E)
                        bend = pool.value_load(nblk[0:1, 4, ds(t, 1)], min_val=0, max_val=E)
                        pool.tensor_copy(woff[:, :], offi[0:P, ds(t, 1)]).then_inc(s("wcopies"), 1)
                        pool.tensor_copy(wrem[:, :], deg[:, ds(t, 1)]).then_inc(s("wcopies"), 1)
                        hold(pool, "wcopies", wsumr * 2 + 2)
                        window(wsumr)
                        hold(pool, f"sum_start{k}", i * 32 + 32)
                        gathers(k, 0, bsum)
                        for b in range(1, WB):
                            with pool.If(nb > b):
                                gathers(k, b, bsum + b)
                        with pool.If(nw > 1):
                            with pool.Fori(1, nw) as w:
                                for j in range(BLK):
                                    hold(pool, f"added{j}", (bsum + w * WB) * 16)
                                pool.tensor_scalar(woff[:, :], woff[:, :], float(WIN), float(E), ALU.add, ALU.min).then_inc(s("wcopies"), 1)
                                pool.tensor_scalar(wrem[:, :], wrem[:, :], float(-WIN), None, ALU.add).then_inc(s("wcopies"), 1)
                                hold(pool, "wcopies", (wsumr + w) * 2 + 2)
                                window(wsumr + w)
                                for b in range(WB):
                                    gathers(k, b, bsum + w * WB + b)
                        for j in range(BLK):
                            hold(pool, f"added{j}", bend * 16)
                        pool.tensor_copy(wsum[:, ds(t, 1), :, :].rearrange("p t a b -> p (t a) b"), gacc[:, k, :, D:ROWW]).then_inc(s("sum_ready"), 1)

                pool.wait_ge(s("zpart"), 1)
                pool.partition_all_reduce(zall, zpart, P, bass.bass_isa.ReduceOp.add).then_inc(s("zall"), 1)
                pool.wait_ge(s("logits"), NT)
                pool.memset(tri, 1.0).then_inc(s("rt"), 1)
                pool.iota(downi, pattern=[[-1, NE]], base=NE, channel_multiplier=0).then_inc(s("rt"), 1)
                pool.iota(node, pattern=[[P, NT]], base=NE * CB, channel_multiplier=1).then_inc(s("rt"), 1)
                pool.wait_ge(s("rt"), 3)
                pool.affine_select(out=tri, in_=tri, compare_op=ALU.is_ge, fill=0.0, base=0, pattern=[[1, P]], channel_multiplier=-1).then_inc(s("rt"), 1)
                pool.tensor_copy(down, downi).then_inc(s("rt"), 1)
                pool.tensor_copy(rdump, node).then_inc(s("rt"), 1)

            @block.vector
            def _(v):
                with v.Fori(0, H) as h:
                    for m in range(3):
                        v.wait_ge(s("wsum_ps"), h * 3 + (m + 1))
                        v.scalar_tensor_tensor(wraw[:, m], bank[m][:, None, 0:D].broadcast_to([128, 2, D]), -1.0 / D, wraw[:, m], ALU.mult, ALU.add).then_inc(s("wcen"), 1)
                    v.wait_ge(s("wc_out"), h * 48)
                    v.wait_ge(s("wcen"), h * 3 + 3)
                    for m in (0, 1):
                        v.tensor_scalar(wc[m][:, 0, :, 0:D], wraw[:, m], 0.25, None, ALU.mult).then_inc(s("whi"), 1)
                    v.wait_ge(s("whi"), h * 4 + 2)
                    for m in (0, 1):
                        v.scalar_tensor_tensor(wc[m][:, 1, :, 0:D], wraw[:, m], 0.25, wc[m][:, 0, :, 0:D], ALU.mult, ALU.subtract).then_inc(s("wlo"), 1)
                    for m in (0, 1):
                        v.wait_ge(s("prod_ps"), h * 3 + (m + 1))
                        v.tensor_scalar(wc[m][:, 0, :, D:2 * D], bank[4 + m][:, :].rearrange("p (a b) -> p a b", a=2), 0.25, None, ALU.mult).then_inc(s("whi"), 1)
                    v.wait_ge(s("whi"), h * 4 + 4)
                    v.wait_ge(s("wlo"), h * 2 + 2)
                    for m in (0, 1):
                        v.scalar_tensor_tensor(wc[m][:, 1, :, D:2 * D], bank[4 + m][:, :].rearrange("p (a b) -> p a b", a=2), 0.25, wc[m][:, 0, :, D:2 * D], ALU.mult, ALU.subtract).then_inc(s("prod_used"), 1)
                    v.wait_ge(s("prod_ps"), h * 3 + 3)
                    v.tensor_copy(bmat, bank[6][:, :].rearrange("p (a b) -> p a b", a=2)).then_inc(s("prod_used"), 1)
                v.memset(zero, 0.0).then_inc(s("zero_ready"), 1)
                v.wait_ge(s("bo_in"), 16)
                v.tensor_copy(acc[:, :, :], brow_bo[:, None, :].broadcast_to([P, NT, D])).then_inc(s("acc_ready"), 1)
                v.wait_ge(s("acc_ready"), 1)
                with v.Fori(0, H) as h:
                    def negate(ph_):
                        def step(k, i, t):
                            v.wait_ge(s(f"{ph_}_sq"), h * NT + (t + 1))
                            v.tensor_scalar(nsq[k], sq[k], -1.0, LOG16, ALU.mult, ALU.subtract).then_inc(s(f"{ph_}_nsq"), 1)
                        return step

                    def k_hi(k, i, t):
                        v.wait_ge(s("k_exp"), h * NT + (t + 1))
                        v.wait_ge(s("k_kv"), h * NT + less(t, 3))
                        v.tensor_scalar(ph[k][:, 0, :], ex[k], PHI_EPS, None, ALU.add).then_inc(s("k_hi"), 1)

                    def k_lo(k, i, t):
                        v.wait_ge(s("k_hi"), h * NT + (t + 1))
                        v.scalar_tensor_tensor(ph[k][:, 1, :], ex[k], PHI_EPS, ph[k][:, 0, :], ALU.add, ALU.subtract).then_inc(s("k_ph"), 1)

                    pipeline(v, [(2, k_hi), (0, negate("k")), (2, k_lo)], NT, 4)
                    v.wait_ge(s("kvo_ps"), h + 1)
                    v.wait_ge(s("q_att"), h * NT)
                    kvp = bank[5][:, :].rearrange("p (a b) -> p a b", a=2)
                    v.tensor_copy(kvo[:, 0, :, 0:D], kvp).then_inc(s("kvo_hi"), 1)
                    v.tensor_copy(kvo[:, 0, :, D:D + 1], kvs[:, :, D:D + 1]).then_inc(s("kvo_hi"), 1)
                    v.wait_ge(s("kvo_hi"), h * 2 + 2)
                    v.tensor_tensor(kvo[:, 1, :, 0:D], kvp, kvo[:, 0, :, 0:D], ALU.subtract).then_inc(s("kvo_lo"), 1)
                    v.wait_ge(s("kvo_lo"), h + 1)
                    v.tensor_tensor(kvo[:, 1, :, D:D + 1], kvs[:, :, D:D + 1], kvo[:, 0, :, D:D + 1], ALU.subtract).then_inc(s("kvo_ready"), 1)

                    def turned(k):
                        return bank[4 + k % 2][:, 0:256].rearrange("p (a b) -> p a b", a=2)[:, :, 0:P]

                    def q_hi(k, i, t):
                        v.wait_ge(s("q_turned"), h * NT + (t + 1))
                        v.wait_ge(s("q_att"), h * NT + less(t, 3))
                        v.tensor_scalar(qt[k][:, 0, :, 0:P], turned(k), PHI_EPS, None, ALU.add).then_inc(s("q_hi"), 1)

                    def q_lo(k, i, t):
                        v.wait_ge(s("q_hi"), h * NT + (t + 1))
                        v.scalar_tensor_tensor(qt[k][:, 1, :, 0:P], turned(k), PHI_EPS, qt[k][:, 0, :, 0:P], ALU.add, ALU.subtract).then_inc(s("q_ph"), 1)

                    def over_z(k, i, t):
                        v.wait_ge(s("q_att"), h * NT + (t + 1))
                        v.wait_ge(s("q_acc"), h * NT + less(t, 3))
                        v.reciprocal(rz[k], bank[6 + k % 2][0:P, D:D + 1]).then_inc(s("q_rz"), 1)

                    def add_head(k, i, t):
                        v.wait_ge(s("q_rz"), h * NT + (t + 1))
                        at = acc[:, ds(t, 1), :].rearrange("p t d -> p (t d)")
                        v.scalar_tensor_tensor(at, bank[6 + k % 2][0:P, 0:D], rz[k], at, ALU.mult, ALU.add).then_inc(s("q_acc"), 1)

                    pipeline(v, [(3, q_hi), (0, negate("q")), (5, over_z), (3, q_lo), (5, add_head)], NT, 4)
                    v.wait_ge(s("q_acc"), (h + 1) * NT)


                def per_row(col, t, n=CH):
                    return col[:, ds(t, n)].rearrange("p (t o) -> p t o", o=1).broadcast_to([P, n, D])

                def norm_stats(n, eps_):
                    me, ve, mo, vo = tst[:, :, 1], tst[:, :, 2], tst[:, :, 4], tst[:, :, 5]
                    q, dm, vs, ve_, va, r0, r2, r3 = tln
                    ln = s("ln")
                    b = 10 * n
                    v.tensor_tensor(q, me, mo, ALU.add).then_inc(ln, 1)
                    v.tensor_tensor(dm, me, mo, ALU.subtract).then_inc(ln, 1)
                    v.tensor_tensor(vs, ve, vo, ALU.add).then_inc(ln, 1)
                    v.wait_ge(ln, b + 3)
                    v.tensor_scalar(mean[:, :], q, 0.5, None, ALU.mult).then_inc(ln, 1)
                    v.scalar_tensor_tensor(r0, dm, 0.25, dm, ALU.mult, ALU.mult).then_inc(ln, 1)
                    v.wait_ge(ln, b + 5)
                    v.scalar_tensor_tensor(va, vs, 1.0 / D, r0, ALU.mult, ALU.add).then_inc(ln, 1)
                    v.wait_ge(ln, b + 6)
                    v.tensor_scalar(ve_, va, eps_, None, ALU.add).then_inc(s("var_ready"), 1)
                    v.wait_ge(s("sqrt_ready"), n + 1)
                    v.reciprocal(r2, r3).then_inc(ln, 1)
                    v.wait_ge(ln, b + 7)
                    v.tensor_tensor(q, r2, r2, ALU.mult).then_inc(ln, 1)
                    v.wait_ge(ln, b + 8)
                    v.scalar_tensor_tensor(dm, q, -0.5, ve_, ALU.mult, ALU.mult).then_inc(ln, 1)
                    v.wait_ge(ln, b + 9)
                    v.scalar_tensor_tensor(rstd[:, :], dm, 1.5, r2, ALU.add, ALU.mult).then_inc(ln, 1)
                    v.wait_ge(ln, b + 10)

                def stats_of(tile, done):
                    v.bn_stats(tst[:, ds(tile, 1), :].rearrange("p t a -> p (t a)"), acc[:, ds(tile, 1), :].rearrange("p t d -> p (t d)")).then_inc(s(done), 1)

                with v.Fori(0, NT // CH // 2) as i:
                    for k in (0, 1):
                        t, n = i * 2 * CH + k * CH, i * 6 + k * 3
                        v.wait_ge(s(f"xc_in{k}"), i * 16 + 16)
                        v.tensor_tensor(xc[k], xc[k], per_row(mean, t), ALU.subtract).then_inc(s("resid"), 1)
                        v.wait_ge(s("resid"), n + 1)
                        v.tensor_tensor(xc[k], xc[k], per_row(rstd, t), ALU.mult).then_inc(s("resid"), 1)
                        v.wait_ge(s("resid"), n + 2)
                        at = acc[:, ds(t, CH), :]
                        v.tensor_tensor(at, at, xc[k], ALU.add).then_inc(s("resid"), 1)
                        v.wait_ge(s("resid"), n + 3)
                        for j in range(CH):
                            stats_of(t + j, f"xc_used{k}")
                for k in (0, 1):
                    v.wait_ge(s(f"xc_used{k}"), NT // 2)
                norm_stats(0, MIX_EPS)
                v.wait_ge(s("tail_in"), 16 * 11)

                def out1(k, i, g):
                    t = g * 2
                    for j in (0, 1):
                        at = acc[:, ds(t + j, 1), :]
                        v.tensor_scalar(at, at, mean[:, ds(t + j, 1)], rstd[:, ds(t + j, 1)], ALU.subtract, ALU.mult).then_inc(s("out1_norm"), 1)
                    at = acc[:, ds(t, 2), :]
                    v.wait_ge(s("out1_norm"), t + 2)
                    v.tensor_tensor(at, at, g1b[:, None, :].broadcast_to([P, 2, D]), ALU.mult).then_inc(s("out1_g"), 1)
                    v.wait_ge(s("out1_g"), g * 2 + 1)
                    v.tensor_tensor(at, at, beta1b[:, None, :].broadcast_to([P, 2, D]), ALU.add).then_inc(s("out1_g"), 1)
                    v.wait_ge(s("out1_g"), g * 2 + 2)
                    hold(v, "out1_turned", less(g, 1), "dve")
                    v.tensor_copy(o1[k], at).then_inc(s("out1_ready"), 1)

                def add_ffn(k, i, g):
                    v.wait_ge(s("ffn_ps"), g + 1)
                    at = acc[:, ds(g * 2, 2), :]
                    v.tensor_tensor(at, at, bank[4 + k][0:P, :].rearrange("p (a b) -> p a b", a=2), ALU.add).then_inc(s("ffn_added"), 1)
                    v.wait_ge(s("ffn_added"), g + 1)
                    v.tensor_tensor(at, at, bias2b[:, None, :].broadcast_to([P, 2, D]), ALU.add).then_inc(s("ffn_bias"), 1)

                def stats2(k, i, g):
                    v.wait_ge(s("ffn_bias"), g + 1)
                    for j in (0, 1):
                        stats_of(g * 2 + j, "stats2")
                pipeline(v, [(0, out1), (3, add_ffn), (4, stats2)], NT // 2)
                v.wait_ge(s("stats2"), NT)
                norm_stats(1, MIX_EPS)
                v.tensor_tensor(beta2b, beta2b, gnnb, ALU.add).then_inc(s("beta2_gnn"), 1)
                v.wait_ge(s("beta2_gnn"), 1)
                with v.Fori(0, NT // CH // 2) as i:
                    for k in (0, 1):
                        t, c = i * 2 * CH + k * CH, i * 2 + k
                        for j in range(CH):
                            at = acc[:, ds(t + j, 1), :]
                            v.tensor_scalar(at, at, mean[:, ds(t + j, 1)], rstd[:, ds(t + j, 1)], ALU.subtract, ALU.mult).then_inc(s("mix_norm"), 1)
                        at = acc[:, ds(t, CH), :]
                        v.wait_ge(s("mix_norm"), t + CH)
                        v.tensor_tensor(at, at, g2b[:, None, :].broadcast_to([P, CH, D]), ALU.mult).then_inc(s("mix_g"), 1)
                        v.wait_ge(s(f"xc2_in{k}"), i * 16 + 16)
                        v.tensor_tensor(xc[k], xc[k], beta2b[:, None, :].broadcast_to([P, CH, D]), ALU.add).then_inc(s("mix_g"), 1)
                        v.wait_ge(s("mix_g"), c * 2 + 2)
                        v.tensor_tensor(at, at, xc[k], ALU.add).then_inc(s(f"xc2_used{k}"), 1)
                for k in (0, 1):
                    v.wait_ge(s(f"xc2_used{k}"), NT // CH // 2)
                v.wait_ge(s("sum_ready"), NT)
                v.tensor_tensor(wfs, wsum[:, :, :, :], wf[:, :, None, GH:2 * GH].broadcast_to([P, NT, BLK, GH]), ALU.mult).then_inc(s("z"), 1)
                v.wait_ge(s("z"), 1)
                v.tensor_reduce(zpart, wfs.rearrange("p t b h -> p h (t b)"), AX.X, ALU.add).then_inc(s("zpart"), 1)
                v.wait_ge(s("zall"), 1)
                v.reciprocal(zpart, zall).then_inc(s("z"), 1)
                v.wait_ge(s("z"), 2)
                v.tensor_tensor(fz, wf[:, :, GH:2 * GH], zpart[:, None, :].broadcast_to([P, NT, GH]), ALU.mult).then_inc(s("fz_ready"), 1)
                v.wait_ge(s("fz_ready"), 1)

                def reduce_sums(k, i, t):
                    v.wait_ge(s(f"sums_in{k}"), i * 16 + 16)
                    v.tensor_reduce(gn[k], nsum_in[k].rearrange("p (b c) -> p c b", b=BLK)[:, 0:D, :], AX.X, ALU.add).then_inc(s("gn_red"), 1)

                def scale_sums(k, i, t):
                    v.wait_ge(s("gn_red"), t + 1)
                    g = gn[k].rearrange("p (h d) -> p h d", h=GH)
                    v.tensor_tensor(g, g, fz[:, ds(t, 1), :].rearrange("p t (h o) -> p (t h) o", o=1).broadcast_to([P, GH, GD]), ALU.mult).then_inc(s("gn_scaled"), 1)

                def add_sums(k, i, t):
                    v.wait_ge(s("gn_scaled"), t + 1)
                    at = acc[:, ds(t, 1), :].rearrange("p t d -> p (t d)")
                    v.tensor_tensor(at, at, gn[k], ALU.add).then_inc(s("gn_added"), 1)

                def stats3(k, i, t):
                    v.wait_ge(s("gn_added"), t + 1)
                    stats_of(t, "acc_new")
                pipeline(v, [(2, stats3), (1, add_sums), (0, reduce_sums), (0, scale_sums)])
                v.wait_ge(s("acc_new"), NT)
                norm_stats(2, LN_EPS)

                def gate_norm(k, i, t):
                    v.wait_ge(s("xf_turned"), less(t, 1))
                    v.tensor_scalar(xfs[k], acc[:, ds(t, 1), :].rearrange("p t d -> p (t d)"), mean[:, ds(t, 1)], rstd[:, ds(t, 1)], ALU.subtract, ALU.mult).then_inc(s("xf_ready"), 1)

                def logits(k, i, t):
                    v.wait_ge(s("lg_ps"), t + 1)
                    v.tensor_tensor(lg[:, ds(t, 1), :].rearrange("p t e -> p (t e)"), bank[2 + k][0:P, 0:NE], gateb, ALU.add).then_inc(s("logits"), 1)
                pipeline(v, [(0, gate_norm), (2, logits)])
                v.wait_ge(s("logits"), NT)
                v.wait_ge(s("rt"), 6)

                def over_experts(col):
                    return col[:, :, None].broadcast_to([P, NT, NE])
                v.tensor_reduce(rmax, lg, AX.X, ALU.max).then_inc(s("route"), 1)
                v.wait_ge(s("route"), 1)
                v.tensor_tensor(lg, lg, over_experts(rmax), ALU.subtract).then_inc(s("route"), 1)
                v.wait_ge(s("rexp"), 1)
                v.tensor_reduce(rsum, rex, AX.X, ALU.add).then_inc(s("route"), 1)
                v.tensor_reduce(rmax, rex, AX.X, ALU.max).then_inc(s("route"), 1)
                v.wait_ge(s("route"), 4)
                v.reciprocal(rinv, rsum).then_inc(s("route"), 1)
                v.tensor_tensor(rex, rex, over_experts(rmax), ALU.is_equal).then_inc(s("route"), 1)
                v.wait_ge(s("route"), 6)
                v.tensor_tensor(rex, rex, down[:, None, :].broadcast_to([P, NT, NE]), ALU.mult).then_inc(s("route"), 1)
                v.tensor_tensor(rinv, rinv, rmax, ALU.mult).then_inc(s("route"), 1)
                v.wait_ge(s("route"), 8)
                v.tensor_reduce(ridx, rex, AX.X, ALU.max).then_inc(s("route"), 1)
                v.wait_ge(s("route"), 9)
                v.tensor_tensor(roh, rex, over_experts(ridx), ALU.is_equal).then_inc(s("onehot_ready"), 1)
                v.wait_ge(s("counts_ps"), 1)
                v.tensor_copy(rtot, bank[1][0:P, 0:NT * NE].rearrange("p (t e) -> p t e", e=NE)).then_inc(s("route"), 1)
                v.wait_ge(s("route"), 10)
                for e in range(NE):
                    v.tensor_tensor_scan(rscan[:, :, e], rtot[:, :, e], rtot[:, :, e], 0.0, ALU.add, ALU.bypass).then_inc(s("route"), 1)
                v.wait_ge(s("route"), 18)
                v.tensor_tensor(rscan, rscan, rtot, ALU.subtract).then_inc(s("route"), 1)
                v.wait_ge(s("route"), 19)
                v.tensor_tensor(rscan, rscan, bank[0][0:P, 0:NT * NE].rearrange("p (t e) -> p t e", e=NE), ALU.add).then_inc(s("route"), 1)
                v.wait_ge(s("route"), 20)
                v.tensor_tensor(rscan, rscan, roh, ALU.mult).then_inc(s("route"), 1)
                v.wait_ge(s("route"), 21)
                v.tensor_reduce(rpos, rscan, AX.X, ALU.add).then_inc(s("route"), 1)
                v.wait_ge(s("route"), 22)
                v.tensor_scalar(rkept, rpos, float(CAP) + 0.5, None, ALU.is_lt).then_inc(s("route"), 1)
                v.tensor_scalar(rpos, rpos, float(CAP), -1.0, ALU.min, ALU.add).then_inc(s("route"), 1)
                v.tensor_scalar(rtmp, ridx, -float(CB), float(NE * CB), ALU.mult, ALU.add).then_inc(s("route"), 1)
                v.wait_ge(s("route"), 25)
                v.tensor_tensor(rtmp, rtmp, rpos, ALU.add).then_inc(s("route"), 1)
                v.tensor_tensor(pk, rinv, rkept, ALU.mult).then_inc(s("route"), 1)
                v.wait_ge(s("route"), 27)
                v.tensor_copy(slot_in, rtmp).then_inc(s("route"), 1)
                v.tensor_tensor(rtmp, rtmp, rdump, ALU.subtract).then_inc(s("route"), 1)
                v.wait_ge(s("route"), 29)
                v.tensor_tensor(rtmp, rtmp, rkept, ALU.mult).then_inc(s("route"), 1)
                v.wait_ge(s("route"), 30)
                v.tensor_tensor(slot_out, rtmp, rdump, ALU.add).then_inc(s("slots_ready"), 1)

            @block.scalar
            def _(a):
                a.activation(spare[:, 0:1], ident[0:P, 0:1], ACT.Exp)
                a.dma_start(brow_bo, bo.rearrange("(o d) -> o d", o=1).broadcast_to([P, D])).then_inc(s("bo_in"), 16)
                a.dma_start(projr, proj.rearrange("(a p) n -> p a n", p=128)).then_inc(s("proj_in"), 16)
                a.wait_ge(s("projt_ps"), 1)
                a.activation(projt, bank[0][:, :].rearrange("p (a b) -> p a b", a=2), ACT.Copy).then_inc(s("projt_ready"), 1)
                with a.Fori(0, H) as h:
                    a.wait_ge(s("prod_ps"), h * 3)
                    for m, w in enumerate((Wq, Wk, Wv)):
                        a.dma_start(wraw[:, m], w[:, ds(h, 1), :].rearrange("(a p) h k -> p a (h k)", p=128)).then_inc(s("w_in"), 16)
                    a.dma_start(wo, Wo[ds(h, 1)].rearrange("h (a p) d -> p (h a) d", p=128)).then_inc(s("w_in"), 16)
                    for m, b in enumerate((bq, bk, bv)):
                        a.dma_start(brow[0:1, m, :], b[ds(h, 1), :]).then_inc(s("w_in"), 16)
                    for m in range(3):
                        a.wait_ge(s("wt_ps"), h * 3 + (m + 1))
                        a.activation(wt[:, m], bank[3][:, :].rearrange("p (a b) -> p a b", a=2), ACT.Copy).then_inc(s("wt_ready"), 1)
                    a.wait_ge(s("prod_used"), h * 3 + 3)
                    for m in (0, 1):
                        a.dma_start(wcat[ds(h, 1), m].rearrange("h p n -> p (h n)"), wc[m].rearrange("p a b c -> p (a b c)")).then_inc(s("wc_out"), 16)
                    a.dma_start(bdram[ds(h, 1)].rearrange("h p n -> p (h n)"), bmat.rearrange("p a b -> p (a b)")).then_inc(s("wc_out"), 16)
                a.wait_ge(s("wc_out"), H * 48)
                def load_head(m, h, name):
                    a.dma_start(wc[m].rearrange("p a b c -> p (a b c)"), wcat[ds(h, 1), m].rearrange("h p n -> p (h n)")).then_inc(s(name), 16)
                with a.Fori(0, H) as h:
                    a.wait_ge(s("k_u"), h * NT)
                    load_head(1, h, "wk_in")
                    a.wait_ge(s("kvo_ps"), h)
                    a.dma_start(bmat.rearrange("p a b -> p (a b)"), bdram[ds(h, 1)].rearrange("h p n -> p (h n)")).then_inc(s("bmat_in"), 16)
                    a.wait_ge(s("q_u"), h * NT)
                    load_head(0, h, "wq_in")

                    def square(ph_):
                        def step(k, i, t):
                            a.wait_ge(s(f"{ph_}_u"), h * NT + (t + 1))
                            a.wait_ge(s(f"{ph_}_exp"), h * NT + less(t, 3))
                            a.activation(sqj[k], fbank[ph_][k][0:P, 0:D], ACT.Square, scale=0.5 ** 0.5, accum_out=sq[k]).then_inc(s(f"{ph_}_sq"), 1)
                        return step

                    def expo(ph_, used):
                        def step(k, i, t):
                            a.wait_ge(s(f"{ph_}_nsq"), h * NT + (t + 1))
                            a.wait_ge(s(used), h * NT + less(t, 3))
                            a.activation(ex[k], fbank[ph_][k][0:P, D:2 * D], ACT.Exp, bias=nsq[k]).then_inc(s(f"{ph_}_exp"), 1)
                        return step

                    a.wait_ge(s("q_turned"), h * NT)
                    pipeline(a, [(0, square("k")), (1, expo("k", "k_ph"))], NT, 4)
                    a.wait_ge(s("k_kv"), (h + 1) * NT)
                    for m in (0, 1):
                        ins = a.activation(kvs[:, m, 0:D + 1], bank[2 + m][:, 0:D + 1], ACT.Copy)
                    ins.then_inc(s("kvs_ready"), 1)
                    a.wait_ge(s("kvt_ps"), h + 1)
                    a.activation(kvt, bank[4][:, :].rearrange("p (a b) -> p a b", a=2), ACT.Copy).then_inc(s("kvt_ready"), 1)
                    a.wait_ge(s("k_ph"), (h + 1) * NT)
                    pipeline(a, [(0, square("q")), (1, expo("q", "q_turned"))], NT, 4)


                a.wait_ge(s("q_acc"), H * NT)
                for to, fro in ((g1b, g1), (beta1b, beta1), (g2b, g2), (beta2b, beta2), (bias2b, bias2), (gnnb, gb), (gateb, gate_b)):
                    a.dma_start(to, fro.rearrange("(o d) -> o d", o=1).broadcast_to([P, to.shape[-1]])).then_inc(s("tail_in"), 16)
                for to, fro in ((W1s, W1), (W2s, W2), (gate, gate_w)):
                    a.dma_start(to, fro.rearrange("(a p) n -> p a n", p=128)).then_inc(s("tail_in"), 16)
                a.dma_start(b1r, bias1.rearrange("(a p) -> a p", p=128)).then_inc(s("tail_in"), 16)

                def load_x(again):
                    with a.Fori(0, NT // CH // 2) as i:
                        for k in (0, 1):
                            a.wait_ge(s(f"xc{again}_used{k}"), i * (1 if again else CH))
                            a.dma_start(xc[k], xv[:, ds(i * 2 * CH + k * CH, CH), :]).then_inc(s(f"xc{again}_in{k}"), 16)
                load_x("")

                def root(n):
                    a.wait_ge(s("var_ready"), n + 1)
                    a.activation(tln[7], tln[3], ACT.Sqrt).then_inc(s("sqrt_ready"), 1)
                root(0)
                a.wait_ge(s("bias1_ps"), 1)
                a.activation(bias1t, bank[6][:, 0:2], ACT.Copy).then_inc(s("bias1_ready"), 1)
                a.activation(spare[:, 1:2], ident[0:P, 0:1], ACT.Relu)

                def out1_t(k, i, g):
                    a.wait_ge(s("out1_turned"), g + 1)
                    a.wait_ge(s("hidden_ps"), less(g, 1))
                    a.activation(ot[k], bank[k][:, 0:4 * P].rearrange("p (a b) -> p a b", a=2), ACT.Copy).then_inc(s("ot_ready"), 1)

                def relu(k, i, g):
                    a.wait_ge(s("bias1_ready"), 1)
                    a.wait_ge(s("hidden_ps"), g + 1)
                    a.wait_ge(s("ffn_ps"), less(g, 1))
                    for fh in (0, 1):
                        a.activation(ht[k][:, fh, :], bank[2 + k][:, fh * 2 * P:fh * 2 * P + 2 * P], ACT.Relu, bias=bias1t[:, fh:fh + 1]).then_inc(s("ht_ready"), 1)
                pipeline(a, [(0, out1_t), (1, relu)], NT // 2)
                root(1)
                for k in (0, 1):
                    a.wait_ge(s(f"xc_used{k}"), NT // 2)
                load_x("2")
                root(2)

                def xf_t(k, i, t):
                    a.wait_ge(s("xf_turned"), t + 1)
                    a.wait_ge(s("lg_ps"), less(t, 1))
                    a.activation(xft[k], bank[k][:, 0:2 * P].rearrange("p (a b) -> p a b", a=2), ACT.Copy).then_inc(s("xft_ready"), 1)
                pipeline(a, [(0, xf_t)])
                a.wait_ge(s("route"), 2)
                a.activation(rex, lg, ACT.Exp).then_inc(s("rexp"), 1)

            @block.tensor
            def _(pe):
                for m in (0, 1):
                    pe.wait_ge(s("proj_in"), 16)
                    for kh in (0, 1):
                        mm = pe.transpose(bank[0][:, kh * M + m * 128:kh * M + m * 128 + 128], projr[:, m, kh * 128:kh * 128 + 128], ident[:, :])
                mm.then_inc(s("projt_ps"), 1)
                pe.wait_ge(s("projt_ready"), 1)
                with pe.Fori(0, H) as h:
                    pe.wait_ge(s("w_in"), h * 112 + 112)
                    for m in range(3):
                        pe.wait_ge(s("wcen"), h * 3)
                        for dh in (0, 1):
                            pe.matmul(bank[m][:, 0:D], ones[:, :], wraw[:, m, dh, :], start=(dh == 0), stop=False)
                        pe.matmul(bank[m][:, 0:D], nones[0:1, :], brow[0:1, m, :], start=False, stop=True).then_inc(s("wsum_ps"), 1)
                    for m in range(3):
                        pe.wait_ge(s("wcen"), h * 3 + (m + 1))
                        pe.wait_ge(s("wt_ready"), h * 3 + m)
                        for kh in (0, 1):
                            for dh in (0, 1):
                                mm = pe.transpose(bank[3][:, kh * D + dh * 128:kh * D + dh * 128 + 128], wraw[:, m, dh, kh * 128:kh * 128 + 128], ident[:, :])
                        mm.then_inc(s("wt_ps"), 1)
                    for m in range(3):
                        pe.wait_ge(s("wt_ready"), h * 3 + (m + 1))
                        pe.wait_ge(s("prod_used"), h * 3)
                        rhs = projt if m < 2 else wo
                        for dh in (0, 1):
                            for kh in (0, 1):
                                mm = pe.matmul(bank[4 + m][:, dh * D:dh * D + D], wt[:, m, kh, dh * 128:dh * 128 + 128], rhs[:, kh, :], start=(kh == 0), stop=(kh == 1))
                        mm.then_inc(s("prod_ps"), 1)
                pe.wait_ge(s("prod_used"), H * 3)
                with pe.Fori(0, H) as h:
                    def features(w, ph_):
                        def step(k, i, t):
                            pe.wait_ge(s(f"{ph_}_exp"), h * NT + less(t, 3))
                            if ph_ == "k" and isinstance(t, int) and t == 2:
                                pe.wait_ge(s("q_acc"), h * NT)
                            n = 0
                            for xh, wh in ((0, 0), (0, 1), (1, 0)):
                                for dh in (0, 1):
                                    mm = pe.matmul(fbank[ph_][k][0:P, :], xt[:, ds(t, 1), 2 * xh + dh, 0:P].rearrange("p t n -> p (t n)"), w[:, wh, dh, :], start=(n == 0), stop=(n == 5))
                                    n += 1
                            mm.then_inc(s(f"{ph_}_u"), 1)
                        return step

                    def kv(k, i, t):
                        pe.wait_ge(s("k_ph"), h * NT + (t + 1))
                        for m in (0, 1):
                            for a, b in ((0, 0), (0, 1), (1, 0)):
                                mm = pe.matmul(bank[2 + m][:, 0:D + 1], ph[k][:, a, m * 128:m * 128 + 128], xa[b][:, ds(t, 1), 0:D + 1].rearrange("p t n -> p (t n)"),
                                               start=False, stop=False, skip_group_check=True)
                        mm.then_inc(s("k_kv"), 1)

                    pe.wait_ge(s("wk_in"), h * 16 + 16)
                    pe.wait_ge(s("zero_ready"), 1)
                    pe.wait_ge(s("kvs_ready"), h)
                    pe.wait_ge(s("q_exp"), h * NT)
                    for m in (0, 1):
                        pe.matmul(bank[2 + m][:, 0:D + 1], zero, xa[0][:, 0, 0:D + 1], start=True, stop=False, skip_group_check=True)
                    pipeline(pe, [(0, features(wc[1], "k")), (3, kv)], NT, 4)
                    pe.wait_ge(s("q_ph"), h * NT)
                    pe.wait_ge(s("kvs_ready"), h + 1)
                    for dh in (0, 1):
                        for m in (0, 1):
                            mm = pe.transpose(bank[4][:, dh * M + m * 128:dh * M + m * 128 + 128], kvs[:, m, dh * 128:dh * 128 + 128], ident[:, :])
                    mm.then_inc(s("kvt_ps"), 1)
                    pe.wait_ge(s("kvt_ready"), h + 1)
                    pe.wait_ge(s("bmat_in"), h * 16 + 16)
                    for m in (0, 1):
                        for dh in (0, 1):
                            mm = pe.matmul(bank[5][:, m * D:m * D + D], kvt[:, dh, m * 128:m * 128 + 128], bmat[:, dh, :], start=(dh == 0), stop=(dh == 1))
                    mm.then_inc(s("kvo_ps"), 1)
                    pe.wait_ge(s("wq_in"), h * 16 + 16)
                    pe.wait_ge(s("k_exp"), (h + 1) * NT)
                    pe.wait_ge(s("kvo_ready"), h + 1)

                    def turn(k, i, t):
                        pe.wait_ge(s("q_exp"), h * NT + (t + 1))
                        pe.wait_ge(s("q_ph"), h * NT + less(t, 1))
                        for m in (0, 1):
                            mm = pe.transpose(bank[4 + k % 2][:, m * 128:m * 128 + P], ex[k][:, m * 128:m * 128 + 128], ident[0:P, 0:P])
                        mm.then_inc(s("q_turned"), 1)

                    def attend(k, i, t):
                        pe.wait_ge(s("q_ph"), h * NT + (t + 1))
                        pe.wait_ge(s("q_acc"), h * NT + less(t, 1))
                        n = 0
                        for a, b in ((0, 0), (0, 1), (1, 0)):
                            for m in (0, 1):
                                mm = pe.matmul(bank[6 + k % 2][0:P, 0:D + 1], qt[k][:, a, m, 0:P], kvo[:, b, m, 0:D + 1], start=(n == 0), stop=(n == 5))
                                n += 1
                        mm.then_inc(s("q_att"), 1)

                    pipeline(pe, [(0, features(wc[0], "q")), (2, turn), (4, attend)], NT, 4)

                pe.wait_ge(s("tail_in"), 16 * 11)
                pe.wait_ge(s("q_acc"), H * NT)
                pe.transpose(bank[6][:, 0:2], b1r, ident[0:2, 0:2]).then_inc(s("bias1_ps"), 1)

                def turn_out1(k, i, g):
                    pe.wait_ge(s("out1_ready"), g + 1)
                    pe.wait_ge(s("ot_ready"), less(g, 1))
                    for dh in (0, 1):
                        for j in (0, 1):
                            mm = pe.transpose(bank[k][:, dh * 2 * P + j * P:dh * 2 * P + j * P + P],
                                              o1[k][:, j, dh * 128:dh * 128 + 128], ident[0:P, 0:P])
                    mm.then_inc(s("out1_turned"), 1)

                def ffn1(k, i, g):
                    pe.wait_ge(s("ot_ready"), g + 1)
                    pe.wait_ge(s("ht_ready"), less(g, 1) * 2)
                    for fh in (0, 1):
                        for dh in (0, 1):
                            mm = pe.matmul(bank[2 + k][:, fh * 2 * P:fh * 2 * P + 2 * P], W1s[:, dh, fh * 128:fh * 128 + 128], ot[k][:, dh, :], start=(dh == 0), stop=(dh == 1))
                    mm.then_inc(s("hidden_ps"), 1)

                def ffn2(k, i, g):
                    pe.wait_ge(s("ht_ready"), g * 2 + 2)
                    pe.wait_ge(s("ffn_added"), g)
                    for j in (0, 1):
                        for fh in (0, 1):
                            mm = pe.matmul(bank[4 + k][0:P, j * D:j * D + D], ht[k][:, fh, j * P:j * P + P], W2s[:, fh, :], start=(fh == 0), stop=(fh == 1))
                    mm.then_inc(s("ffn_ps"), 1)
                pipeline(pe, [(0, turn_out1), (1, ffn1), (2, ffn2)], NT // 2)

                def turn_xf(k, i, t):
                    pe.wait_ge(s("xf_ready"), t + 1)
                    pe.wait_ge(s("xft_ready"), less(t, 1))
                    for dh in (0, 1):
                        mm = pe.transpose(bank[k][:, dh * P:dh * P + P], xfs[k][:, dh * 128:dh * 128 + 128], ident[0:P, 0:P])
                    mm.then_inc(s("xf_turned"), 1)

                def gate_logits(k, i, t):
                    pe.wait_ge(s("xft_ready"), t + 1)
                    pe.wait_ge(s("logits"), t)
                    for dh in (0, 1):
                        mm = pe.matmul(bank[2 + k][0:P, 0:NE], xft[k][:, dh, :], gate[:, dh, :], start=(dh == 0), stop=(dh == 1))
                    mm.then_inc(s("lg_ps"), 1)
                pipeline(pe, [(0, turn_xf), (1, gate_logits)])
                pe.wait_ge(s("onehot_ready"), 1)
                oh = roh.rearrange("p t e -> p (t e)")
                pe.matmul(bank[0][0:P, 0:NT * NE], tri, oh, start=True, stop=True)
                pe.matmul(bank[1][0:P, 0:NT * NE], ones[0:P, 0:P], oh, start=True, stop=True).then_inc(s("counts_ps"), 1)


        next_part()

        with nc.Block() as block:
            @block.sync
            def _(sp):
                for k in range(CH):
                    sp.wait_ge(s(f"scattered{k}"), 16 * (NT // CH))

                def load_rows(k, i, t):
                    e, half = (i * 2 + k // 2), k % 2
                    if half == 0:
                        sp.wait_ge(s("ye_ready"), less(t, 2) * 2)
                        w1s, w2s = we[k // 2]
                        sp.dma_start(w1s, w1[ds(e, 1)].rearrange("e (a p) f -> p (e a) f", p=128)).then_inc(s(f"we_in{k // 2}"), 16)
                        sp.dma_start(w2s, w2[ds(e, 1)].rearrange("e (a p) d -> p (e a) d", p=128)).then_inc(s(f"we_in{k // 2}"), 16)
                        sp.dma_start(b2b[k // 2], b2[ds(e, 1), :].broadcast_to([P, D])).then_inc(s(f"b2_in{k // 2}"), 16)
                    sp.wait_ge(s("xe_turned"), less(t, 1))
                    sp.dma_start(xe[k % 2], ebuf[0:NE * CB].rearrange("(u j p) d -> u p j d", p=P, j=4)[ds(t, 1)].rearrange("u p j d -> p (u j) d")).then_inc(s(f"xe_in{k % 2}"), 16)

                def store_rows(k, i, t):
                    sp.wait_ge(s("ye_ready"), t * 2 + 2)
                    sp.dma_start(ybuf.rearrange("(u j p) d -> u p j d", p=P, j=4)[ds(t, 1)].rearrange("u p j d -> p (u j) d"), ye).then_inc(s("ye_out"), 16)
                pipeline(sp, [(0, load_rows), (2, store_rows)], 2 * NE, 4)
                ov = out.rearrange("(t p) d -> p t d", p=P)
                with sp.Fori(0, NT // CH) as i:
                    sp.wait_ge(s("out_ready"), i + 1)
                    sp.dma_start(ov[:, ds(i * CH, CH), :], acc[:, ds(i * CH, CH), :]).then_inc(s("out_stored"), 16)
                sp.wait_ge(s("out_stored"), 16 * (NT // CH))

            @block.gpsimd
            def _(pool):
                with pool.Fori(0, NT // CH) as i:
                    for k in range(CH):
                        hold(pool, f"scattered{k}", i * 16)
                        pool.tensor_copy(oslot[k], slot_out[:, ds(i * CH + k, 1)]).then_inc(s("oslot"), 1)
                        hold(pool, "oslot", i * CH + (k + 1))
                        hold(pool, f"xs_ready{k}", i + 1)
                        pool.indirect_dma_start(out=ebuf, out_offset=bass.IndirectOffsetOnAxis(ap=oslot[k], axis=0), in_=xs[k], in_offset=None).then_inc(s(f"scattered{k}"), 16)
                pool.wait_ge(s("ye_out"), 16 * 2 * NE)
                with pool.Fori(0, NT // CH // 2) as i:
                    for c in (0, 1):
                        hold(pool, f"yg_used{c}", i)
                        for k in range(CH):
                            pool.tensor_copy(islot[c * CH + k], slot_in[:, ds(i * 2 * CH + (c * CH + k), 1)]).then_inc(s("islot"), 1)
                            hold(pool, "islot", i * 2 * CH + (c * CH + k + 1))
                            pool.indirect_dma_start(out=yg[c][:, k, :], out_offset=None, in_=ybuf,
                                                    in_offset=bass.IndirectOffsetOnAxis(ap=islot[c * CH + k], axis=0)).then_inc(s(f"yg_in{c}"), 16)

            @block.vector
            def _(v):
                def per_row(col, t, n=CH):
                    return col[:, ds(t, n)].rearrange("p (t o) -> p t o", o=1).broadcast_to([P, n, D])


                with v.Fori(0, NT // CH) as i:
                    for k in range(CH):
                        v.wait_ge(s(f"scattered{k}"), i * 16)
                        t = i * CH + k
                        v.tensor_scalar(xs[k], acc[:, ds(t, 1), :].rearrange("p t d -> p (t d)"), mean[:, ds(t, 1)], rstd[:, ds(t, 1)], ALU.subtract, ALU.mult).then_inc(s(f"xs_ready{k}"), 1)

                v.wait_ge(s("b1t_ps"), 1)
                v.tensor_copy(b1t.rearrange("p a b -> p (a b)"), bank[7][:, 0:NE * F // 128]).then_inc(s("b1t_ready"), 1)
                def copy_rows(k, i, t):
                    v.wait_ge(s("xe_turned"), t + 1)
                    v.wait_ge(s("hid_block"), less(t, 1) * (F // 128))
                    for dh in (0, 1):
                        v.tensor_copy(xet[k % 2][:, dh, :], bank[dh][:, 0:4 * P]).then_inc(s("xet_ready"), 1)

                def add_b2(k, i, t):
                    v.wait_ge(s("ye_ps"), t + 1)
                    v.wait_ge(s(f"b2_in{k // 2}"), i * 16 + 16)
                    v.wait_ge(s("ye_out"), t * 16)
                    for j in (0, 1):
                        v.tensor_tensor(ye[:, 2 * j:2 * j + 2, :], bank[5 + j][0:P, :].rearrange("p (a b) -> p a b", a=2), b2b[k // 2][:, None, :].broadcast_to([P, 2, D]), ALU.add).then_inc(s("ye_ready"), 1)
                pipeline(v, [(0, copy_rows), (1, add_b2)], 2 * NE, 4)

                v.memset(fill[0], 0.0).then_inc(s("fills"), 1)
                v.memset(fill[1], 10000.0).then_inc(s("fills"), 1)
                v.memset(fill[2], -10000.0).then_inc(s("fills"), 1)
                v.wait_ge(s("fills"), 3)
                with v.Fori(0, NT // CH // 2) as i:
                    for k in (0, 1):
                        t, n = i * 2 * CH + k * CH, i * 12 + k * 6
                        v.wait_ge(s(f"yg_in{k}"), i * 16 * CH + 16 * CH)
                        v.tensor_tensor(yg[k], yg[k], per_row(pk, t), ALU.mult).then_inc(s("fin"), 1)
                        v.wait_ge(s("fin"), n + 1)
                        v.tensor_tensor(msk[0], yg[k], yg[k], ALU.not_equal).then_inc(s("fin"), 1)
                        v.tensor_scalar(msk[1], yg[k], 3.4028234e38, None, ALU.is_gt).then_inc(s("fin"), 1)
                        hold(v, "fin", n + 3, "dve")
                        v.copy_predicated(yg[k], msk[1], fill[1][:, None, :].broadcast_to([P, CH, D])).then_inc(s("fin"), 1)
                        hold(v, "fin", n + 4, "dve")
                        v.copy_predicated(yg[k], msk[0], fill[0][:, None, :].broadcast_to([P, CH, D])).then_inc(s("fin"), 1)
                        v.wait_ge(s("fin"), n + 5)
                        v.tensor_scalar(msk[1], yg[k], -3.4028234e38, None, ALU.is_lt).then_inc(s("fin"), 1)
                        hold(v, "fin", n + 6, "dve")
                        v.copy_predicated(yg[k], msk[1], fill[2][:, None, :].broadcast_to([P, CH, D])).then_inc(s("fin2"), 1)
                        v.wait_ge(s("fin2"), i * 2 + (k + 1))
                        at = acc[:, ds(t, CH), :]
                        v.tensor_tensor(at, at, yg[k], ALU.add).then_inc(s(f"yg_used{k}"), 1)
                        v.wait_ge(s(f"yg_used{k}"), i + 1)
                        v.sem_inc(s("out_ready"), 1)

            @block.scalar
            def _(a):
                for k in range(CH):
                    a.wait_ge(s(f"scattered{k}"), 16 * (NT // CH))
                a.dma_start(b1rows, b1.rearrange("e (a p) -> (e a) p", p=128)).then_inc(s("b1_in"), 16)
                a.wait_ge(s("b1t_ready"), 1)

                def hidden(k, i, t):
                    a.wait_ge(s("ye_ps"), t)
                    for fb in range(F // 128):
                        hold(a, "hid_block", t * (F // 128) + (fb + 1), "act")
                        a.activation(hid[:, fb, :], bank[2 + fb % 3][:, 0:4 * P], ACT.Relu, bias=b1t[:, ds(i * 2 + k // 2, 1), fb:fb + 1].rearrange("p a b -> p (a b)")).then_inc(s("hid_ready"), 1)
                pipeline(a, [(0, hidden)], 2 * NE, 4)

            @block.tensor
            def _(pe):
                pe.wait_ge(s("b1_in"), 16)
                pe.transpose(bank[7][:, 0:NE * F // 128], b1rows, ident[0:NE * F // 128, 0:NE * F // 128]).then_inc(s("b1t_ps"), 1)

                def turn_rows(k, i, t):
                    pe.wait_ge(s(f"xe_in{k % 2}"), i * 32 + (k // 2 * 16 + 16))
                    pe.wait_ge(s("xet_ready"), 2 * t)
                    for dh in (0, 1):
                        for j in range(4):
                            mm = pe.transpose(bank[dh][:, j * P:j * P + P], xe[k % 2][:, j, dh * 128:dh * 128 + 128], ident[0:P, 0:P])
                    mm.then_inc(s("xe_turned"), 1)

                def expert1(k, i, t):
                    pe.wait_ge(s("xet_ready"), 2 * t + 2)
                    pe.wait_ge(s(f"we_in{k // 2}"), i * 32 + 32)
                    for fb in range(F // 128):
                        if fb >= 3:
                            pe.wait_ge(s("hid_ready"), t * (F // 128) + (fb - 2))
                        else:
                            pe.wait_ge(s("hid_ready"), t * (F // 128))
                        for dh in (0, 1):
                            mm = pe.matmul(bank[2 + fb % 3][:, 0:4 * P], we[k // 2][0][:, dh, fb * 128:fb * 128 + 128], xet[k % 2][:, dh, :], start=(dh == 0), stop=(dh == 1))
                        mm.then_inc(s("hid_block"), 1)

                def expert2(k, i, t):
                    pe.wait_ge(s("hid_ready"), (t + 1) * (F // 128))
                    pe.wait_ge(s("ye_ready"), 2 * t)
                    for j in range(4):
                        for fb in range(F // 128):
                            mm = pe.matmul(bank[5 + j // 2][0:P, j % 2 * D:j % 2 * D + D], hid[:, fb, j * P:j * P + P], we[k // 2][1][:, fb, :], start=(fb == 0), stop=(fb == F // 128 - 1))
                    mm.then_inc(s("ye_ps"), 1)
                pipeline(pe, [(0, turn_rows), (1, expert1), (1, expert2)], 2 * NE, 4)


_INS = ["x", "src", "dst", "L0_gnn_W", "L0_gnn_att", "L0_gnn_b", "L0_mix_Wq", "L0_mix_bq", "L0_mix_Wk", "L0_mix_bk",
        "L0_mix_Wv", "L0_mix_bv", "L0_mix_Wo", "L0_mix_bo", "L0_mix_proj", "L0_mix_W1", "L0_mix_bias1", "L0_mix_W2",
        "L0_mix_bias2", "L0_mix_g1", "L0_mix_beta1", "L0_mix_g2", "L0_mix_beta2", "L0_ffn_gate_w", "L0_ffn_gate_b",
        "L0_ffn_w1", "L0_ffn_b1", "L0_ffn_w2", "L0_ffn_b2"]


def kernel(**inputs):
    import numpy as _np
    import concourse.bacc as _bacc
    from concourse import mybir as _mybir
    from concourse.bass_utils import run_bass_kernel_spmd as _run

    nc = _bacc.Bacc("TRN2", target_bir_lowering=False, num_devices=1)
    arrays, args = {}, []
    for name in _INS:
        a = _np.ascontiguousarray(inputs[name])
        arrays[f"in_{name}_dram"] = a
        args.append(nc.dram_tensor(f"in_{name}_dram", a.shape, _mybir.dt.from_np(a.dtype), kind="ExternalInput").ap())
    args.append(nc.dram_tensor("out_0_dram", (N, D), F32, kind="ExternalOutput").ap())
    gps_layer(nc, *args)
    r = _run(nc, [arrays], core_ids=[0])
    return r.results[0]["out_0_dram"]
```

```python
import math
from contextlib import ExitStack, contextmanager

import concourse.bass as bass
from concourse import mybir

F32, I32 = mybir.dt.float32, mybir.dt.int32
F16, BF16 = mybir.dt.float16, mybir.dt.bfloat16
ALU, ACT, AX = mybir.AluOpType, mybir.ActivationFunctionType, mybir.AxisListType
ds = bass.ds

N, D, E = 6250, 256, 200000
P = 125
NT = N // P
GH, GD = 4, 64
H, M = 8, 256
NE, F = 8, 1024
CAP = -(-5 * N // (4 * NE))
CT = 8
CB = CT * P
LOG16 = 2.772588722239781
LN_EPS, MIX_EPS, PHI_EPS = 1e-5, 1e-6, 1e-6
ROWW = D + GH
SR = 400
NS = E // SR
WIN, BLK = 64, 4
WB = WIN // BLK
SHIFT = 32.0
NBK = 64
NSB = -(-NBK * NT // 512)
CH = 5
LCH = 10


@contextmanager
def steps(engine, n, step):
    with engine.Fori(0, n // step) as i:
        yield i * step


def gps_layer(nc, x, src, dst, gW, gatt, gb, Wq, bq, Wk, bk, Wv, bv, Wo, bo, proj, W1, bias1, W2, bias2,
              g1, beta1, g2, beta2, gate_w, gate_b, w1, b1, w2, b2, out):
    ctx = ExitStack()
    with ctx:
        def sb(name, shape, dt=F32):
            return ctx.enter_context(nc.sbuf_tensor(name, shape, dt))

        def sem(name):
            return ctx.enter_context(nc.semaphore(name))

        def scratch(name, shape, dt=F32):
            return nc.dram_tensor(name, shape, dt, kind="Internal").ap()

        table = scratch("gather_table", [N + 1, ROWW])
        srcpad = scratch("src_padded", [E + WIN], I32)
        by_degree = scratch("nodes_by_degree", [N, 2], I32)
        sums = scratch("neighbour_sums", [N, ROWW])
        acc = sb("acc", [P, NT, D])
        xa_full = [sb(f"xa{i}", [128, NT, D + 2], F16) for i in (0, 1)]
        xa = [full[0:P] for full in xa_full]
        xt = xt_all = sb("xt", [128, NT, 4, 128], F16)
        mean = sb("mean", [P, NT])
        rstd = sb("rstd", [P, NT])
        wf = sb("wf", [P, NT, 2 * GH])
        ident = sb("ident", [128, 128])
        identh = sb("identh", [128, 128], F16)
        ones = sb("ones", [128, 128])
        spare = sb("spare", [P, 2])
        nones = sb("nones", [1, 128])
        bank = [ctx.enter_context(nc.psum_tensor(f"bank{i}", [128, 512], F32)) for i in range(8)]
        gacc = sb("gacc", [P, 2, BLK, ROWW])
        rank = sb("rank", [P, NT], I32)
        perm = sb("perm", [P, NT, 2], I32)
        nblk = sb("nblk", [1, 4, NT], I32)
        woff = [sb(f"woff{k}", [P, 1], I32) for k in (0, 1)]
        wrem = [sb(f"wrem{k}", [P, 1]) for k in (0, 1)]
        widx = [sb(f"widx{k}", [P, WIN], I32) for k in (0, 1)]
        wmask = sb("wmask", [P, WIN], I32)
        gidx = [sb(f"gidx{k}", [P, WIN], I32) for k in (0, 1)]
        kpos = sb("kpos", [P, WIN])
        zrow = sb("zrow", [1, ROWW])
        arena = sb("arena", [128, 9720])
        a_off = [0]

        def cut(shape, dt=F32, parts=128, at=None):
            n = math.prod(shape) * (2 if dt in (F16, BF16) else 4)
            o = a_off[0] if at is None else at
            a_off[0] = o + -(-n // 4)
            assert a_off[0] <= 9720, a_off[0]
            v = arena[0:parts, o:o + -(-n // 4)]
            if dt != F32:
                v = v.bitcast(dt)
            if len(shape) == 2:
                v = v.rearrange("p (a b) -> p a b", b=shape[1])
            if len(shape) == 3:
                v = v.rearrange("p (a b c) -> p a b c", b=shape[1], c=shape[2])
            if len(shape) == 4:
                v = v.rearrange("p (a b c d) -> p a b c d", b=shape[1], c=shape[2], d=shape[3])
            return v

        a_off[0] = 0
        st6 = cut([NT, 6], F32, P)
        stt = [cut([NT], F32, P) for _ in range(9)]
        eps = cut([1], F32, P)
        shf = cut([1], F32, P)
        gwf = cut([2, D])
        gw = cut([2, 2, D], F16)
        attb = cut([2, D], F32, P)
        lk = cut([CH, D], F32, P)
        tat_at = a_off[0]
        tat = cut([CH * 2, D], F32, P)
        mx = cut([2 * GH], F32, P)
        mxa = cut([2 * GH], F32, P)
        firsts = cut([NS], F32, P + 1)
        first1 = arena[0:1, tat_at:tat_at + NS].bitcast(I32)
        first1f = arena[0:1, tat_at + NS:tat_at + 2 * NS]
        dq = cut([NT], F32, P + 1)
        cnt1 = cut([NT], F32, P + 1)
        cnt2 = cut([NT], F32, P + 1)
        offf = cut([NT], F32, P + 1)
        ri = cut([NT], I32, P + 1)
        junk_at = a_off[0]
        junk = cut([2, 512], F16, P + 1)
        rslot = [cut([1], I32, P + 1) for _ in range(CH)]
        drow_at = a_off[0]
        drow = cut([CH, SR], I32, P + 1)
        srcs = arena[0:P, drow_at:drow_at + E // P].bitcast(I32)
        offT = cut([P + 1], F32, NT)
        degT = cut([P], F32, NT)
        mxd = cut([4], F32, NT)
        lk_at = tat_at - CH * D
        tot = arena[0:P, lk_at:lk_at + NBK * NT].rearrange("p (b t) -> p b t", t=NT)
        tri = arena[0:P, junk_at:junk_at + P]
        trih = arena[0:P, junk_at + 126:junk_at + 190].bitcast(BF16)[:, 0:P]
        onesh = arena[0:P, junk_at + 190:junk_at + 254].bitcast(BF16)[:, 0:P]
        bids_i = arena[0:P, junk_at + 254:junk_at + 254 + NBK].bitcast(I32)
        bids = arena[0:P, junk_at + 320:junk_at + 320 + NBK]
        oh = arena[0:P, drow_at:drow_at + NBK * NT // 2].bitcast(BF16).rearrange("p (b t) -> p b t", t=NT)
        o = drow_at + NBK * NT // 2
        nrow = arena[0:1, o:o + 4 * NT].rearrange("p (a b) -> p a b", b=NT)
        nsum = arena[0:1, o + 4 * NT:o + 6 * NT].rearrange("p (a b) -> p a b", b=NT)
        entry = arena[0:P, o + 6 * NT:o + 8 * NT].bitcast(I32).rearrange("p (t a) -> p t a", a=2)
        bucket = cnt1[0:P]
        degs = arena[0:P, tat_at + 2000:tat_at + 2000 + NT]
        pslot = [arena[0:P, tat_at + 2050 + 15 * c:tat_at + 2055 + 15 * c].bitcast(I32) for c in (0, 1)]
        eslot = [arena[0:P, tat_at + 2055 + 15 * c:tat_at + 2065 + 15 * c].bitcast(I32).rearrange("p (t a) -> p t a", a=2) for c in (0, 1)]
        mxi = cut([2], I32, NT)

        a_off[0] = 0
        wc = [cut([2, 2, 2 * D], F16) for _ in (0, 1)]
        bmat = cut([2, D])
        wbase = a_off[0]
        ex = [cut([M], F32, P) for _ in range(4)]
        sqj = [cut([M], F32, P) for _ in range(4)]
        sq = [cut([1], F32, P) for _ in range(4)]
        nsq = [cut([1], F32, P) for _ in range(4)]
        ph = [cut([2, M], BF16, P) for _ in range(4)]
        kvs = cut([2, D + 2])
        kvt = cut([2, M])
        kvo = cut([2, 2, D + 2], BF16)
        qt = [cut([2, 2, 128], BF16) for _ in range(4)]
        rz = [cut([1], F32, P) for _ in range(4)]
        fbank = {"k": [bank[j] for j in (0, 1, 6, 7)], "q": [bank[j] for j in (0, 1, 2, 3)]}
        zero = cut([128], BF16, P)
        mix_end = a_off[0]
        a_off[0] = wbase
        wraw = cut([3, 2, D])
        wo = cut([2, D])
        brow = cut([3, D], F32, 1)
        brow_bo = cut([D], F32, P)
        wt = cut([3, 2, D])
        projr = cut([2, D])
        projt = cut([2, M])
        wcat = scratch("mix_weights", [H, 2, 128, 2 * 2 * 2 * D], F16)
        bdram = scratch("mix_wv_wo", [H, 128, 2 * D])

        a_off[0] = 0
        tst = cut([NT, 6], F32, P)
        tln = [cut([NT], F32, P) for _ in range(8)]
        slot_out = cut([NT], I32, P)
        slot_in = cut([NT], I32, P)
        pk = cut([NT], F32, P)
        b1t = cut([NE, F // 128])
        flags = cut([2 * NE], F32, P)
        bad = cut([2], F32, P)
        badi = cut([1], I32, P)
        gate = cut([2, NE])
        gateb = cut([NE], F32, P)
        tail = a_off[0]
        g1b, beta1b, g2b, beta2b, bias2b, gnnb = (cut([D], F32, P) for _ in range(6))
        W1s, W2s = (cut([2, D]) for _ in (0, 1))
        b1r = cut([128], F32, 2)
        bias1t = cut([2])
        xc = [cut([CH, D], F32, P) for _ in (0, 1)]
        fbase = a_off[0]
        ot = [cut([2, 2 * P]) for _ in (0, 1)]
        ht = [cut([2, 2 * P]) for _ in (0, 1)]
        a_off[0] = fbase
        a_off[0] = tail
        gs = [cut([CH, ROWW], F32, P) for _ in (0, 1)]
        own = [cut([CH, ROWW], F32, P) for _ in (0, 1)]
        gslot = [cut([CH], I32, P) for _ in (0, 1)]
        zw = cut([NT, GH], F32, P)
        zpart = cut([GH], F32, P)
        zall = cut([GH], F32, P)
        assert a_off[0] < fbase + 500
        a_off[0] = fbase + 500
        scaled = xt_all[:, :, :, :].rearrange("p t j n -> p (t j n)").bitcast(F32)[0:P].rearrange("p (t d) -> p t d", d=D)
        lg = cut([NT, NE], F32, P)
        a_off[0] = fbase + 1000
        xft = [cut([2, P]) for _ in range(4)]
        o1 = [xc[k][:, 0:2, :] for k in (0, 1)]
        xfs = [xc[k // 2][:, k % 2, :] for k in range(4)]
        a_off[0] = tail
        rmax, rsum, rinv, ridx, rpos, rkept, rdump, rslot_o, rtmp = (cut([NT], F32, P) for _ in range(9))
        rex, roh, rtot, rscan, rall = (cut([NT, NE], F32, P) for _ in range(5))
        upper = cut([P], F32, P)
        down = cut([NE], F32, P)
        downi = cut([NE], I32, P)
        node = cut([NT], I32, P)
        xs = [cut([D], F32, P) for _ in range(CH)]
        oslot = [cut([1], I32, P) for _ in range(CH)]
        assert a_off[0] < fbase
        a_off[0] = tail
        xe = [cut([4, D], F32, P) for _ in (0, 1)]
        xet = [cut([2, 2, 4 * P], F16) for _ in (0, 1)]
        hid0 = cut([2, F // 128, 4 * P], F16)
        b1rows = arena[0:NE * F // 128, a_off[0] - 4 * P:a_off[0] - 4 * P + 128]
        xt_words = xt_all[:, :, :, :].rearrange("p t j n -> p (t j n)").bitcast(F32)
        WW = 2 * F + F // 128 * D
        ws = []
        for k in (0, 1):
            w = xt_words[:, k * WW:k * WW + WW]
            ws.append((w[:, 0:2 * F].rearrange("p (a f) -> p a f", a=2), w[:, 2 * F:WW].rearrange("p (a d) -> p a d", d=D)))
        hid = [hid0, xt_words[:, 2 * WW:2 * WW + F // 128 * 4 * P].bitcast(F16).rearrange("p (h a b) -> p h a b", h=2, a=F // 128)]
        relus = [cut([4 * P]), xt_words[:, 2 * WW + F // 128 * 4 * P:2 * WW + (F // 128 + 1) * 4 * P]]
        gflat = gacc[:, :, :, :].rearrange("p a b c -> p (a b c)")
        ye = gflat[:, 0:4 * D].rearrange("p (a b) -> p a b", b=D)
        b2b = [gflat[:, (4 + k) * D:(5 + k) * D] for k in (0, 1)]
        junk_y = gflat[:, 6 * D:8 * D].bitcast(BF16).rearrange("p (a b) -> p a b", b=D)
        we = []
        for full in xa_full:
            w = full[:, :, :].rearrange("p t d -> p (t d)")
            we.append((w[:, 0:4 * F].rearrange("p (h a f) -> p h a f", h=2, a=2), w[:, 4 * F:2 * WW].rearrange("p (h a d) -> p h a d", h=2, d=D)))
        a_off[0] = tail
        yg = [cut([CH, D], F32, P) for _ in (0, 1)]
        msk = [cut([CH, D], I32, P) for _ in (0, 1)]
        fill = [cut([D], F32, P) for _ in range(3)]
        islot = [cut([1], I32, P) for _ in range(2 * CH)]
        ebuf = scratch("expert_rows", [NE * CB + N, D])
        ybuf = scratch("expert_out", [NE * CB, D])

        S, kept = {}, {}
        def s(name):
            if name in kept:
                return kept[name]
            if name not in S:
                S[name] = nc.alloc_semaphore(name)
            return S[name]

        for name in [f"row_in{k}" for k in range(CH)] + ["widx_in", "more_in", "entries_out0", "entries_out1", "gs_in0", "gs_in1"] + [f"added{j}" for j in range(BLK)] + [f"scattered{k}" for k in range(CH)] + ["yg_in0", "yg_in1"]:
            kept[name] = sem(name)

        def next_part():
            for handle in S.values():
                nc.gpsimd.sem_clear(handle)
                nc.release_semaphore(handle)
            S.clear()
            nc.all_engine_barrier()

        def hold(e, name, value, who="pool"):
            e.wait_ge(s(name), value)
            e.sem_inc(s(who + "_passed"), 1)

        xv = x.rearrange("(t p) d -> p t d", p=P)

        def split_weights(pool, c, name, n):
            for m in (0, 1):
                pool.tensor_copy(we[c][m][:, 0], ws[c][m]).then_inc(s(name + "_hi"), 1)
            hold(pool, name + "_hi", n * 2 + 2)
            for m in (0, 1):
                pool.tensor_tensor(we[c][m][:, 1], ws[c][m], we[c][m][:, 0], ALU.subtract).then_inc(s(name), 1)

        def less(t, n):
            return max(t - n, 0) if isinstance(t, int) else t + -n

        def pipeline(e, stages, n=NT, un=2):
            lag = max(a for a, _ in stages)
            ramp = lag + un - 1
            rounds = (n - ramp) // un
            for t in range(ramp):
                for a, step in stages:
                    if t >= a:
                        step((t - a) % un, (t - a) // un, t - a)
            with e.Fori(0, rounds) as i:
                for u in range(un):
                    for a, step in stages:
                        o = ramp + u - a
                        step(o % un, i + o // un, i * un + o)
            for t in range(ramp + un * rounds, n + lag):
                for a, step in stages:
                    if t - a < n:
                        step((t - a) % un, (t - a) // un, t - a)


        with nc.Block() as block:
            @block.sync
            def _(sp):
                sp.dma_start(first1, dst.rearrange("(a b) -> a b", b=SR)[:, 0:1].rearrange("a b -> b a"), allow_slow_non_contiguous=True).then_inc(s("firsts_in"), 16)
                sp.dma_start(srcs, src.rearrange("(p b) -> p b", p=P)).then_inc(s("src_in"), 16)
                for c in range(NT // LCH):
                    sp.dma_start(acc[:, c * LCH:(c + 1) * LCH, :], xv[:, c * LCH:(c + 1) * LCH, :]).then_inc(s(f"x_in{c}"), 16)
                sp.dma_start(gwf, gW.rearrange("(a p) n -> p a n", p=128)).then_inc(s("gw_in"), 16)
                av = gatt.rearrange("o h (s d) -> o s h d", s=2)
                for k in (0, 1):
                    sp.dma_start(attb[:, k, :].rearrange("p (h d) -> p h d", d=GD),
                                 av[:, k].broadcast_to([P, GH, GD])).then_inc(s("att_in"), 16)
                sp.wait_ge(s("src_plus"), 1)
                sp.dma_start(srcpad[0:E].rearrange("(p b) -> p b", p=P), srcs).then_inc(s("src_out"), 16)
                sp.wait_ge(s("zeros_ready"), 1)
                sp.dma_start(srcpad[E:E + WIN].rearrange("(o n) -> o n", o=1), zrow[0:1, 0:WIN].bitcast(I32)).then_inc(s("src_out"), 16)
                sp.dma_start(table[0:1, :], zrow[:, :]).then_inc(s("table_in"), 16)
                tv = table[1:N + 1, :].rearrange("(t p) d -> p t d", p=P)
                sp.wait_ge(s("w_ready"), 1)
                sp.dma_start(tv[:, :, D:D + GH], wf[:, :, 0:GH]).then_inc(s("table_in"), 16)
                with steps(sp, NT, CH) as t:
                    sp.wait_ge(s("g_ready"), t + CH)
                    sp.dma_start(tv[:, ds(t, CH), 0:D], acc[:, ds(t, CH), :]).then_inc(s("table_in"), 16)
                sp.wait_ge(s("gacc_zero"), 1)
                for c in range(NE * CB * D // (P * 8 * D)):
                    sp.dma_start(ebuf[0:NE * CB, :].rearrange("(c p r) d -> c p (r d)", p=P, r=8)[c], gacc[:, :, :, :].rearrange("p a b c -> p (a b c)")[:, 0:8 * D]).then_inc(s("ebuf_zero"), 16)
                sp.wait_ge(s("ebuf_zero"), 16 * (NE * CB // (P * 8)))
                sp.wait_ge(s("table_in"), 16 * (2 + NT // CH))

            @block.gpsimd
            def _(pool):
                pool.memset(zrow[:, :], 0.0).then_inc(s("zeros_ready"), 1)
                pool.memset(gacc[:, :, :, :].rearrange("p a b c -> p (a b c)")[:, 0:8 * D], 0.0).then_inc(s("gacc_zero"), 1)
                pool.memset(ones[:, :], 1.0).then_inc(s("ones_ready"), 1)
                pool.memset(nones[:, :], -1.0).then_inc(s("ones_ready"), 1)
                pool.memset(ident[:, :], 0.0).then_inc(s("id0"), 1)
                pool.wait_ge(s("id0"), 1)
                pool.affine_select(out=ident[:, :], in_=ident[:, :], compare_op=ALU.not_equal, fill=1.0, base=0,
                                   pattern=[[-1, 128]], channel_multiplier=1).then_inc(s("ident_ready"), 1)
                pool.wait_ge(s("ident_ready"), 1)
                pool.tensor_copy(identh[:, :], ident[:, :]).then_inc(s("identh_ready"), 1)
                pool.iota(ri, pattern=[[P, NT]], base=0, channel_multiplier=1).then_inc(s("iotas"), 1)
                pool.iota(gidx[0][:, :], pattern=[[1, WIN]], base=0, channel_multiplier=0).then_inc(s("iotas"), 1)
                pool.memset(eps, LN_EPS).then_inc(s("eps_ready"), 1)
                pool.memset(shf, SHIFT).then_inc(s("eps_ready"), 1)
                pool.wait_ge(s("iotas"), 2)
                pool.tensor_copy(dq, ri).then_inc(s("dq_ready"), 1)
                pool.tensor_copy(kpos[:, :], gidx[0][:, :]).then_inc(s("kpos_ready"), 1)
                for k in (0, 1):
                    pool.memset(xa[k][:, :, D:D + 2], 1.0 - k).then_inc(s("xa_ones"), 1)
                pool.wait_ge(s("src_in"), 16)
                pool.tensor_scalar(srcs, srcs, 1.0, None, ALU.add).then_inc(s("src_plus"), 1)
                pool.wait_ge(s("src_out"), 32)
                pool.wait_ge(s("ri_ready"), 1)
                with steps(pool, NT, CH) as t:
                    for k in range(CH):
                        pool.wait_ge(s("rows_counted"), t)
                        pool.tensor_copy(rslot[k], ri[:, ds(t + k, 1)]).then_inc(s("rslot_ready"), 1)
                        hold(pool, "rslot_ready", t + (k + 1))
                        pool.indirect_dma_start(out=drow[:, k, :], out_offset=None, in_=dst.rearrange("(a b) -> a b", b=SR),
                                                in_offset=bass.IndirectOffsetOnAxis(ap=rslot[k], axis=0)).then_inc(s(f"row_in{k}"), 16)
                pool.wait_ge(s("mx_ready"), 1)
                pool.partition_all_reduce(mxa, mx, P, bass.bass_isa.ReduceOp.max).then_inc(s("mxa_ready"), 1)
                pool.wait_ge(s("rows_counted"), NT)
                pool.memset(tri, -1.0).then_inc(s("sort_consts"), 1)
                pool.tensor_copy(onesh, ones[0:P, 0:P]).then_inc(s("sort_consts"), 1)
                pool.iota(bids_i, pattern=[[1, NBK]], base=0, channel_multiplier=0).then_inc(s("sort_consts"), 1)
                pool.wait_ge(s("sort_consts"), 3)
                pool.affine_select(out=tri, in_=tri, compare_op=ALU.is_ge, fill=0.0, base=-1, pattern=[[-1, P]], channel_multiplier=1).then_inc(s("sort_consts"), 1)
                pool.tensor_copy(bids, bids_i).then_inc(s("sort_consts"), 1)
                pool.wait_ge(s("sort_consts"), 5)
                pool.tensor_copy(trih, tri).then_inc(s("sort_consts"), 1)
                pool.wait_ge(s("rank_ready"), 1)
                pool.wait_ge(s("entry_ready"), 2)
                with pool.Fori(0, NT // CH // 2) as i:
                    for c in (0, 1):
                        t = i * 2 * CH + c * CH
                        hold(pool, f"entries_out{c}", i * 16 * CH)
                        pool.tensor_copy(pslot[c], rank[:, ds(t, CH)]).then_inc(s("entry_slot"), 1)
                        pool.tensor_copy(eslot[c].bitcast(F32), entry[:, ds(t, CH), :].bitcast(F32)).then_inc(s("entry_slot"), 1)
                        hold(pool, "entry_slot", i * 4 + (c * 2 + 2))
                        for j in range(CH):
                            pool.indirect_dma_start(out=by_degree, out_offset=bass.IndirectOffsetOnAxis(ap=pslot[c][:, j:j + 1], axis=0),
                                                    in_=eslot[c][:, j, :], in_offset=None).then_inc(s(f"entries_out{c}"), 16)
            @block.vector
            def _(v):
                v.wait_ge(s("firsts_in"), 16)
                v.tensor_copy(first1f, first1).then_inc(s("first1f_ready"), 1)
                v.wait_ge(s("firsts_bcast"), 1)
                v.tensor_copy(firsts, bank[7][0:P + 1, 0:NS]).then_inc(s("firsts_ready"), 1)
                v.wait_ge(s("firsts_ready"), 1)
                v.wait_ge(s("dq_ready"), 1)
                with steps(v, NT, 2) as t:
                    for k in (0, 1):
                        v.wait_ge(s("cnt1"), t + (k - 1) if k else t)
                        v.tensor_scalar(junk[:, k, 0:NS], firsts, dq[:, ds(t + k, 1)], 0.0, ALU.is_lt, ALU.add,
                                        accum_out=cnt1[:, ds(t + k, 1)]).then_inc(s("cnt1"), 1)
                v.wait_ge(s("cnt1"), NT)
                v.tensor_scalar(ri, cnt1, -1.0, 0.0, ALU.add, ALU.max).then_inc(s("ri_ready"), 1)

                for c in range(NT // LCH):
                    v.wait_ge(s(f"x_in{c}"), 16)
                    with v.Fori(c * LCH, (c + 1) * LCH) as t:
                        v.bn_stats(st6[:, ds(t, 1), :].rearrange("p t a -> p (t a)"), acc[:, ds(t, 1), :].rearrange("p t d -> p (t d)")).then_inc(s("stats"), 1)
                v.wait_ge(s("stats"), NT)
                me, ve, mo, vo = st6[:, :, 1], st6[:, :, 2], st6[:, :, 4], st6[:, :, 5]
                q, dm, vs, ve_, va, r0, r2, r3 = stt[0:8]
                v.tensor_tensor(q, me, mo, ALU.add).then_inc(s("ln"), 1)
                v.tensor_tensor(dm, me, mo, ALU.subtract).then_inc(s("ln"), 1)
                v.tensor_tensor(vs, ve, vo, ALU.add).then_inc(s("ln"), 1)
                v.wait_ge(s("ln"), 3)
                v.tensor_scalar(mean[:, :], q, 0.5, None, ALU.mult).then_inc(s("ln"), 1)
                v.scalar_tensor_tensor(r0, dm, 0.25, dm, ALU.mult, ALU.mult).then_inc(s("ln"), 1)
                v.wait_ge(s("ln"), 5)
                v.scalar_tensor_tensor(va, vs, 1.0 / D, r0, ALU.mult, ALU.add).then_inc(s("ln"), 1)
                v.wait_ge(s("ln"), 6)
                v.tensor_scalar(ve_, va, LN_EPS, None, ALU.add).then_inc(s("var_ready"), 1)
                v.wait_ge(s("sqrt_ready"), 1)
                v.reciprocal(r2, r3).then_inc(s("ln"), 1)
                v.wait_ge(s("ln"), 7)
                v.tensor_tensor(q, r2, r2, ALU.mult).then_inc(s("ln"), 1)
                v.wait_ge(s("ln"), 8)
                v.scalar_tensor_tensor(dm, q, -0.5, ve_, ALU.mult, ALU.mult).then_inc(s("ln"), 1)
                v.wait_ge(s("ln"), 9)
                v.scalar_tensor_tensor(rstd[:, :], dm, 1.5, r2, ALU.add, ALU.mult).then_inc(s("ln"), 1)
                v.wait_ge(s("ln"), 10)
                v.wait_ge(s("colsum"), 1)
                v.scalar_tensor_tensor(gwf, bank[6][:, None, 0:D].broadcast_to([128, 2, D]), -1.0 / D, gwf, ALU.mult, ALU.add).then_inc(s("gwc"), 1)
                v.wait_ge(s("gwc"), 1)
                v.tensor_copy(gw[:, 0], gwf).then_inc(s("gwh"), 1)
                v.wait_ge(s("gwh"), 1)
                v.tensor_tensor(gw[:, 1], gwf, gw[:, 0], ALU.subtract).then_inc(s("gw_ready"), 1)
                with v.Fori(0, NT // CH) as i:
                    t = i * CH
                    for k in range(CH):
                        xn = acc[:, ds(t + k, 1), :]
                        v.tensor_scalar(xn, xn, mean[:, ds(t + k, 1)], rstd[:, ds(t + k, 1)], ALU.subtract, ALU.mult).then_inc(s("xn"), 1)
                    v.wait_ge(s("xn"), t + CH)
                    xn = acc[:, ds(t, CH), :]
                    hi, lo = (xa[k][:, ds(t, CH), 0:D] for k in (0, 1))
                    v.tensor_scalar(hi, xn, 1.0, None, ALU.add).then_inc(s("xa_hi"), CH)
                    v.wait_ge(s("xa_hi"), t + CH)
                    v.scalar_tensor_tensor(lo, xn, 1.0, hi, ALU.add, ALU.subtract).then_inc(s("xa_ready"), CH)
                    for k in range(CH):
                        v.wait_ge(s(f"row_in{k}"), i * 16 + 16)
                        if k >= 2:
                            v.wait_ge(s("cnt2"), t + (k - 1))
                        else:
                            v.wait_ge(s("cnt2"), t)
                        v.tensor_scalar(junk[:, k % 2, 0:SR], drow[:, k, :], dq[:, ds(t + k, 1)], 0.0, ALU.is_lt, ALU.add,
                                        accum_out=cnt2[:, ds(t + k, 1)]).then_inc(s("cnt2"), 1)
                    v.wait_ge(s("cnt2"), t + CH)
                    v.sem_inc(s("rows_counted"), CH)
                v.wait_ge(s("att_in"), 32)
                with v.Fori(0, NT // CH) as i:
                    t = i * CH
                    v.wait_ge(s("h_ready"), t + CH)
                    v.wait_ge(s("scored"), t)
                    ht = acc[:, ds(t, CH), :]
                    v.scalar_tensor_tensor(lk, ht, 0.2, ht, ALU.mult, ALU.max).then_inc(s("leaky"), CH)
                    v.wait_ge(s("leaky"), t + CH)
                    t4 = tat.rearrange("p (c s) d -> p c s d", s=2)
                    v.tensor_tensor(t4, lk[:, :, None, :].broadcast_to([P, CH, 2, D]), attb[:, None, :, :].broadcast_to([P, CH, 2, D]), ALU.mult).then_inc(s("tat_ready"), CH)
                    v.wait_ge(s("tat_ready"), t + CH)
                    v.tensor_reduce(wf[:, ds(t, CH), :].rearrange("p t h -> p (t h)"), tat.rearrange("p c (h d) -> p (c h) d", d=GD), AX.X, ALU.add).then_inc(s("scored"), CH)
                v.wait_ge(s("scored"), NT)
                v.tensor_reduce(mx, wf[:, :, :].rearrange("p t h -> p h t"), AX.X, ALU.max).then_inc(s("mx_ready"), 1)
                v.scalar_tensor_tensor(offf, ri, float(SR), cnt2, ALU.mult, ALU.add).then_inc(s("off_ready"), 1)
                v.wait_ge(s("off_ready"), 1)
                v.wait_ge(s("mx_ready"), 1)
                v.tensor_copy(entry[:, :, 0], offf[0:P]).then_inc(s("entry_ready"), 1)
                v.wait_ge(s("off_t"), 1)
                v.tensor_copy(offT, bank[7][0:NT, 0:P + 1]).then_inc(s("offT"), 1)
                v.wait_ge(s("offT"), 1)
                v.tensor_tensor(degT, offT[:, 1:P + 1], offT[:, 0:P], ALU.subtract).then_inc(s("degT"), 1)
                v.wait_ge(s("deg_t"), 1)
                v.tensor_copy(entry[:, :, 1].bitcast(F32), bank[6][0:P, 0:NT]).then_inc(s("entry_ready"), 1)
                v.tensor_scalar(bucket, bank[6][0:P, 0:NT], float(NBK - 1), None, ALU.min).then_inc(s("bucket_ready"), 1)
                v.wait_ge(s("sort_consts"), 6)
                v.wait_ge(s("bucket_ready"), 1)
                v.tensor_tensor(oh, bids[:, :, None].broadcast_to([P, NBK, NT]), bucket[:, None, :].broadcast_to([P, NBK, NT]), ALU.is_equal).then_inc(s("oh_ready"), 1)
                v.wait_ge(s("tot_ready"), NSB)
                flat = tot.rearrange("p b t -> p (b t)")
                v.tensor_tensor_scan(flat, flat, flat, 0.0, ALU.add, ALU.bypass).then_inc(s("sorting"), 1)
                v.wait_ge(s("sorting"), 1)
                v.wait_ge(s("below_ps"), NSB)
                for c in range(NSB):
                    n = min(512, NBK * NT - 512 * c)
                    v.tensor_tensor(flat[:, 512 * c:512 * c + n], flat[:, 512 * c:512 * c + n], bank[c][0:P, 0:n], ALU.add).then_inc(s("sorting"), 1)
                v.wait_ge(s("sorting"), 1 + NSB)
                v.tensor_tensor(tot, tot, oh, ALU.mult).then_inc(s("sorting"), 1)
                v.wait_ge(s("sorting"), 2 + NSB)
                v.tensor_reduce(bucket, tot.rearrange("p b t -> p t b"), AX.X, ALU.add).then_inc(s("sorting"), 1)
                v.wait_ge(s("sorting"), 3 + NSB)
                v.tensor_scalar(rank[:, :], bucket, -1.0, None, ALU.add).then_inc(s("rank_ready"), 1)
                v.wait_ge(s("mxa_ready"), 1)
                v.tensor_tensor(wf[:, :, :], wf[:, :, :], mxa[:, None, :].broadcast_to([P, NT, 2 * GH]), ALU.subtract).then_inc(s("score_shifted"), 1)
                v.wait_ge(s("w_ready"), 1)
                with steps(v, NT, CH) as t:
                    g4 = acc[:, ds(t, CH), :].rearrange("p t (h d) -> p t h d", d=GD)
                    v.tensor_tensor(g4, g4, wf[:, ds(t, CH), 0:GH].rearrange("p t (h o) -> p t h o", o=1).broadcast_to([P, CH, GH, GD]), ALU.mult).then_inc(s("g_ready"), CH)
                v.wait_ge(s("sorted_t"), 1)
                v.tensor_reduce(mxd[:, 0:1], bank[5][0:NT, 0:P], AX.X, ALU.max).then_inc(s("mxd"), 1)
                v.wait_ge(s("mxd"), 1)
                v.tensor_scalar(mxi[:, 0:1], mxd[:, 0:1], 1.0, float(BLK - 1), ALU.max, ALU.add).then_inc(s("mxd"), 1)
                v.tensor_scalar(mxi[:, 1:2], mxd[:, 0:1], 1.0, -1.0, ALU.max, ALU.add).then_inc(s("mxd"), 1)
                v.wait_ge(s("mxd"), 3)
                v.tensor_scalar(mxi[:, 0:1], mxi[:, 0:1], 2, None, ALU.arith_shift_right).then_inc(s("mxd"), 1)
                v.tensor_scalar(mxi[:, 1:2], mxi[:, 1:2], 6, None, ALU.arith_shift_right).then_inc(s("mxd"), 1)
                v.wait_ge(s("mxd"), 5)
                v.tensor_scalar(mxd[:, 0:1], mxi[:, 0:1], float(WB), None, ALU.min).then_inc(s("mxd"), 1)
                v.tensor_copy(mxd[:, 1:2], mxi[:, 1:2]).then_inc(s("mxd"), 1)
                v.wait_ge(s("mxd"), 7)
                v.tensor_scalar(mxd[:, 3:4], mxd[:, 1:2], float(WB), None, ALU.mult).then_inc(s("mxd"), 1)
                v.wait_ge(s("mxd"), 8)
                v.tensor_tensor(mxd[:, 2:3], mxd[:, 3:4], mxd[:, 0:1], ALU.add).then_inc(s("mxd"), 1)
                v.wait_ge(s("nblk_t"), 1)
                v.tensor_copy(nrow, bank[4][0:1, 0:4 * NT].rearrange("p (a b) -> p a b", b=NT)).then_inc(s("nrow"), 1)
                v.wait_ge(s("nrow"), 1)
                for k, what in ((0, 2), (1, 1)):
                    v.tensor_tensor_scan(nsum[:, k, :], nrow[:, what, :], nrow[:, what, :], 0.0, ALU.add, ALU.bypass).then_inc(s("nrow"), 1)
                v.wait_ge(s("nrow"), 3)
                for k, what in ((0, 2), (1, 1)):
                    v.tensor_tensor(nblk[:, 2 + k, :], nsum[:, k, :], nrow[:, what, :], ALU.subtract).then_inc(s("nrow"), 1)
                v.tensor_copy(nblk[:, 0:2, :], nrow[:, 0:2, :]).then_inc(s("nrow"), 1)

            @block.scalar
            def _(a):
                a.wait_ge(s("var_ready"), 1)
                a.activation(stt[7], stt[3], ACT.Sqrt).then_inc(s("sqrt_ready"), 1)
                a.wait_ge(s("eps_ready"), 2)
                a.activation(stt[8][:, 0:1], shf, ACT.Exp, scale=0.0).then_inc(s("exp_table"), 1)
                with steps(a, NT, 2) as t:
                    for k in (0, 1):
                        a.wait_ge(s("xt_ps"), t + (k + 1))
                        a.activation(xt[:, ds(t + k, 1), :, 0:P].rearrange("p t j n -> p (t j) n"),
                                     bank[k][:, 0:256].bitcast(F16).rearrange("p (j n) -> p j n", j=4)[:, :, 0:P], ACT.Copy).then_inc(s("xt_ready"), 1)
                        a.wait_ge(s("h_ps"), t + (k + 1))
                        a.activation(acc[:, ds(t + k, 1), :].rearrange("p t d -> p (t d)"), bank[2 + k][0:P, 0:D], ACT.Copy).then_inc(s("h_ready"), 1)
                for c in range(NSB):
                    n = min(512, NBK * NT - 512 * c)
                    a.wait_ge(s("tot_ps"), c + 1)
                    a.activation(tot.rearrange("p b t -> p (b t)")[:, 512 * c:512 * c + n], bank[c][0:P, 0:n], ACT.Copy).then_inc(s("tot_ready"), 1)
                a.wait_ge(s("score_shifted"), 1)
                a.activation(wf[:, :, :], wf[:, :, :], ACT.Exp, bias=shf).then_inc(s("w_ready"), 1)
                for c in (0, 1):
                    a.wait_ge(s(f"entries_out{c}"), 16 * NT // 2)
                a.dma_start(perm[:, :, :], by_degree.rearrange("(t p) a -> p t a", p=P)).then_inc(s("perm_in"), 16)
                a.wait_ge(s("perm_in"), 16)
                a.activation(degs, perm[:, :, 1].bitcast(F32), ACT.Copy).then_inc(s("degs_ready"), 1)

            @block.tensor
            def _(pe):
                pe.wait_ge(s("first1f_ready"), 1)
                pe.wait_ge(s("ones_ready"), 2)
                pe.matmul(bank[7][0:P + 1, 0:NS], ones[0:1, 0:P + 1], first1f, start=True, stop=True).then_inc(s("firsts_bcast"), 1)
                pe.wait_ge(s("gw_in"), 16)
                for k in (0, 1):
                    mm = pe.matmul(bank[6][:, 0:D], ones[:, :], gwf[:, k, :], start=(k == 0), stop=(k == 1))
                mm.then_inc(s("colsum"), 1)
                pe.wait_ge(s("identh_ready"), 1)
                pe.wait_ge(s("gw_ready"), 1)

                def transpose_x(t, k, wait_bank):
                    for j in range(4):
                        mm = pe.transpose(bank[k][:, 0:256].bitcast(F16).rearrange("p (j n) -> p j n", j=4)[:, j, 0:P],
                                          xa[j // 2][:, ds(t, 1), 128 * (j % 2):128 * (j % 2) + 128].rearrange("p t d -> p (t d)"), identh[0:P, 0:P])
                    mm.then_inc(s("xt_ps"), 1)

                with steps(pe, NT, 2) as t:
                    for k in (0, 1):
                        pe.wait_ge(s("xa_ready"), t + (k + 1))
                        pe.wait_ge(s("xt_ready"), t)
                        transpose_x(t + k, k, None)
                    for k in (0, 1):
                        pe.wait_ge(s("xt_ready"), t + (k + 1))
                        pe.wait_ge(s("h_ready"), t)
                        n = 0
                        for xh, wh in ((0, 0), (0, 1), (1, 0)):
                            for dh in (0, 1):
                                mm = pe.matmul(bank[2 + k][0:P, 0:D], xt[:, ds(t + k, 1), 2 * xh + dh, 0:P].rearrange("p t n -> p (t n)"), gw[:, wh, dh, :],
                                               start=(n == 0), stop=(n == 5))
                                n += 1
                        mm.then_inc(s("h_ps"), 1)
                pe.wait_ge(s("off_ready"), 1)
                pe.wait_ge(s("ident_ready"), 1)
                pe.wait_ge(s("firsts_ready"), 1)
                pe.transpose(bank[7][0:NT, 0:P + 1], offf, ident[0:P + 1, 0:P + 1]).then_inc(s("off_t"), 1)
                pe.wait_ge(s("degT"), 1)
                pe.wait_ge(s("gwc"), 1)
                pe.transpose(bank[6][0:P, 0:NT], degT, ident[0:NT, 0:NT]).then_inc(s("deg_t"), 1)
                pe.wait_ge(s("oh_ready"), 1)
                pe.wait_ge(s("h_ready"), NT)
                ohf = oh.rearrange("p b t -> p (b t)")
                for w, done in ((onesh, "tot_ps"), (trih, "below_ps")):
                    for c in range(NSB):
                        if done == "below_ps":
                            pe.wait_ge(s("tot_ready"), c + 1)
                        n = min(512, NBK * NT - 512 * c)
                        pe.matmul(bank[c][0:P, 0:n], w, ohf[:, 512 * c:512 * c + n], start=True, stop=True).then_inc(s(done), 1)
                pe.wait_ge(s("degs_ready"), 1)
                pe.wait_ge(s("rank_ready"), 1)
                pe.transpose(bank[5][0:NT, 0:P], degs, ident[0:P, 0:P]).then_inc(s("sorted_t"), 1)
                pe.wait_ge(s("mxd"), 9)
                for k in range(4):
                    mm = pe.transpose(bank[4][0:1, k * NT:(k + 1) * NT], mxd[:, k:k + 1], ident[0:NT, 0:NT])
                mm.then_inc(s("nblk_t"), 1)


        next_part()

        with nc.Block() as block:
            @block.sync
            def _(sp):
                def start_sums(k):
                    sp.dma_start(gacc[:, k].rearrange("p a b -> p (a b)"), table[0:1, :].rearrange("o (a b) -> o a b", a=1).broadcast_to([P, BLK, ROWW])).then_inc(s(f"sum_start{k}"), 16)

                def store_sums(t, k, n):
                    sp.wait_ge(s("sum_ready"), t + 1)
                    sp.dma_start(sums[ds(t * P, P), :], gacc[:, k, 0, :]).then_inc(s(f"sum_stored{k}"), 16)
                    sp.wait_ge(s(f"sum_stored{k}"), n * 16 + 16)
                for k in (0, 1):
                    start_sums(k)
                with sp.Fori(0, NT // 2 - 1) as i:
                    for k in (0, 1):
                        store_sums(i * 2 + k, k, i)
                        start_sums(k)
                for k in (0, 1):
                    store_sums(NT - 2 + k, k, NT // 2 - 1)
                for k in (0, 1):
                    sp.wait_ge(s(f"xc2_used{k}"), NT // CH // 2)
                tv = table[1:N + 1, :].rearrange("(t p) d -> p t d", p=P)
                with sp.Fori(0, NT // CH // 2) as i:
                    for k in (0, 1):
                        sp.wait_ge(s(f"gs_used{k}"), i)
                        sp.dma_start(own[k], tv[:, ds(i * 2 * CH + k * CH, CH), :]).then_inc(s(f"own_in{k}"), 16)
                sp.wait_ge(s("acc_sum"), GH)
                for c in (0, 1):
                    w1s, w2s = ws[c]
                    sp.dma_start(w1s, w1[ds(c, 1)].rearrange("e (a p) f -> p (e a) f", p=128)).then_inc(s(f"first_w_in"), 16)
                    sp.dma_start(w2s, w2[ds(c, 1)].rearrange("e (a p) d -> p (e a) d", p=128)).then_inc(s(f"first_w_in"), 16)

            @block.gpsimd
            def _(pool):
                def index_ops(k, name, n):
                    pool.tensor_scalar(wmask[:, :], kpos[:, :], wrem[k][:, 0:1], None, ALU.is_lt).then_inc(s(name), 1)
                    hold(pool, name, n + 1)
                    pool.tensor_tensor(gidx[k][:, :], widx[k][:, :], wmask[:, :], ALU.mult).then_inc(s(name), 1)
                    hold(pool, name, n + 2)

                def fetch_window(k, name):
                    pool.indirect_dma_start(out=widx[k][:, :], out_offset=None, in_=srcpad.rearrange("(n o) -> n o", o=1),
                                            in_offset=bass.IndirectOffsetOnAxis(ap=woff[k][:, 0:1], axis=0)).then_inc(s(name), 16)

                def fetch_first(t, k):
                    pool.tensor_copy(woff[k][:, :], perm[:, ds(t, 1), 0:1].rearrange("p t a -> p (t a)")).then_inc(s("wcopies"), 1)
                    pool.tensor_copy(wrem[k][:, :], perm[:, ds(t, 1), 1:2].rearrange("p t a -> p (t a)").bitcast(F32)).then_inc(s("wcopies"), 1)
                    hold(pool, "wcopies", t * 2 + 2)
                    fetch_window(k, "widx_in")

                def gathers(k, b, n):
                    for j in range(BLK):
                        hold(pool, f"added{j}", n * 16)
                        pool.indirect_dma_start(out=gacc[:, k, j, :], out_offset=None, in_=table,
                                                in_offset=bass.IndirectOffsetOnAxis(ap=gidx[k][:, BLK * b + j:BLK * b + j + 1], axis=0),
                                                compute_op=ALU.add).then_inc(s(f"added{j}"), 16)

                def finish(k, t):
                    pool.tensor_tensor(gacc[:, k, 0:2, :], gacc[:, k, 0:2, :], gacc[:, k, 2:4, :], ALU.add).then_inc(s("halved"), 1)
                    hold(pool, "halved", t + 1)
                    pool.tensor_tensor(gacc[:, k, 0, :], gacc[:, k, 0, :], gacc[:, k, 1, :], ALU.add).then_inc(s("sum_ready"), 1)

                def tile(t, k, n, first=False, last=False):
                    nb = pool.value_load(nblk[0:1, 0, ds(t, 1)], min_val=1, max_val=WB)
                    more = pool.value_load(nblk[0:1, 1, ds(t, 1)], min_val=0, max_val=E // WIN)
                    before = pool.value_load(nblk[0:1, 2, ds(t, 1)], min_val=0, max_val=E)
                    mbefore = pool.value_load(nblk[0:1, 3, ds(t, 1)], min_val=0, max_val=E)
                    hold(pool, f"sum_start{k}", n * 16 + 16)
                    gathers(k, 0, before)
                    if not first:
                        finish(1 - k, t - 1 if isinstance(t, int) else t + -1)
                    if not last:
                        fetch_first(t + 1, 1 - k)
                    for b in range(1, WB):
                        with pool.If(nb > b):
                            gathers(k, b, before + b)
                    with pool.If(more > 0):
                        with pool.Fori(0, more) as w:
                            for j in range(BLK):
                                hold(pool, f"added{j}", (before + w * WB + WB) * 16)
                            pool.tensor_scalar(woff[k][:, :], woff[k][:, :], float(WIN), float(E), ALU.add, ALU.min).then_inc(s("more_ops"), 1)
                            pool.tensor_scalar(wrem[k][:, :], wrem[k][:, :], float(-WIN), None, ALU.add).then_inc(s("more_ops"), 1)
                            hold(pool, "more_ops", (mbefore + w) * 4 + 2)
                            fetch_window(k, "more_in")
                            hold(pool, "more_in", (mbefore + w) * 16 + 16)
                            index_ops(k, "more_ops", (mbefore + w) * 4 + 2)
                            for b in range(WB):
                                gathers(k, b, before + (w * WB + (WB + b)))
                    if not last:
                        hold(pool, "widx_in", t * 16 + 32)
                        index_ops(1 - k, "index_ops", t * 2 + 2)
                    else:
                        for j in range(BLK):
                            hold(pool, f"added{j}", (before + nb + more * WB) * 16)
                        finish(k, t)

                fetch_first(0, 0)
                hold(pool, "widx_in", 16)
                index_ops(0, "index_ops", 0)
                tile(0, 0, 0, first=True)
                with pool.Fori(0, NT // 2 - 1) as i:
                    tile(i * 2 + 1, 1, i)
                    tile(i * 2 + 2, 0, i + 1)
                tile(NT - 1, 1, NT // 2 - 1, last=True)

                for k in (0, 1):
                    pool.wait_ge(s(f"sum_stored{k}"), 16 * (NT // 2))
                    pool.wait_ge(s(f"xc2_used{k}"), NT // CH // 2)
                with pool.Fori(0, NT // CH // 2) as i:
                    for c in (0, 1):
                        hold(pool, f"gs_used{c}", i)
                        pool.tensor_copy(gslot[c], rank[:, ds(i * 2 * CH + c * CH, CH)]).then_inc(s("gslot"), 1)
                        hold(pool, "gslot", i * 2 + (c + 1))
                        for j in range(CH):
                            pool.indirect_dma_start(out=gs[c][:, j, :], out_offset=None, in_=sums,
                                                    in_offset=bass.IndirectOffsetOnAxis(ap=gslot[c][:, j:j + 1], axis=0)).then_inc(s(f"gs_in{c}"), 16)
                pool.wait_ge(s("zpart"), 1)
                pool.partition_all_reduce(zall, zpart, P, bass.bass_isa.ReduceOp.add).then_inc(s("zall"), 1)
                pool.wait_ge(s("first_w_in"), 64)
                for c in (0, 1):
                    split_weights(pool, c, "first_w", c)
                pool.wait_ge(s("logits"), NT)
                pool.memset(upper, 1.0).then_inc(s("rt"), 1)
                pool.iota(downi, pattern=[[-1, NE]], base=NE, channel_multiplier=0).then_inc(s("rt"), 1)
                pool.iota(node, pattern=[[P, NT]], base=NE * CB, channel_multiplier=1).then_inc(s("rt"), 1)
                pool.wait_ge(s("rt"), 3)
                pool.affine_select(out=upper, in_=upper, compare_op=ALU.is_ge, fill=0.0, base=0, pattern=[[1, P]], channel_multiplier=-1).then_inc(s("rt"), 1)
                pool.tensor_copy(down, downi).then_inc(s("rt"), 1)
                pool.tensor_copy(rdump, node).then_inc(s("rt"), 1)

            @block.vector
            def _(v):
                with v.Fori(0, H) as h:
                    for m in range(3):
                        v.wait_ge(s("wsum_ps"), h * 3 + (m + 1))
                        v.scalar_tensor_tensor(wraw[:, m], bank[m][:, None, 0:D].broadcast_to([128, 2, D]), -1.0 / D, wraw[:, m], ALU.mult, ALU.add).then_inc(s("wcen"), 1)
                    v.wait_ge(s("wc_out"), h * 48)
                    v.wait_ge(s("wcen"), h * 3 + 3)
                    for m in (0, 1):
                        v.tensor_scalar(wc[m][:, 0, :, 0:D], wraw[:, m], 0.25, None, ALU.mult).then_inc(s("whi"), 1)
                    v.wait_ge(s("whi"), h * 4 + 2)
                    for m in (0, 1):
                        v.scalar_tensor_tensor(wc[m][:, 1, :, 0:D], wraw[:, m], 0.25, wc[m][:, 0, :, 0:D], ALU.mult, ALU.subtract).then_inc(s("wlo"), 1)
                    for m in (0, 1):
                        v.wait_ge(s("prod_ps"), h * 3 + (m + 1))
                        v.tensor_scalar(wc[m][:, 0, :, D:2 * D], bank[4 + m][:, :].rearrange("p (a b) -> p a b", a=2), 0.25, None, ALU.mult).then_inc(s("whi"), 1)
                    v.wait_ge(s("whi"), h * 4 + 4)
                    v.wait_ge(s("wlo"), h * 2 + 2)
                    for m in (0, 1):
                        v.scalar_tensor_tensor(wc[m][:, 1, :, D:2 * D], bank[4 + m][:, :].rearrange("p (a b) -> p a b", a=2), 0.25, wc[m][:, 0, :, D:2 * D], ALU.mult, ALU.subtract).then_inc(s("prod_used"), 1)
                    v.wait_ge(s("prod_ps"), h * 3 + 3)
                    v.tensor_copy(bmat, bank[6][:, :].rearrange("p (a b) -> p a b", a=2)).then_inc(s("prod_used"), 1)
                v.memset(zero, 0.0).then_inc(s("zero_ready"), 1)
                v.wait_ge(s("bo_in"), 16)
                v.tensor_copy(acc[:, :, :], brow_bo[:, None, :].broadcast_to([P, NT, D])).then_inc(s("acc_ready"), 1)
                v.wait_ge(s("acc_ready"), 1)
                with v.Fori(0, H) as h:
                    def negate(ph_):
                        def step(k, i, t):
                            v.wait_ge(s(f"{ph_}_sq"), h * NT + (t + 1))
                            v.tensor_scalar(nsq[k], sq[k], -1.0, LOG16, ALU.mult, ALU.subtract).then_inc(s(f"{ph_}_nsq"), 1)
                        return step

                    def k_hi(k, i, t):
                        v.wait_ge(s("k_exp"), h * NT + (t + 1))
                        v.wait_ge(s("k_kv"), h * NT + less(t, 3))
                        v.tensor_scalar(ph[k][:, 0, :], ex[k], PHI_EPS, None, ALU.add).then_inc(s("k_hi"), 1)

                    def k_lo(k, i, t):
                        v.wait_ge(s("k_hi"), h * NT + (t + 1))
                        v.scalar_tensor_tensor(ph[k][:, 1, :], ex[k], PHI_EPS, ph[k][:, 0, :], ALU.add, ALU.subtract).then_inc(s("k_ph"), 1)

                    pipeline(v, [(2, k_hi), (0, negate("k")), (2, k_lo)], NT, 4)
                    v.wait_ge(s("kvo_ps"), h + 1)
                    v.wait_ge(s("q_att"), h * NT)
                    kvp = bank[5][:, :].rearrange("p (a b) -> p a b", a=2)
                    v.tensor_copy(kvo[:, 0, :, 0:D], kvp).then_inc(s("kvo_hi"), 1)
                    v.tensor_copy(kvo[:, 0, :, D:D + 1], kvs[:, :, D:D + 1]).then_inc(s("kvo_hi"), 1)
                    v.wait_ge(s("kvo_hi"), h * 2 + 2)
                    v.tensor_tensor(kvo[:, 1, :, 0:D], kvp, kvo[:, 0, :, 0:D], ALU.subtract).then_inc(s("kvo_lo"), 1)
                    v.wait_ge(s("kvo_lo"), h + 1)
                    v.tensor_tensor(kvo[:, 1, :, D:D + 1], kvs[:, :, D:D + 1], kvo[:, 0, :, D:D + 1], ALU.subtract).then_inc(s("kvo_ready"), 1)

                    def turned(k):
                        return bank[4 + k % 2][:, 0:256].rearrange("p (a b) -> p a b", a=2)[:, :, 0:P]

                    def q_hi(k, i, t):
                        v.wait_ge(s("q_turned"), h * NT + (t + 1))
                        v.wait_ge(s("q_att"), h * NT + less(t, 3))
                        v.tensor_scalar(qt[k][:, 0, :, 0:P], turned(k), PHI_EPS, None, ALU.add).then_inc(s("q_hi"), 1)

                    def q_lo(k, i, t):
                        v.wait_ge(s("q_hi"), h * NT + (t + 1))
                        v.scalar_tensor_tensor(qt[k][:, 1, :, 0:P], turned(k), PHI_EPS, qt[k][:, 0, :, 0:P], ALU.add, ALU.subtract).then_inc(s("q_ph"), 1)

                    def over_z(k, i, t):
                        v.wait_ge(s("q_att"), h * NT + (t + 1))
                        v.wait_ge(s("q_acc"), h * NT + less(t, 3))
                        v.reciprocal(rz[k], bank[6 + k % 2][0:P, D:D + 1]).then_inc(s("q_rz"), 1)

                    def add_head(k, i, t):
                        v.wait_ge(s("q_rz"), h * NT + (t + 1))
                        at = acc[:, ds(t, 1), :].rearrange("p t d -> p (t d)")
                        v.scalar_tensor_tensor(at, bank[6 + k % 2][0:P, 0:D], rz[k], at, ALU.mult, ALU.add).then_inc(s("q_acc"), 1)

                    pipeline(v, [(3, q_hi), (0, negate("q")), (5, over_z), (3, q_lo), (5, add_head)], NT, 4)
                    v.wait_ge(s("q_acc"), (h + 1) * NT)


                def per_row(col, t, n=CH):
                    return col[:, ds(t, n)].rearrange("p (t o) -> p t o", o=1).broadcast_to([P, n, D])

                def norm_stats(n, eps_):
                    me, ve, mo, vo = tst[:, :, 1], tst[:, :, 2], tst[:, :, 4], tst[:, :, 5]
                    q, dm, vs, ve_, va, r0, r2, r3 = tln
                    ln = s("ln")
                    b = 10 * n
                    v.tensor_tensor(q, me, mo, ALU.add).then_inc(ln, 1)
                    v.tensor_tensor(dm, me, mo, ALU.subtract).then_inc(ln, 1)
                    v.tensor_tensor(vs, ve, vo, ALU.add).then_inc(ln, 1)
                    v.wait_ge(ln, b + 3)
                    v.tensor_scalar(mean[:, :], q, 0.5, None, ALU.mult).then_inc(ln, 1)
                    v.scalar_tensor_tensor(r0, dm, 0.25, dm, ALU.mult, ALU.mult).then_inc(ln, 1)
                    v.wait_ge(ln, b + 5)
                    v.scalar_tensor_tensor(va, vs, 1.0 / D, r0, ALU.mult, ALU.add).then_inc(ln, 1)
                    v.wait_ge(ln, b + 6)
                    v.tensor_scalar(ve_, va, eps_, None, ALU.add).then_inc(s("var_ready"), 1)
                    v.wait_ge(s("sqrt_ready"), n + 1)
                    v.reciprocal(r2, r3).then_inc(ln, 1)
                    v.wait_ge(ln, b + 7)
                    v.tensor_tensor(q, r2, r2, ALU.mult).then_inc(ln, 1)
                    v.wait_ge(ln, b + 8)
                    v.scalar_tensor_tensor(dm, q, -0.5, ve_, ALU.mult, ALU.mult).then_inc(ln, 1)
                    v.wait_ge(ln, b + 9)
                    v.scalar_tensor_tensor(rstd[:, :], dm, 1.5, r2, ALU.add, ALU.mult).then_inc(ln, 1)
                    v.wait_ge(ln, b + 10)

                def stats_of(tile, done):
                    v.bn_stats(tst[:, ds(tile, 1), :].rearrange("p t a -> p (t a)"), acc[:, ds(tile, 1), :].rearrange("p t d -> p (t d)")).then_inc(s(done), 1)

                with v.Fori(0, NT // CH // 2) as i:
                    for k in (0, 1):
                        t, n = i * 2 * CH + k * CH, i * 6 + k * 3
                        v.wait_ge(s(f"xc_in{k}"), i * 16 + 16)
                        v.tensor_tensor(xc[k], xc[k], per_row(mean, t), ALU.subtract).then_inc(s("resid"), 1)
                        v.wait_ge(s("resid"), n + 1)
                        v.tensor_tensor(xc[k], xc[k], per_row(rstd, t), ALU.mult).then_inc(s("resid"), 1)
                        v.wait_ge(s("resid"), n + 2)
                        at = acc[:, ds(t, CH), :]
                        v.tensor_tensor(at, at, xc[k], ALU.add).then_inc(s("resid"), 1)
                        v.wait_ge(s("resid"), n + 3)
                        for j in range(CH):
                            stats_of(t + j, f"xc_used{k}")
                for k in (0, 1):
                    v.wait_ge(s(f"xc_used{k}"), NT // 2)
                norm_stats(0, MIX_EPS)
                v.wait_ge(s("tail_in"), 16 * 11)

                def out1(k, i, g):
                    t = g * 2
                    for j in (0, 1):
                        at = acc[:, ds(t + j, 1), :]
                        v.tensor_scalar(at, at, mean[:, ds(t + j, 1)], rstd[:, ds(t + j, 1)], ALU.subtract, ALU.mult).then_inc(s("out1_norm"), 1)
                    at = acc[:, ds(t, 2), :]
                    v.wait_ge(s("out1_norm"), t + 2)
                    v.tensor_tensor(at, at, g1b[:, None, :].broadcast_to([P, 2, D]), ALU.mult).then_inc(s("out1_g"), 1)
                    v.wait_ge(s("out1_g"), g * 2 + 1)
                    v.tensor_tensor(at, at, beta1b[:, None, :].broadcast_to([P, 2, D]), ALU.add).then_inc(s("out1_g"), 1)
                    v.wait_ge(s("out1_g"), g * 2 + 2)
                    hold(v, "out1_turned", less(g, 1), "dve")
                    v.tensor_copy(o1[k], at).then_inc(s("out1_ready"), 1)

                def add_ffn(k, i, g):
                    v.wait_ge(s("ffn_ps"), g + 1)
                    at = acc[:, ds(g * 2, 2), :]
                    v.tensor_tensor(at, at, bank[4 + k][0:P, :].rearrange("p (a b) -> p a b", a=2), ALU.add).then_inc(s("ffn_added"), 1)
                    v.wait_ge(s("ffn_added"), g + 1)
                    v.tensor_tensor(at, at, bias2b[:, None, :].broadcast_to([P, 2, D]), ALU.add).then_inc(s("ffn_bias"), 1)

                def stats2(k, i, g):
                    v.wait_ge(s("ffn_bias"), g + 1)
                    for j in (0, 1):
                        stats_of(g * 2 + j, "stats2")
                pipeline(v, [(0, out1), (3, add_ffn), (4, stats2)], NT // 2)
                v.wait_ge(s("stats2"), NT)
                norm_stats(1, MIX_EPS)
                v.tensor_tensor(beta2b, beta2b, gnnb, ALU.add).then_inc(s("beta2_gnn"), 1)
                v.wait_ge(s("beta2_gnn"), 1)
                with v.Fori(0, NT // CH // 2) as i:
                    for k in (0, 1):
                        t, c = i * 2 * CH + k * CH, i * 2 + k
                        for j in range(CH):
                            at = acc[:, ds(t + j, 1), :]
                            v.tensor_scalar(at, at, mean[:, ds(t + j, 1)], rstd[:, ds(t + j, 1)], ALU.subtract, ALU.mult).then_inc(s("mix_norm"), 1)
                        at = acc[:, ds(t, CH), :]
                        v.wait_ge(s("mix_norm"), t + CH)
                        v.tensor_tensor(at, at, g2b[:, None, :].broadcast_to([P, CH, D]), ALU.mult).then_inc(s("mix_g"), 1)
                        v.wait_ge(s(f"xc2_in{k}"), i * 16 + 16)
                        v.tensor_tensor(xc[k], xc[k], beta2b[:, None, :].broadcast_to([P, CH, D]), ALU.add).then_inc(s("mix_g"), 1)
                        v.wait_ge(s("mix_g"), c * 2 + 2)
                        v.tensor_tensor(at, at, xc[k], ALU.add).then_inc(s(f"xc2_used{k}"), 1)
                for k in (0, 1):
                    v.wait_ge(s(f"xc2_used{k}"), NT // CH // 2)
                f4 = wf[:, :, GH:2 * GH]
                with v.Fori(0, NT // CH // 2) as i:
                    for k in (0, 1):
                        t, n = i * 2 * CH + k * CH, i * 4 + k * 2
                        v.wait_ge(s(f"own_in{k}"), i * 16 + 16)
                        v.wait_ge(s(f"gs_in{k}"), i * 16 * CH + 16 * CH)
                        v.tensor_tensor(gs[k], gs[k], own[k], ALU.add).then_inc(s("own_added"), 1)
                        v.wait_ge(s("own_added"), i * 2 + (k + 1))
                        v.tensor_tensor(zw[:, ds(t, CH), :], gs[k][:, :, D:ROWW], f4[:, ds(t, CH), :], ALU.mult).then_inc(s("scaled"), 1)
                        v.tensor_tensor(scaled[:, ds(t, CH), :].rearrange("p t (h d) -> p t h d", d=GD), gs[k][:, :, 0:D].rearrange("p t (h d) -> p t h d", d=GD),
                                        f4[:, ds(t, CH), :, None].broadcast_to([P, CH, GH, GD]), ALU.mult).then_inc(s("scaled"), 1)
                        v.wait_ge(s("scaled"), n + 2)
                        v.sem_inc(s(f"gs_used{k}"), 1)
                v.tensor_reduce(zpart, zw.rearrange("p t h -> p h t"), AX.X, ALU.add).then_inc(s("zpart"), 1)
                v.wait_ge(s("zpart"), 1)
                v.wait_ge(s("zall"), 1)
                v.reciprocal(zpart, zall).then_inc(s("z"), 1)
                v.wait_ge(s("z"), 1)
                for h in range(GH):
                    v.scalar_tensor_tensor(acc[:, :, GD * h:GD * h + GD], scaled[:, :, GD * h:GD * h + GD], zpart[:, h:h + 1], acc[:, :, GD * h:GD * h + GD], ALU.mult, ALU.add).then_inc(s("acc_sum"), 1)
                v.wait_ge(s("acc_sum"), GH)
                with v.Fori(0, NT) as t:
                    stats_of(t, "acc_new")
                v.wait_ge(s("acc_new"), NT)
                norm_stats(2, LN_EPS)

                def gate_norm(k, i, t):
                    v.wait_ge(s("xf_turned"), less(t, 3))
                    v.tensor_scalar(xfs[k], acc[:, ds(t, 1), :].rearrange("p t d -> p (t d)"), mean[:, ds(t, 1)], rstd[:, ds(t, 1)], ALU.subtract, ALU.mult).then_inc(s("xf_ready"), 1)

                def logits(k, i, t):
                    v.wait_ge(s("lg_ps"), t + 1)
                    v.tensor_tensor(lg[:, ds(t, 1), :].rearrange("p t e -> p (t e)"), bank[4 + k][0:P, 0:NE], gateb, ALU.add).then_inc(s("logits"), 1)
                pipeline(v, [(0, gate_norm), (4, logits)], NT, 4)
                v.wait_ge(s("logits"), NT)
                v.wait_ge(s("rt"), 6)

                def over_experts(col):
                    return col[:, :, None].broadcast_to([P, NT, NE])
                v.tensor_reduce(rmax, lg, AX.X, ALU.max).then_inc(s("route"), 1)
                v.wait_ge(s("route"), 1)
                v.tensor_tensor(lg, lg, over_experts(rmax), ALU.subtract).then_inc(s("route"), 1)
                v.wait_ge(s("rexp"), 1)
                v.tensor_reduce(rsum, rex, AX.X, ALU.add).then_inc(s("route"), 1)
                v.tensor_reduce(rmax, rex, AX.X, ALU.max).then_inc(s("route"), 1)
                v.wait_ge(s("route"), 4)
                v.reciprocal(rinv, rsum).then_inc(s("route"), 1)
                v.tensor_tensor(rex, rex, over_experts(rmax), ALU.is_equal).then_inc(s("route"), 1)
                v.wait_ge(s("route"), 6)
                v.tensor_tensor(rex, rex, down[:, None, :].broadcast_to([P, NT, NE]), ALU.mult).then_inc(s("route"), 1)
                v.tensor_tensor(rinv, rinv, rmax, ALU.mult).then_inc(s("route"), 1)
                v.wait_ge(s("route"), 8)
                v.tensor_reduce(ridx, rex, AX.X, ALU.max).then_inc(s("route"), 1)
                v.wait_ge(s("route"), 9)
                v.tensor_tensor(roh, rex, over_experts(ridx), ALU.is_equal).then_inc(s("onehot_ready"), 1)
                v.wait_ge(s("counts_ps"), 1)
                v.tensor_copy(rtot, bank[1][0:P, 0:NT * NE].rearrange("p (t e) -> p t e", e=NE)).then_inc(s("route"), 1)
                v.wait_ge(s("route"), 10)
                for e in range(NE):
                    v.tensor_tensor_scan(rscan[:, :, e], rtot[:, :, e], rtot[:, :, e], 0.0, ALU.add, ALU.bypass).then_inc(s("route"), 1)
                v.wait_ge(s("route"), 18)
                v.tensor_tensor(rscan, rscan, rtot, ALU.subtract).then_inc(s("route"), 1)
                v.wait_ge(s("route"), 19)
                v.tensor_tensor(rscan, rscan, bank[0][0:P, 0:NT * NE].rearrange("p (t e) -> p t e", e=NE), ALU.add).then_inc(s("route"), 1)
                v.wait_ge(s("route"), 20)
                v.tensor_tensor(rscan, rscan, roh, ALU.mult).then_inc(s("route"), 1)
                v.wait_ge(s("route"), 21)
                v.tensor_reduce(rpos, rscan, AX.X, ALU.add).then_inc(s("route"), 1)
                v.wait_ge(s("route"), 22)
                v.tensor_scalar(rkept, rpos, float(CAP) + 0.5, None, ALU.is_lt).then_inc(s("route"), 1)
                v.tensor_scalar(rpos, rpos, float(CAP), -1.0, ALU.min, ALU.add).then_inc(s("route"), 1)
                v.tensor_scalar(rtmp, ridx, -float(CB), float(NE * CB), ALU.mult, ALU.add).then_inc(s("route"), 1)
                v.wait_ge(s("route"), 25)
                v.tensor_tensor(rtmp, rtmp, rpos, ALU.add).then_inc(s("route"), 1)
                v.tensor_tensor(pk, rinv, rkept, ALU.mult).then_inc(s("route"), 1)
                v.wait_ge(s("route"), 27)
                v.tensor_copy(slot_in, rtmp).then_inc(s("route"), 1)
                v.tensor_tensor(rtmp, rtmp, rdump, ALU.subtract).then_inc(s("route"), 1)
                v.wait_ge(s("route"), 29)
                v.tensor_tensor(rtmp, rtmp, rkept, ALU.mult).then_inc(s("route"), 1)
                v.wait_ge(s("route"), 30)
                v.tensor_tensor(slot_out, rtmp, rdump, ALU.add).then_inc(s("slots_ready"), 1)

            @block.scalar
            def _(a):
                a.activation(spare[:, 0:1], ident[0:P, 0:1], ACT.Exp)
                a.dma_start(brow_bo, bo.rearrange("(o d) -> o d", o=1).broadcast_to([P, D])).then_inc(s("bo_in"), 16)
                a.dma_start(projr, proj.rearrange("(a p) n -> p a n", p=128)).then_inc(s("proj_in"), 16)
                a.wait_ge(s("projt_ps"), 1)
                a.activation(projt, bank[0][:, :].rearrange("p (a b) -> p a b", a=2), ACT.Copy).then_inc(s("projt_ready"), 1)
                with a.Fori(0, H) as h:
                    a.wait_ge(s("prod_ps"), h * 3)
                    for m, w in enumerate((Wq, Wk, Wv)):
                        a.dma_start(wraw[:, m], w[:, ds(h, 1), :].rearrange("(a p) h k -> p a (h k)", p=128)).then_inc(s("w_in"), 16)
                    a.dma_start(wo, Wo[ds(h, 1)].rearrange("h (a p) d -> p (h a) d", p=128)).then_inc(s("w_in"), 16)
                    for m, b in enumerate((bq, bk, bv)):
                        a.dma_start(brow[0:1, m, :], b[ds(h, 1), :]).then_inc(s("w_in"), 16)
                    for m in range(3):
                        a.wait_ge(s("wt_ps"), h * 3 + (m + 1))
                        a.activation(wt[:, m], bank[3][:, :].rearrange("p (a b) -> p a b", a=2), ACT.Copy).then_inc(s("wt_ready"), 1)
                    a.wait_ge(s("prod_used"), h * 3 + 3)
                    for m in (0, 1):
                        a.dma_start(wcat[ds(h, 1), m].rearrange("h p n -> p (h n)"), wc[m].rearrange("p a b c -> p (a b c)")).then_inc(s("wc_out"), 16)
                    a.dma_start(bdram[ds(h, 1)].rearrange("h p n -> p (h n)"), bmat.rearrange("p a b -> p (a b)")).then_inc(s("wc_out"), 16)
                a.wait_ge(s("wc_out"), H * 48)
                def load_head(m, h, name):
                    a.dma_start(wc[m].rearrange("p a b c -> p (a b c)"), wcat[ds(h, 1), m].rearrange("h p n -> p (h n)")).then_inc(s(name), 16)
                with a.Fori(0, H) as h:
                    a.wait_ge(s("k_u"), h * NT)
                    load_head(1, h, "wk_in")
                    a.wait_ge(s("kvo_ps"), h)
                    a.dma_start(bmat.rearrange("p a b -> p (a b)"), bdram[ds(h, 1)].rearrange("h p n -> p (h n)")).then_inc(s("bmat_in"), 16)
                    a.wait_ge(s("q_u"), h * NT)
                    load_head(0, h, "wq_in")

                    def square(ph_):
                        def step(k, i, t):
                            a.wait_ge(s(f"{ph_}_u"), h * NT + (t + 1))
                            a.wait_ge(s(f"{ph_}_exp"), h * NT + less(t, 3))
                            a.activation(sqj[k], fbank[ph_][k][0:P, 0:D], ACT.Square, scale=0.5 ** 0.5, accum_out=sq[k]).then_inc(s(f"{ph_}_sq"), 1)
                        return step

                    def expo(ph_, used):
                        def step(k, i, t):
                            a.wait_ge(s(f"{ph_}_nsq"), h * NT + (t + 1))
                            a.wait_ge(s(used), h * NT + less(t, 3))
                            a.activation(ex[k], fbank[ph_][k][0:P, D:2 * D], ACT.Exp, bias=nsq[k]).then_inc(s(f"{ph_}_exp"), 1)
                        return step

                    a.wait_ge(s("q_turned"), h * NT)
                    pipeline(a, [(0, square("k")), (1, expo("k", "k_ph"))], NT, 4)
                    a.wait_ge(s("k_kv"), (h + 1) * NT)
                    for m in (0, 1):
                        ins = a.activation(kvs[:, m, 0:D + 1], bank[2 + m][:, 0:D + 1], ACT.Copy)
                    ins.then_inc(s("kvs_ready"), 1)
                    a.wait_ge(s("kvt_ps"), h + 1)
                    a.activation(kvt, bank[4][:, :].rearrange("p (a b) -> p a b", a=2), ACT.Copy).then_inc(s("kvt_ready"), 1)
                    a.wait_ge(s("k_ph"), (h + 1) * NT)
                    pipeline(a, [(0, square("q")), (1, expo("q", "q_turned"))], NT, 4)


                a.wait_ge(s("q_acc"), H * NT)
                for to, fro in ((g1b, g1), (beta1b, beta1), (g2b, g2), (beta2b, beta2), (bias2b, bias2), (gnnb, gb), (gateb, gate_b)):
                    a.dma_start(to, fro.rearrange("(o d) -> o d", o=1).broadcast_to([P, to.shape[-1]])).then_inc(s("tail_in"), 16)
                for to, fro in ((W1s, W1), (W2s, W2), (gate, gate_w)):
                    a.dma_start(to, fro.rearrange("(a p) n -> p a n", p=128)).then_inc(s("tail_in"), 16)
                a.dma_start(b1r, bias1.rearrange("(a p) -> a p", p=128)).then_inc(s("tail_in"), 16)

                def load_x(again):
                    with a.Fori(0, NT // CH // 2) as i:
                        for k in (0, 1):
                            a.wait_ge(s(f"xc{again}_used{k}"), i * (1 if again else CH))
                            a.dma_start(xc[k], xv[:, ds(i * 2 * CH + k * CH, CH), :]).then_inc(s(f"xc{again}_in{k}"), 16)
                load_x("")

                def root(n):
                    a.wait_ge(s("var_ready"), n + 1)
                    a.activation(tln[7], tln[3], ACT.Sqrt).then_inc(s("sqrt_ready"), 1)
                root(0)
                a.wait_ge(s("bias1_ps"), 1)
                a.activation(bias1t, bank[6][:, 0:2], ACT.Copy).then_inc(s("bias1_ready"), 1)
                a.activation(spare[:, 1:2], ident[0:P, 0:1], ACT.Relu)

                def out1_t(k, i, g):
                    a.wait_ge(s("out1_turned"), g + 1)
                    a.wait_ge(s("hidden_ps"), less(g, 1))
                    a.activation(ot[k], bank[k][:, 0:4 * P].rearrange("p (a b) -> p a b", a=2), ACT.Copy).then_inc(s("ot_ready"), 1)

                def relu(k, i, g):
                    a.wait_ge(s("bias1_ready"), 1)
                    a.wait_ge(s("hidden_ps"), g + 1)
                    a.wait_ge(s("ffn_ps"), less(g, 1))
                    for fh in (0, 1):
                        a.activation(ht[k][:, fh, :], bank[2 + k][:, fh * 2 * P:fh * 2 * P + 2 * P], ACT.Relu, bias=bias1t[:, fh:fh + 1]).then_inc(s("ht_ready"), 1)
                pipeline(a, [(0, out1_t), (1, relu)], NT // 2)
                root(1)
                for k in (0, 1):
                    a.wait_ge(s(f"xc_used{k}"), NT // 2)
                load_x("2")
                root(2)

                def xf_t(k, i, t):
                    a.wait_ge(s("xf_turned"), t + 1)
                    a.wait_ge(s("lg_ps"), less(t, 3))
                    a.activation(xft[k], bank[k][:, 0:2 * P].rearrange("p (a b) -> p a b", a=2), ACT.Copy).then_inc(s("xft_ready"), 1)
                pipeline(a, [(0, xf_t)], NT, 4)
                a.wait_ge(s("route"), 2)
                a.activation(rex, lg, ACT.Exp).then_inc(s("rexp"), 1)

            @block.tensor
            def _(pe):
                for m in (0, 1):
                    pe.wait_ge(s("proj_in"), 16)
                    for kh in (0, 1):
                        mm = pe.transpose(bank[0][:, kh * M + m * 128:kh * M + m * 128 + 128], projr[:, m, kh * 128:kh * 128 + 128], ident[:, :])
                mm.then_inc(s("projt_ps"), 1)
                pe.wait_ge(s("projt_ready"), 1)
                with pe.Fori(0, H) as h:
                    pe.wait_ge(s("w_in"), h * 112 + 112)
                    for m in range(3):
                        pe.wait_ge(s("wcen"), h * 3)
                        for dh in (0, 1):
                            pe.matmul(bank[m][:, 0:D], ones[:, :], wraw[:, m, dh, :], start=(dh == 0), stop=False)
                        pe.matmul(bank[m][:, 0:D], nones[0:1, :], brow[0:1, m, :], start=False, stop=True).then_inc(s("wsum_ps"), 1)
                    for m in range(3):
                        pe.wait_ge(s("wcen"), h * 3 + (m + 1))
                        pe.wait_ge(s("wt_ready"), h * 3 + m)
                        for kh in (0, 1):
                            for dh in (0, 1):
                                mm = pe.transpose(bank[3][:, kh * D + dh * 128:kh * D + dh * 128 + 128], wraw[:, m, dh, kh * 128:kh * 128 + 128], ident[:, :])
                        mm.then_inc(s("wt_ps"), 1)
                    for m in range(3):
                        pe.wait_ge(s("wt_ready"), h * 3 + (m + 1))
                        pe.wait_ge(s("prod_used"), h * 3)
                        rhs = projt if m < 2 else wo
                        for dh in (0, 1):
                            for kh in (0, 1):
                                mm = pe.matmul(bank[4 + m][:, dh * D:dh * D + D], wt[:, m, kh, dh * 128:dh * 128 + 128], rhs[:, kh, :], start=(kh == 0), stop=(kh == 1))
                        mm.then_inc(s("prod_ps"), 1)
                pe.wait_ge(s("prod_used"), H * 3)
                with pe.Fori(0, H) as h:
                    def features(w, ph_):
                        def step(k, i, t):
                            pe.wait_ge(s(f"{ph_}_exp"), h * NT + less(t, 3))
                            if ph_ == "k" and isinstance(t, int) and t == 2:
                                pe.wait_ge(s("q_acc"), h * NT)
                            n = 0
                            for xh, wh in ((0, 0), (0, 1), (1, 0)):
                                for dh in (0, 1):
                                    mm = pe.matmul(fbank[ph_][k][0:P, :], xt[:, ds(t, 1), 2 * xh + dh, 0:P].rearrange("p t n -> p (t n)"), w[:, wh, dh, :], start=(n == 0), stop=(n == 5))
                                    n += 1
                            mm.then_inc(s(f"{ph_}_u"), 1)
                        return step

                    def kv(k, i, t):
                        pe.wait_ge(s("k_ph"), h * NT + (t + 1))
                        for m in (0, 1):
                            for a, b in ((0, 0), (0, 1), (1, 0)):
                                mm = pe.matmul(bank[2 + m][:, 0:D + 1], ph[k][:, a, m * 128:m * 128 + 128], xa[b][:, ds(t, 1), 0:D + 1].rearrange("p t n -> p (t n)"),
                                               start=False, stop=False, skip_group_check=True)
                        mm.then_inc(s("k_kv"), 1)

                    pe.wait_ge(s("wk_in"), h * 16 + 16)
                    pe.wait_ge(s("zero_ready"), 1)
                    pe.wait_ge(s("kvs_ready"), h)
                    pe.wait_ge(s("q_exp"), h * NT)
                    for m in (0, 1):
                        pe.matmul(bank[2 + m][:, 0:D + 1], zero, xa[0][:, 0, 0:D + 1], start=True, stop=False, skip_group_check=True)
                    pipeline(pe, [(0, features(wc[1], "k")), (3, kv)], NT, 4)
                    pe.wait_ge(s("q_ph"), h * NT)
                    pe.wait_ge(s("kvs_ready"), h + 1)
                    for dh in (0, 1):
                        for m in (0, 1):
                            mm = pe.transpose(bank[4][:, dh * M + m * 128:dh * M + m * 128 + 128], kvs[:, m, dh * 128:dh * 128 + 128], ident[:, :])
                    mm.then_inc(s("kvt_ps"), 1)
                    pe.wait_ge(s("kvt_ready"), h + 1)
                    pe.wait_ge(s("bmat_in"), h * 16 + 16)
                    for m in (0, 1):
                        for dh in (0, 1):
                            mm = pe.matmul(bank[5][:, m * D:m * D + D], kvt[:, dh, m * 128:m * 128 + 128], bmat[:, dh, :], start=(dh == 0), stop=(dh == 1))
                    mm.then_inc(s("kvo_ps"), 1)
                    pe.wait_ge(s("wq_in"), h * 16 + 16)
                    pe.wait_ge(s("k_exp"), (h + 1) * NT)
                    pe.wait_ge(s("kvo_ready"), h + 1)

                    def turn(k, i, t):
                        pe.wait_ge(s("q_exp"), h * NT + (t + 1))
                        pe.wait_ge(s("q_ph"), h * NT + less(t, 1))
                        for m in (0, 1):
                            mm = pe.transpose(bank[4 + k % 2][:, m * 128:m * 128 + P], ex[k][:, m * 128:m * 128 + 128], ident[0:P, 0:P])
                        mm.then_inc(s("q_turned"), 1)

                    def attend(k, i, t):
                        pe.wait_ge(s("q_ph"), h * NT + (t + 1))
                        pe.wait_ge(s("q_acc"), h * NT + less(t, 1))
                        n = 0
                        for a, b in ((0, 0), (0, 1), (1, 0)):
                            for m in (0, 1):
                                mm = pe.matmul(bank[6 + k % 2][0:P, 0:D + 1], qt[k][:, a, m, 0:P], kvo[:, b, m, 0:D + 1], start=(n == 0), stop=(n == 5))
                                n += 1
                        mm.then_inc(s("q_att"), 1)

                    pipeline(pe, [(0, features(wc[0], "q")), (2, turn), (4, attend)], NT, 4)

                pe.wait_ge(s("tail_in"), 16 * 11)
                pe.wait_ge(s("q_acc"), H * NT)
                pe.transpose(bank[6][:, 0:2], b1r, ident[0:2, 0:2]).then_inc(s("bias1_ps"), 1)

                def turn_out1(k, i, g):
                    pe.wait_ge(s("out1_ready"), g + 1)
                    pe.wait_ge(s("ot_ready"), less(g, 1))
                    for dh in (0, 1):
                        for j in (0, 1):
                            mm = pe.transpose(bank[k][:, dh * 2 * P + j * P:dh * 2 * P + j * P + P],
                                              o1[k][:, j, dh * 128:dh * 128 + 128], ident[0:P, 0:P])
                    mm.then_inc(s("out1_turned"), 1)

                def ffn1(k, i, g):
                    pe.wait_ge(s("ot_ready"), g + 1)
                    pe.wait_ge(s("ht_ready"), less(g, 1) * 2)
                    for fh in (0, 1):
                        for dh in (0, 1):
                            mm = pe.matmul(bank[2 + k][:, fh * 2 * P:fh * 2 * P + 2 * P], W1s[:, dh, fh * 128:fh * 128 + 128], ot[k][:, dh, :], start=(dh == 0), stop=(dh == 1))
                    mm.then_inc(s("hidden_ps"), 1)

                def ffn2(k, i, g):
                    pe.wait_ge(s("ht_ready"), g * 2 + 2)
                    pe.wait_ge(s("ffn_added"), g)
                    for j in (0, 1):
                        for fh in (0, 1):
                            mm = pe.matmul(bank[4 + k][0:P, j * D:j * D + D], ht[k][:, fh, j * P:j * P + P], W2s[:, fh, :], start=(fh == 0), stop=(fh == 1))
                    mm.then_inc(s("ffn_ps"), 1)
                pipeline(pe, [(0, turn_out1), (1, ffn1), (2, ffn2)], NT // 2)

                def turn_xf(k, i, t):
                    pe.wait_ge(s("xf_ready"), t + 1)
                    pe.wait_ge(s("xft_ready"), less(t, 3))
                    for dh in (0, 1):
                        mm = pe.transpose(bank[k][:, dh * P:dh * P + P], xfs[k][:, dh * 128:dh * 128 + 128], ident[0:P, 0:P])
                    mm.then_inc(s("xf_turned"), 1)

                def gate_logits(k, i, t):
                    pe.wait_ge(s("xft_ready"), t + 1)
                    pe.wait_ge(s("logits"), less(t, 3))
                    for dh in (0, 1):
                        mm = pe.matmul(bank[4 + k][0:P, 0:NE], xft[k][:, dh, :], gate[:, dh, :], start=(dh == 0), stop=(dh == 1))
                    mm.then_inc(s("lg_ps"), 1)
                pipeline(pe, [(0, turn_xf), (2, gate_logits)], NT, 4)
                pe.wait_ge(s("onehot_ready"), 1)
                one_hot = roh.rearrange("p t e -> p (t e)")
                pe.matmul(bank[0][0:P, 0:NT * NE], upper, one_hot, start=True, stop=True)
                pe.matmul(bank[1][0:P, 0:NT * NE], ones[0:P, 0:P], one_hot, start=True, stop=True).then_inc(s("counts_ps"), 1)


        next_part()

        with nc.Block() as block:
            @block.sync
            def _(sp):
                for k in range(CH):
                    sp.wait_ge(s(f"scattered{k}"), 16 * (NT // CH))

                def load_rows(k, i, t):
                    e, half = (i * 2 + k // 2), k % 2
                    if half == 0:
                        if not isinstance(t, int) or t >= 4:
                            sp.wait_ge(s("w_split"), less(t, 6))
                            w1s, w2s = ws[k // 2]
                            sp.dma_start(w1s, w1[ds(e, 1)].rearrange("e (a p) f -> p (e a) f", p=128)).then_inc(s(f"we_in{k // 2}"), 16)
                            sp.dma_start(w2s, w2[ds(e, 1)].rearrange("e (a p) d -> p (e a) d", p=128)).then_inc(s(f"we_in{k // 2}"), 16)
                        sp.wait_ge(s("ye_ready"), less(t, 2) * 2)
                        sp.dma_start(b2b[k // 2], b2[ds(e, 1), :].broadcast_to([P, D])).then_inc(s(f"b2_in{k // 2}"), 16)
                    sp.wait_ge(s("xe_turned"), less(t, 1))
                    sp.dma_start(xe[k % 2], ebuf[0:NE * CB].rearrange("(u j p) d -> u p j d", p=P, j=4)[ds(t, 1)].rearrange("u p j d -> p (u j) d")).then_inc(s(f"xe_in{k % 2}"), 16)

                def store_rows(k, i, t):
                    sp.wait_ge(s("flagged"), t + 1)
                    sp.dma_start(ybuf.rearrange("(u j p) d -> u p j d", p=P, j=4)[ds(t, 1)].rearrange("u p j d -> p (u j) d"), ye).then_inc(s("ye_out"), 16)
                pipeline(sp, [(0, load_rows), (3, store_rows)], 2 * NE, 4)
                ov = out.rearrange("(t p) d -> p t d", p=P)
                with sp.Fori(0, NT // CH) as i:
                    sp.wait_ge(s("out_ready"), i + 1)
                    sp.dma_start(ov[:, ds(i * CH, CH), :], acc[:, ds(i * CH, CH), :]).then_inc(s("out_stored"), 16)
                sp.wait_ge(s("out_stored"), 16 * (NT // CH))

            @block.gpsimd
            def _(pool):
                with pool.Fori(0, NT // CH) as i:
                    for k in range(CH):
                        hold(pool, f"scattered{k}", i * 16)
                        pool.tensor_copy(oslot[k], slot_out[:, ds(i * CH + k, 1)]).then_inc(s("oslot"), 1)
                        hold(pool, "oslot", i * CH + (k + 1))
                        hold(pool, f"xs_ready{k}", i + 1)
                        pool.indirect_dma_start(out=ebuf, out_offset=bass.IndirectOffsetOnAxis(ap=oslot[k], axis=0), in_=xs[k], in_offset=None).then_inc(s(f"scattered{k}"), 16)
                with pool.Fori(1, NE // 2) as i:
                    for c in (0, 1):
                        hold(pool, f"we_in{c}", i * 32)
                        hold(pool, "ye_ps", i * 4 + (2 * c - 2))
                        split_weights(pool, c, "w_split", i * 2 + (c - 2))
                pool.wait_ge(s("finite"), 2)
                pool.partition_all_reduce(bad[:, 1:2], bad[:, 0:1], P, bass.bass_isa.ReduceOp.add).then_inc(s("bad_all"), 1)
                pool.wait_ge(s("ye_out"), 16 * 2 * NE)
                with pool.Fori(0, NT // CH // 2) as i:
                    for c in (0, 1):
                        hold(pool, f"yg_used{c}", i)
                        for k in range(CH):
                            pool.tensor_copy(islot[c * CH + k], slot_in[:, ds(i * 2 * CH + (c * CH + k), 1)]).then_inc(s("islot"), 1)
                            hold(pool, "islot", i * 2 * CH + (c * CH + k + 1))
                            pool.indirect_dma_start(out=yg[c][:, k, :], out_offset=None, in_=ybuf,
                                                    in_offset=bass.IndirectOffsetOnAxis(ap=islot[c * CH + k], axis=0)).then_inc(s(f"yg_in{c}"), 16)

            @block.vector
            def _(v):
                def per_row(col, t, n=CH):
                    return col[:, ds(t, n)].rearrange("p (t o) -> p t o", o=1).broadcast_to([P, n, D])


                with v.Fori(0, NT // CH) as i:
                    for k in range(CH):
                        v.wait_ge(s(f"scattered{k}"), i * 16)
                        t = i * CH + k
                        v.tensor_scalar(xs[k], acc[:, ds(t, 1), :].rearrange("p t d -> p (t d)"), mean[:, ds(t, 1)], rstd[:, ds(t, 1)], ALU.subtract, ALU.mult).then_inc(s(f"xs_ready{k}"), 1)

                v.wait_ge(s("b1t_ps"), 1)
                v.tensor_copy(b1t.rearrange("p a b -> p (a b)"), bank[7][:, 0:NE * F // 128]).then_inc(s("b1t_ready"), 1)
                def copy_rows(k, i, t):
                    v.wait_ge(s("xe_turned"), t + 1)
                    v.wait_ge(s("hid_block"), less(t, 1) * (F // 128))
                    for dh in (0, 1):
                        v.tensor_copy(xet[k % 2][:, 0, dh, :], bank[dh][:, 0:4 * P]).then_inc(s("xet_hi"), 1)
                    v.wait_ge(s("xet_hi"), t * 2 + 2)
                    for dh in (0, 1):
                        v.tensor_tensor(xet[k % 2][:, 1, dh, :], bank[dh][:, 0:4 * P], xet[k % 2][:, 0, dh, :], ALU.subtract).then_inc(s("xet_ready"), 1)

                def hidden_lo(k, i, t):
                    for fb in range(F // 128):
                        v.wait_ge(s("relu_ready"), t * (F // 128) + (fb + 1))
                        v.tensor_tensor(hid[k % 2][:, 1, fb, :], relus[fb % 2], hid[k % 2][:, 0, fb, :], ALU.subtract).then_inc(s("hid_ready"), 1)

                def add_b2(k, i, t):
                    v.wait_ge(s("ye_ps"), t + 1)
                    v.wait_ge(s(f"b2_in{k // 2}"), i * 16 + 16)
                    v.wait_ge(s("ye_out"), t * 16)
                    for j in (0, 1):
                        v.tensor_tensor(ye[:, 2 * j:2 * j + 2, :], bank[5 + j][0:P, :].rearrange("p (a b) -> p a b", a=2), b2b[k // 2][:, None, :].broadcast_to([P, 2, D]), ALU.add).then_inc(s("ye_ready"), 1)
                    v.wait_ge(s("ye_ready"), t * 2 + 2)
                    v.wait_ge(s("flagged"), t)
                    v.tensor_scalar(junk_y, ye, 0.0, 0.0, ALU.mult, ALU.add, accum_out=flags[:, ds(t, 1)]).then_inc(s("flagged"), 1)
                pipeline(v, [(0, copy_rows), (1, hidden_lo), (2, add_b2)], 2 * NE, 4)
                v.wait_ge(s("flagged"), 2 * NE)
                v.tensor_scalar(flags, flags, 0.0, None, ALU.not_equal).then_inc(s("finite"), 1)
                v.wait_ge(s("finite"), 1)
                v.tensor_reduce(bad[:, 0:1], flags, AX.X, ALU.add).then_inc(s("finite"), 1)
                v.wait_ge(s("bad_all"), 1)
                v.tensor_copy(badi, bad[:, 1:2]).then_inc(s("finite"), 1)
                v.wait_ge(s("finite"), 3)

                v.memset(fill[0], 0.0).then_inc(s("fills"), 1)
                v.memset(fill[1], 10000.0).then_inc(s("fills"), 1)
                v.memset(fill[2], -10000.0).then_inc(s("fills"), 1)
                v.wait_ge(s("fills"), 3)
                any_bad = v.value_load(badi[0:1, 0:1], min_val=0, max_val=2 * NE * P)
                with v.If(any_bad > 0):
                    with v.Fori(0, NT // CH // 2) as i:
                        for k in (0, 1):
                            t, n = i * 2 * CH + k * CH, i * 12 + k * 6
                            v.wait_ge(s(f"yg_in{k}"), i * 16 * CH + 16 * CH)
                            v.tensor_tensor(yg[k], yg[k], per_row(pk, t), ALU.mult).then_inc(s("fin"), 1)
                            v.wait_ge(s("fin"), n + 1)
                            v.tensor_tensor(msk[0], yg[k], yg[k], ALU.not_equal).then_inc(s("fin"), 1)
                            v.tensor_scalar(msk[1], yg[k], 3.4028234e38, None, ALU.is_gt).then_inc(s("fin"), 1)
                            hold(v, "fin", n + 3, "dve")
                            v.copy_predicated(yg[k], msk[1], fill[1][:, None, :].broadcast_to([P, CH, D])).then_inc(s("fin"), 1)
                            hold(v, "fin", n + 4, "dve")
                            v.copy_predicated(yg[k], msk[0], fill[0][:, None, :].broadcast_to([P, CH, D])).then_inc(s("fin"), 1)
                            v.wait_ge(s("fin"), n + 5)
                            v.tensor_scalar(msk[1], yg[k], -3.4028234e38, None, ALU.is_lt).then_inc(s("fin"), 1)
                            hold(v, "fin", n + 6, "dve")
                            v.copy_predicated(yg[k], msk[1], fill[2][:, None, :].broadcast_to([P, CH, D])).then_inc(s("fin2"), 1)
                            v.wait_ge(s("fin2"), i * 2 + (k + 1))
                            at = acc[:, ds(t, CH), :]
                            v.tensor_tensor(at, at, yg[k], ALU.add).then_inc(s(f"yg_used{k}"), 1)
                            v.wait_ge(s(f"yg_used{k}"), i + 1)
                            v.sem_inc(s("out_ready"), 1)
                with v.If(any_bad < 1):
                    with v.Fori(0, NT // CH // 2) as i:
                        for k in (0, 1):
                            t = i * 2 * CH + k * CH
                            v.wait_ge(s(f"yg_in{k}"), i * 16 * CH + 16 * CH)
                            for j in range(CH):
                                at = acc[:, ds(t + j, 1), :].rearrange("p t d -> p (t d)")
                                v.scalar_tensor_tensor(at, yg[k][:, j, :], pk[:, ds(t + j, 1)], at, ALU.mult, ALU.add).then_inc(s("added_up"), 1)
                            v.wait_ge(s("added_up"), t + CH)
                            v.sem_inc(s(f"yg_used{k}"), 1)
                            v.sem_inc(s("out_ready"), 1)

            @block.scalar
            def _(a):
                for k in range(CH):
                    a.wait_ge(s(f"scattered{k}"), 16 * (NT // CH))
                a.dma_start(b1rows, b1.rearrange("e (a p) -> (e a) p", p=128)).then_inc(s("b1_in"), 16)
                a.wait_ge(s("b1t_ready"), 1)

                def hidden(k, i, t):
                    a.wait_ge(s("ye_ps"), less(t, 1))
                    for fb in range(F // 128):
                        hold(a, "hid_block", t * (F // 128) + (fb + 1), "act")
                        b1c = b1t[:, ds(i * 2 + k // 2, 1), fb:fb + 1].rearrange("p a b -> p (a b)")
                        a.activation(hid[k % 2][:, 0, fb, :], bank[2 + fb % 3][:, 0:4 * P], ACT.Relu, bias=b1c).then_inc(s("relu_hi"), 1)
                        if fb >= 2:
                            hold(a, "hid_ready", t * (F // 128) + (fb - 1), "act")
                        else:
                            hold(a, "hid_ready", less(t, 1) * (F // 128) + (F // 128 - 1 + fb if not isinstance(t, int) or t > 0 else 0), "act")
                        a.activation(relus[fb % 2], bank[2 + fb % 3][:, 0:4 * P], ACT.Relu, bias=b1c).then_inc(s("relu_ready"), 1)
                pipeline(a, [(0, hidden)], 2 * NE, 4)

            @block.tensor
            def _(pe):
                pe.wait_ge(s("b1_in"), 16)
                pe.transpose(bank[7][:, 0:NE * F // 128], b1rows, ident[0:NE * F // 128, 0:NE * F // 128]).then_inc(s("b1t_ps"), 1)

                def turn_rows(k, i, t):
                    pe.wait_ge(s(f"xe_in{k % 2}"), i * 32 + (k // 2 * 16 + 16))
                    pe.wait_ge(s("xet_ready"), 2 * t)
                    for dh in (0, 1):
                        for j in range(4):
                            mm = pe.transpose(bank[dh][:, j * P:j * P + P], xe[k % 2][:, j, dh * 128:dh * 128 + 128], ident[0:P, 0:P])
                    mm.then_inc(s("xe_turned"), 1)

                def expert1(k, i, t):
                    pe.wait_ge(s("xet_ready"), 2 * t + 2)
                    if not isinstance(t, int) or t >= 4:
                        pe.wait_ge(s("w_split"), (i * 2 + (k // 2 - 1)) * 2)
                    for fb in range(F // 128):
                        if fb >= 3:
                            pe.wait_ge(s("relu_ready"), t * (F // 128) + (fb - 2))
                        else:
                            pe.wait_ge(s("relu_ready"), t * (F // 128))
                        n = 0
                        for xh, wh in ((0, 0), (1, 0), (0, 1)):
                            for dh in (0, 1):
                                mm = pe.matmul(bank[2 + fb % 3][:, 0:4 * P], we[k // 2][0][:, wh, dh, fb * 128:fb * 128 + 128], xet[k % 2][:, xh, dh, :], start=(n == 0), stop=(n == 5))
                                n += 1
                        mm.then_inc(s("hid_block"), 1)

                def expert2(k, i, t):
                    pe.wait_ge(s("hid_ready"), (t + 1) * (F // 128))
                    pe.wait_ge(s("ye_ready"), 2 * t)
                    for j in range(4):
                        n = 0
                        for fb in range(F // 128):
                            for hh, wh in ((0, 0), (0, 1), (1, 0)):
                                mm = pe.matmul(bank[5 + j // 2][0:P, j % 2 * D:j % 2 * D + D], hid[k % 2][:, hh, fb, j * P:j * P + P], we[k // 2][1][:, wh, fb, :],
                                               start=(n == 0), stop=(n == 3 * F // 128 - 1))
                                n += 1
                    mm.then_inc(s("ye_ps"), 1)
                pipeline(pe, [(0, turn_rows), (1, expert1), (2, expert2)], 2 * NE, 4)


_INS = ["x", "src", "dst", "L0_gnn_W", "L0_gnn_att", "L0_gnn_b", "L0_mix_Wq", "L0_mix_bq", "L0_mix_Wk", "L0_mix_bk",
        "L0_mix_Wv", "L0_mix_bv", "L0_mix_Wo", "L0_mix_bo", "L0_mix_proj", "L0_mix_W1", "L0_mix_bias1", "L0_mix_W2",
        "L0_mix_bias2", "L0_mix_g1", "L0_mix_beta1", "L0_mix_g2", "L0_mix_beta2", "L0_ffn_gate_w", "L0_ffn_gate_b",
        "L0_ffn_w1", "L0_ffn_b1", "L0_ffn_w2", "L0_ffn_b2"]


def kernel(**inputs):
    import numpy as _np
    import concourse.bacc as _bacc
    from concourse import mybir as _mybir
    from concourse.bass_utils import run_bass_kernel_spmd as _run

    nc = _bacc.Bacc("TRN2", target_bir_lowering=False, num_devices=1)
    arrays, args = {}, []
    for name in _INS:
        a = _np.ascontiguousarray(inputs[name])
        arrays[f"in_{name}_dram"] = a
        args.append(nc.dram_tensor(f"in_{name}_dram", a.shape, _mybir.dt.from_np(a.dtype), kind="ExternalInput").ap())
    args.append(nc.dram_tensor("out_0_dram", (N, D), F32, kind="ExternalOutput").ap())
    gps_layer(nc, *args)
    r = _run(nc, [arrays], core_ids=[0])
    return r.results[0]["out_0_dram"]
```

```python
import math
from contextlib import ExitStack, contextmanager

import concourse.bass as bass
from concourse import mybir

F32, I32 = mybir.dt.float32, mybir.dt.int32
F16, BF16 = mybir.dt.float16, mybir.dt.bfloat16
ALU, ACT, AX = mybir.AluOpType, mybir.ActivationFunctionType, mybir.AxisListType
ds = bass.ds

N, D, E = 6250, 256, 200000
P = 125
NT = N // P
GH, GD = 4, 64
H, M = 8, 256
NE, F = 8, 1024
CAP = -(-5 * N // (4 * NE))
CT = 8
CB = CT * P
LOG16 = 2.772588722239781
LN_EPS, MIX_EPS, PHI_EPS = 1e-5, 1e-6, 1e-6
ROWW = D + GH
SR = 400
NS = E // SR
WIN, BLK = 64, 4
WB = WIN // BLK
SHIFT = 32.0
NBK = 64
NSB = -(-NBK * NT // 512)
CH = 5
ARENA = 9720
LCH = 10


@contextmanager
def steps(engine, n, step):
    with engine.Fori(0, n // step) as i:
        yield i * step


def gps_layer(nc, x, src, dst, gW, gatt, gb, Wq, bq, Wk, bk, Wv, bv, Wo, bo, proj, W1, bias1, W2, bias2,
              g1, beta1, g2, beta2, gate_w, gate_b, w1, b1, w2, b2, out):
    ctx = ExitStack()
    with ctx:
        def sb(name, shape, dt=F32):
            return ctx.enter_context(nc.sbuf_tensor(name, shape, dt))

        def sem(name):
            return ctx.enter_context(nc.semaphore(name))

        def scratch(name, shape, dt=F32):
            return nc.dram_tensor(name, shape, dt, kind="Internal").ap()

        table = scratch("gather_table", [N + 1, ROWW])
        srcpad = scratch("src_padded", [E + WIN], I32)
        by_degree = scratch("nodes_by_degree", [N, 2], I32)
        sums = scratch("neighbour_sums", [N, ROWW])
        acc = sb("acc", [P, NT, D])
        xa_full = [sb(f"xa{i}", [128, NT, D + 2], F16) for i in (0, 1)]
        xa = [full[0:P] for full in xa_full]
        xt = xt_all = sb("xt", [128, NT, 4, 128], F16)
        mean = sb("mean", [P, NT])
        rstd = sb("rstd", [P, NT])
        nmr = sb("nmr", [P, NT])
        wf = sb("wf", [P, NT, 2 * GH])
        ident = sb("ident", [128, 128])
        identh = sb("identh", [128, 128], F16)
        ones = sb("ones", [128, 128])
        spare = sb("spare", [P, 2])
        nones = sb("nones", [1, 128])
        bank = [ctx.enter_context(nc.psum_tensor(f"bank{i}", [128, 512], F32)) for i in range(8)]
        gacc = sb("gacc", [P, 2, BLK, ROWW])
        rank = sb("rank", [P, NT], I32)
        perm = sb("perm", [P, NT, 2], I32)
        nblk = sb("nblk", [1, 4, NT], I32)
        woff = [sb(f"woff{k}", [P, 1], I32) for k in (0, 1)]
        wrem = [sb(f"wrem{k}", [P, 1]) for k in (0, 1)]
        widx = [sb(f"widx{k}", [P, WIN], I32) for k in (0, 1)]
        wmask = sb("wmask", [P, WIN], I32)
        gidx = [sb(f"gidx{k}", [P, WIN], I32) for k in (0, 1)]
        kpos = sb("kpos", [P, WIN])
        zrow = sb("zrow", [1, ROWW])
        arena = sb("arena", [128, ARENA])
        a_off = [0]

        def cut(shape, dt=F32, parts=128):
            n = math.prod(shape) * (2 if dt in (F16, BF16) else 4)
            o = a_off[0]
            a_off[0] = o + -(-n // 4)
            assert a_off[0] <= ARENA, a_off[0]
            v = arena[0:parts, o:o + -(-n // 4)]
            if dt != F32:
                v = v.bitcast(dt)
            if len(shape) == 2:
                v = v.rearrange("p (a b) -> p a b", b=shape[1])
            if len(shape) == 3:
                v = v.rearrange("p (a b c) -> p a b c", b=shape[1], c=shape[2])
            if len(shape) == 4:
                v = v.rearrange("p (a b c d) -> p a b c d", b=shape[1], c=shape[2], d=shape[3])
            return v

        a_off[0] = 0
        st6 = cut([NT, 6], F32, P)
        stt = [cut([NT], F32, P) for _ in range(9)]
        eps = cut([1], F32, P)
        shf = cut([1], F32, P)
        gwf = cut([2, D])
        gw = cut([2, 2, D], F16)
        attb = cut([2, D], F32, P)
        lk = cut([CH, D], F32, P)
        tat_at = a_off[0]
        tat = cut([CH * 2, D], F32, P)
        mx = cut([2 * GH], F32, P)
        mxa = cut([2 * GH], F32, P)
        firsts = cut([NS], F32, P + 1)
        first1 = arena[0:1, tat_at:tat_at + NS].bitcast(I32)
        first1f = arena[0:1, tat_at + NS:tat_at + 2 * NS]
        dq = cut([NT], F32, P + 1)
        cnt1 = cut([NT], F32, P + 1)
        cnt2 = cut([NT], F32, P + 1)
        offf = cut([NT], F32, P + 1)
        ri = cut([NT], I32, P + 1)
        junk_at = a_off[0]
        junk = cut([2, 512], F16, P + 1)
        rslot = [cut([1], I32, P + 1) for _ in range(CH)]
        drow_at = a_off[0]
        drow = cut([CH, SR], I32, P + 1)
        srcs = arena[0:P, drow_at:drow_at + E // P].bitcast(I32)
        offT = cut([P + 1], F32, NT)
        degT = cut([P], F32, NT)
        mxd = cut([4], F32, NT)
        lk_at = tat_at - CH * D
        tot = arena[0:P, lk_at:lk_at + NBK * NT].rearrange("p (b t) -> p b t", t=NT)
        tri = arena[0:P, junk_at:junk_at + P]
        trih = arena[0:P, junk_at + 126:junk_at + 190].bitcast(BF16)[:, 0:P]
        onesh = arena[0:P, junk_at + 190:junk_at + 254].bitcast(BF16)[:, 0:P]
        bids_i = arena[0:P, junk_at + 254:junk_at + 254 + NBK].bitcast(I32)
        bids = arena[0:P, junk_at + 320:junk_at + 320 + NBK]
        oh = arena[0:P, drow_at:drow_at + NBK * NT // 2].bitcast(BF16).rearrange("p (b t) -> p b t", t=NT)
        o = drow_at + NBK * NT // 2
        nrow = arena[0:1, o:o + 4 * NT].rearrange("p (a b) -> p a b", b=NT)
        nsum = arena[0:1, o + 4 * NT:o + 6 * NT].rearrange("p (a b) -> p a b", b=NT)
        entry = arena[0:P, o + 6 * NT:o + 8 * NT].bitcast(I32).rearrange("p (t a) -> p t a", a=2)
        bucket = cnt1[0:P]
        degs = arena[0:P, junk_at + 384:junk_at + 384 + NT]
        pslot = [arena[0:P, junk_at + 440 + 15 * c:junk_at + 445 + 15 * c].bitcast(I32) for c in (0, 1)]
        eslot = [arena[0:P, junk_at + 445 + 15 * c:junk_at + 455 + 15 * c].bitcast(I32).rearrange("p (t a) -> p t a", a=2) for c in (0, 1)]
        mxi = cut([2], I32, NT)

        a_off[0] = 0
        wc = [cut([2, 2, 2 * D], F16) for _ in (0, 1)]
        bmat = cut([2, D])
        wbase = a_off[0]
        ex = [cut([M], F32, P) for _ in range(4)]
        sqj = [cut([M], F32, P) for _ in range(4)]
        sq = [cut([1], F32, P) for _ in range(4)]
        nsq = [cut([1], F32, P) for _ in range(4)]
        ph = [cut([2, M], BF16, P) for _ in range(4)]
        kvs = cut([2, D + 2])
        kvt = cut([2, M])
        kvo = cut([2, 2, D + 2], BF16)
        qt = [cut([2, 2, 128], BF16) for _ in range(4)]
        rz = [cut([1], F32, P) for _ in range(4)]
        fbank = {"k": [bank[j] for j in (0, 1, 6, 7)], "q": [bank[j] for j in (0, 1, 2, 3)]}
        zero = cut([128], BF16, P)
        a_off[0] = wbase
        wraw = cut([3, 2, D])
        wo = cut([2, D])
        brow = cut([3, D], F32, 1)
        brow_bo = cut([D], F32, P)
        wt = cut([3, 2, D])
        projr = cut([2, D])
        projt = cut([2, M])
        wcat = scratch("mix_weights", [H, 2, 128, 2 * 2 * 2 * D], F16)
        bdram = scratch("mix_wv_wo", [H, 128, 2 * D])

        a_off[0] = 0
        tst = cut([NT, 6], F32, P)
        tln = [cut([NT], F32, P) for _ in range(8)]
        slot_out = cut([NT], I32, P)
        slot_in = cut([NT], I32, P)
        pk = cut([NT], F32, P)
        b1t = cut([NE, F // 128])
        flags = cut([2 * NE], F32, P)
        bad = cut([2], F32, P)
        badi = cut([1], I32, P)
        used = cut([NE, 2], I32, 1)
        rows_of = cut([NE, 2], F32, 1)
        above = cut([NE, 2], F32, 1)
        gate = cut([2, NE])
        gateb = cut([NE], F32, P)
        tail = a_off[0]
        g1b, beta1b, g2b, beta2b, bias2b, gnnb = (cut([D], F32, P) for _ in range(6))
        W1s, W2s = (cut([2, D]) for _ in (0, 1))
        b1r = cut([128], F32, 2)
        bias1t = cut([2])
        xc = [cut([CH, D], F32, P) for _ in (0, 1)]
        fbase = a_off[0]
        xr = xc + [cut([CH, D], F32, P)]
        a_off[0] = fbase
        ot = [cut([2, 2 * P]) for _ in (0, 1)]
        ht = [cut([2, 2 * P]) for _ in (0, 1)]
        a_off[0] = fbase

        def rows_in(full, k):
            w = full[0:P].rearrange("p t d -> p (t d)").bitcast(F32)
            return w[:, k * LCH * ROWW:(k + 1) * LCH * ROWW].rearrange("p (t d) -> p t d", d=ROWW)
        gs = [rows_in(xa_full[0], k) for k in (0, 1)]
        own = [rows_in(xa_full[1], k) for k in (0, 1)]
        a_off[0] = fbase + 1000
        gslot = [cut([LCH], I32, P) for _ in (0, 1)]
        zw = cut([NT, GH], F32, P)
        zpart = cut([GH], F32, P)
        zall = cut([GH], F32, P)
        upper = cut([P], F32, P)
        down = cut([NE], F32, P)
        downi = cut([NE], I32, P)
        node = cut([NT], I32, P)
        rdump = cut([NT], F32, P)
        scaled = xt_all[:, :, :, :].rearrange("p t j n -> p (t j n)").bitcast(F32)[0:P].rearrange("p (t d) -> p t d", d=D)
        lg = cut([NT, NE], F32, P)
        xft = [cut([2, P]) for _ in range(CH)]
        o1 = [xc[k // 2][:, 2 * (k % 2):2 * (k % 2) + 2, :] for k in range(4)]
        xfs = xc
        a_off[0] = tail
        rmax, rsum, rinv, ridx, rpos, rkept, rtmp = (cut([NT], F32, P) for _ in range(7))
        rex, roh, rtot, rscan = (cut([NT, NE], F32, P) for _ in range(4))
        xs = [cut([D], F32, P) for _ in range(CH)]
        oslot = [cut([1], I32, P) for _ in range(CH)]
        assert a_off[0] < fbase
        a_off[0] = tail
        xe = [cut([4, D], F32, P) for _ in (0, 1)]
        xet = [cut([2, 2, 4 * P], F16) for _ in (0, 1)]
        hid0 = cut([2, F // 128, 4 * P], F16)
        b1rows = arena[0:NE * F // 128, a_off[0] - 4 * P:a_off[0] - 4 * P + 128]
        xt_words = xt_all[:, :, :, :].rearrange("p t j n -> p (t j n)").bitcast(F32)
        WW = 2 * F + F // 128 * D
        ws = []
        for k in (0, 1):
            w = xt_words[:, k * WW:k * WW + WW]
            ws.append((w[:, 0:2 * F].rearrange("p (a f) -> p a f", a=2), w[:, 2 * F:WW].rearrange("p (a d) -> p a d", d=D)))
        hid = [hid0, xt_words[:, 2 * WW:2 * WW + F // 128 * 4 * P].bitcast(F16).rearrange("p (h a b) -> p h a b", h=2, a=F // 128)]
        relus = [cut([4 * P]), xt_words[:, 2 * WW + F // 128 * 4 * P:2 * WW + (F // 128 + 1) * 4 * P]]
        gflat = gacc[:, :, :, :].rearrange("p a b c -> p (a b c)")
        ye = gflat[:, 0:4 * D].rearrange("p (a b) -> p a b", b=D)
        b2b = [gflat[:, (4 + k) * D:(5 + k) * D] for k in (0, 1)]
        junk_y = gflat[:, 6 * D:8 * D].bitcast(BF16).rearrange("p (a b) -> p a b", b=D)
        we = []
        for full in xa_full:
            w = full[:, :, :].rearrange("p t d -> p (t d)")
            we.append((w[:, 0:4 * F].rearrange("p (h a f) -> p h a f", h=2, a=2), w[:, 4 * F:2 * WW].rearrange("p (h a d) -> p h a d", h=2, d=D)))
        a_off[0] = tail
        yg = [cut([CH, D], F32, P) for _ in (0, 1)]
        msk = [cut([CH, D], I32, P) for _ in (0, 1)]
        fill = [cut([D], F32, P) for _ in range(3)]
        islot = [cut([1], I32, P) for _ in range(2 * CH)]
        ebuf = scratch("expert_rows", [NE * CB + N, D])
        ybuf = scratch("expert_out", [NE * CB, D])

        S, kept = {}, {}

        def s(name):
            if name in kept:
                return kept[name]
            if name not in S:
                S[name] = nc.alloc_semaphore(name)
            return S[name]

        for name in (["widx_in", "more_in", "entries_out0", "entries_out1", "gs_in0", "gs_in1", "yg_in0", "yg_in1"]
                     + [f"row_in{k}" for k in range(CH)] + [f"added{j}" for j in range(BLK)] + [f"scattered{k}" for k in range(CH)]):
            kept[name] = sem(name)

        def next_part():
            for handle in S.values():
                nc.gpsimd.sem_clear(handle)
                nc.release_semaphore(handle)
            S.clear()
            nc.all_engine_barrier()

        def hold(e, name, value, who="pool"):
            e.wait_ge(s(name), value)
            e.sem_inc(s(who + "_passed"), 1)

        xv = x.rearrange("(t p) d -> p t d", p=P)

        def split_weights(pool, c, m, name, n):
            pool.tensor_copy(we[c][m][:, 0], ws[c][m]).then_inc(s(name + "_hi"), 1)
            hold(pool, name + "_hi", n + 1)
            pool.tensor_tensor(we[c][m][:, 1], ws[c][m], we[c][m][:, 0], ALU.subtract).then_inc(s(name), 1)

        def less(t, n):
            return max(t - n, 0) if isinstance(t, int) else t + -n

        def pipeline(e, stages, n=NT, un=2):
            lag = max(a for a, _ in stages)
            ramp = lag + un - 1
            rounds = (n - ramp) // un
            for t in range(ramp):
                for a, step in stages:
                    if t >= a:
                        step((t - a) % un, (t - a) // un, t - a)
            with e.Fori(0, rounds) as i:
                for u in range(un):
                    for a, step in stages:
                        o = ramp + u - a
                        step(o % un, i + o // un, i * un + o)
            for t in range(ramp + un * rounds, n + lag):
                for a, step in stages:
                    if t - a < n:
                        step((t - a) % un, (t - a) // un, t - a)


        with nc.Block() as block:
            @block.sync
            def _(sp):
                sp.dma_start(first1, dst.rearrange("(a b) -> a b", b=SR)[:, 0:1].rearrange("a b -> b a"), allow_slow_non_contiguous=True).then_inc(s("firsts_in"), 16)
                sp.dma_start(srcs, src.rearrange("(p b) -> p b", p=P)).then_inc(s("src_in"), 16)
                for c in range(NT // LCH):
                    sp.dma_start(acc[:, c * LCH:(c + 1) * LCH, :], xv[:, c * LCH:(c + 1) * LCH, :]).then_inc(s(f"x_in{c}"), 16)
                sp.dma_start(gwf, gW.rearrange("(a p) n -> p a n", p=128)).then_inc(s("gw_in"), 16)
                av = gatt.rearrange("o h (s d) -> o s h d", s=2)
                for k in (0, 1):
                    sp.dma_start(attb[:, k, :].rearrange("p (h d) -> p h d", d=GD),
                                 av[:, k].broadcast_to([P, GH, GD])).then_inc(s("att_in"), 16)
                sp.wait_ge(s("src_plus"), 1)
                sp.dma_start(srcpad[0:E].rearrange("(p b) -> p b", p=P), srcs).then_inc(s("src_out"), 16)
                sp.wait_ge(s("zeros_ready"), 1)
                sp.dma_start(srcpad[E:E + WIN].rearrange("(o n) -> o n", o=1), zrow[0:1, 0:WIN].bitcast(I32)).then_inc(s("src_out"), 16)
                sp.dma_start(table[0:1, :], zrow[:, :]).then_inc(s("table_in"), 16)
                sp.wait_ge(s("gacc_zero"), 1)
                for c in range(NE * CB * D // (P * 8 * D)):
                    sp.dma_start(ebuf[0:NE * CB, :].rearrange("(c p r) d -> c p (r d)", p=P, r=8)[c], gacc[:, :, :, :].rearrange("p a b c -> p (a b c)")[:, 0:8 * D]).then_inc(s("ebuf_zero"), 16)
                tv = table[1:N + 1, :].rearrange("(t p) d -> p t d", p=P)
                sp.wait_ge(s("w_ready"), 1)
                sp.dma_start(tv[:, :, D:D + GH], wf[:, :, 0:GH]).then_inc(s("table_in"), 16)
                with steps(sp, NT, CH) as t:
                    sp.wait_ge(s("g_ready"), t + CH)
                    sp.dma_start(tv[:, ds(t, CH), 0:D], acc[:, ds(t, CH), :]).then_inc(s("table_in"), 16)
                sp.wait_ge(s("ebuf_zero"), 16 * (NE * CB // (P * 8)))
                sp.wait_ge(s("table_in"), 16 * (2 + NT // CH))

            @block.gpsimd
            def _(pool):
                pool.memset(zrow[:, :], 0.0).then_inc(s("zeros_ready"), 1)
                pool.memset(gacc[:, :, :, :].rearrange("p a b c -> p (a b c)")[:, 0:8 * D], 0.0).then_inc(s("gacc_zero"), 1)
                pool.memset(ones[:, :], 1.0).then_inc(s("ones_ready"), 1)
                pool.memset(nones[:, :], -1.0).then_inc(s("ones_ready"), 1)
                pool.memset(ident[:, :], 0.0).then_inc(s("id0"), 1)
                pool.wait_ge(s("id0"), 1)
                pool.affine_select(out=ident[:, :], in_=ident[:, :], compare_op=ALU.not_equal, fill=1.0, base=0,
                                   pattern=[[-1, 128]], channel_multiplier=1).then_inc(s("ident_ready"), 1)
                pool.wait_ge(s("ident_ready"), 1)
                pool.tensor_copy(identh[:, :], ident[:, :]).then_inc(s("identh_ready"), 1)
                pool.iota(ri, pattern=[[P, NT]], base=0, channel_multiplier=1).then_inc(s("iotas"), 1)
                pool.iota(gidx[0][:, :], pattern=[[1, WIN]], base=0, channel_multiplier=0).then_inc(s("iotas"), 1)
                pool.memset(eps, LN_EPS).then_inc(s("eps_ready"), 1)
                pool.memset(shf, SHIFT).then_inc(s("eps_ready"), 1)
                pool.wait_ge(s("iotas"), 2)
                pool.tensor_copy(dq, ri).then_inc(s("dq_ready"), 1)
                pool.tensor_copy(kpos[:, :], gidx[0][:, :]).then_inc(s("kpos_ready"), 1)
                for k in (0, 1):
                    pool.memset(xa[k][:, :, D:D + 2], 1.0 - k).then_inc(s("xa_ones"), 1)
                pool.wait_ge(s("src_in"), 16)
                pool.tensor_scalar(srcs, srcs, 1.0, None, ALU.add).then_inc(s("src_plus"), 1)
                pool.wait_ge(s("src_out"), 32)
                pool.wait_ge(s("ri_ready"), 1)

                def fetch_row(t, k):
                    pool.tensor_copy(rslot[k], ri[:, ds(t, 1)]).then_inc(s("rslot_ready"), 1)
                    hold(pool, "rslot_ready", t + 1)
                    pool.indirect_dma_start(out=drow[:, k, :], out_offset=None, in_=dst.rearrange("(a b) -> a b", b=SR),
                                            in_offset=bass.IndirectOffsetOnAxis(ap=rslot[k], axis=0)).then_inc(s(f"row_in{k}"), 16)
                for k in range(CH):
                    fetch_row(k, k)
                with pool.Fori(1, NT // CH) as i:
                    for k in range(CH):
                        pool.wait_ge(s("cnt2"), i * CH + (k + 1 - CH))
                        fetch_row(i * CH + k, k)
                pool.wait_ge(s("cnt2"), NT)
                pool.memset(tri, -1.0).then_inc(s("sort_consts"), 1)
                pool.tensor_copy(onesh, ones[0:P, 0:P]).then_inc(s("sort_consts"), 1)
                pool.iota(bids_i, pattern=[[1, NBK]], base=0, channel_multiplier=0).then_inc(s("sort_consts"), 1)
                pool.wait_ge(s("sort_consts"), 3)
                pool.affine_select(out=tri, in_=tri, compare_op=ALU.is_ge, fill=0.0, base=-1, pattern=[[-1, P]], channel_multiplier=1).then_inc(s("sort_consts"), 1)
                pool.tensor_copy(bids, bids_i).then_inc(s("sort_consts"), 1)
                pool.wait_ge(s("sort_consts"), 5)
                pool.tensor_copy(trih, tri).then_inc(s("sort_consts"), 1)
                pool.wait_ge(s("rank_ready"), 1)
                pool.wait_ge(s("entry_ready"), 2)
                with pool.Fori(0, NT // CH // 2) as i:
                    for c in (0, 1):
                        t = i * 2 * CH + c * CH
                        hold(pool, f"entries_out{c}", i * 16 * CH)
                        pool.tensor_copy(pslot[c], rank[:, ds(t, CH)]).then_inc(s("entry_slot"), 1)
                        pool.tensor_copy(eslot[c].bitcast(F32), entry[:, ds(t, CH), :].bitcast(F32)).then_inc(s("entry_slot"), 1)
                        hold(pool, "entry_slot", i * 4 + (c * 2 + 2))
                        for j in range(CH):
                            pool.indirect_dma_start(out=by_degree, out_offset=bass.IndirectOffsetOnAxis(ap=pslot[c][:, j:j + 1], axis=0),
                                                    in_=eslot[c][:, j, :], in_offset=None).then_inc(s(f"entries_out{c}"), 16)
                pool.wait_ge(s("mx_ready"), 1)
                pool.partition_all_reduce(mxa, mx, P, bass.bass_isa.ReduceOp.max).then_inc(s("mxa_ready"), 1)

            @block.vector
            def _(v):
                v.wait_ge(s("firsts_in"), 16)
                v.tensor_copy(first1f, first1).then_inc(s("first1f_ready"), 1)
                v.wait_ge(s("firsts_bcast"), 1)
                v.tensor_copy(firsts, bank[7][0:P + 1, 0:NS]).then_inc(s("firsts_ready"), 1)
                v.wait_ge(s("firsts_ready"), 1)
                v.wait_ge(s("dq_ready"), 1)
                with steps(v, NT, 2) as t:
                    for k in (0, 1):
                        v.wait_ge(s("cnt1"), t + (k - 1) if k else t)
                        v.tensor_scalar(junk[:, k, 0:NS], firsts, dq[:, ds(t + k, 1)], 0.0, ALU.is_lt, ALU.add,
                                        accum_out=cnt1[:, ds(t + k, 1)]).then_inc(s("cnt1"), 1)
                v.wait_ge(s("cnt1"), NT)
                v.tensor_scalar(ri, cnt1, -1.0, 0.0, ALU.add, ALU.max).then_inc(s("ri_ready"), 1)

                for c in range(NT // LCH):
                    v.wait_ge(s(f"x_in{c}"), 16)
                    with v.Fori(c * LCH, (c + 1) * LCH) as t:
                        v.bn_stats(st6[:, ds(t, 1), :].rearrange("p t a -> p (t a)"), acc[:, ds(t, 1), :].rearrange("p t d -> p (t d)")).then_inc(s("stats"), 1)
                v.wait_ge(s("stats"), NT)
                me, ve, mo, vo = st6[:, :, 1], st6[:, :, 2], st6[:, :, 4], st6[:, :, 5]
                q, dm, vs, ve_, va, r0, r2, r3 = stt[0:8]
                v.tensor_tensor(q, me, mo, ALU.add).then_inc(s("ln"), 1)
                v.tensor_tensor(dm, me, mo, ALU.subtract).then_inc(s("ln"), 1)
                v.tensor_tensor(vs, ve, vo, ALU.add).then_inc(s("ln"), 1)
                v.wait_ge(s("ln"), 3)
                v.tensor_scalar(mean[:, :], q, 0.5, None, ALU.mult).then_inc(s("ln"), 1)
                v.scalar_tensor_tensor(r0, dm, 0.25, dm, ALU.mult, ALU.mult).then_inc(s("ln"), 1)
                v.wait_ge(s("ln"), 5)
                v.scalar_tensor_tensor(va, vs, 1.0 / D, r0, ALU.mult, ALU.add).then_inc(s("ln"), 1)
                v.wait_ge(s("ln"), 6)
                v.tensor_scalar(ve_, va, LN_EPS, None, ALU.add).then_inc(s("var_ready"), 1)
                v.wait_ge(s("sqrt_ready"), 1)
                v.reciprocal(r2, r3).then_inc(s("ln"), 1)
                v.wait_ge(s("ln"), 7)
                v.tensor_tensor(q, r2, r2, ALU.mult).then_inc(s("ln"), 1)
                v.wait_ge(s("ln"), 8)
                v.scalar_tensor_tensor(dm, q, -0.5, ve_, ALU.mult, ALU.mult).then_inc(s("ln"), 1)
                v.wait_ge(s("ln"), 9)
                v.scalar_tensor_tensor(rstd[:, :], dm, 1.5, r2, ALU.add, ALU.mult).then_inc(s("ln"), 1)
                v.wait_ge(s("ln"), 10)
                v.wait_ge(s("colsum"), 1)
                v.scalar_tensor_tensor(gwf, bank[6][:, None, 0:D].broadcast_to([128, 2, D]), -1.0 / D, gwf, ALU.mult, ALU.add).then_inc(s("gwc"), 1)
                v.wait_ge(s("gwc"), 1)
                v.tensor_copy(gw[:, 0], gwf).then_inc(s("gwh"), 1)
                v.wait_ge(s("gwh"), 1)
                v.tensor_tensor(gw[:, 1], gwf, gw[:, 0], ALU.subtract).then_inc(s("gw_ready"), 1)
                v.scalar_tensor_tensor(nmr[:, :], mean[:, :], -1.0, rstd[:, :], ALU.mult, ALU.mult).then_inc(s("nmr_ready"), 1)
                with v.Fori(0, NT // CH) as i:
                    t = i * CH
                    v.wait_ge(s("xn"), t + CH)
                    xn = acc[:, ds(t, CH), :]
                    hi, lo = (xa[k][:, ds(t, CH), 0:D] for k in (0, 1))
                    v.tensor_scalar(hi, xn, 1.0, None, ALU.add).then_inc(s("xa_hi"), CH)
                    v.wait_ge(s("xa_hi"), t + CH)
                    v.scalar_tensor_tensor(lo, xn, 1.0, hi, ALU.add, ALU.subtract).then_inc(s("xa_ready"), CH)
                    for k in range(CH):
                        v.wait_ge(s(f"row_in{k}"), i * 16 + 16)
                        if k >= 2:
                            v.wait_ge(s("cnt2"), t + (k - 1))
                        else:
                            v.wait_ge(s("cnt2"), t)
                        v.tensor_scalar(junk[:, k % 2, 0:SR], drow[:, k, :], dq[:, ds(t + k, 1)], 0.0, ALU.is_lt, ALU.add,
                                        accum_out=cnt2[:, ds(t + k, 1)]).then_inc(s("cnt2"), 1)
                v.wait_ge(s("cnt2"), NT)
                v.scalar_tensor_tensor(offf, ri, float(SR), cnt2, ALU.mult, ALU.add).then_inc(s("off_ready"), 1)
                v.wait_ge(s("off_ready"), 1)
                v.tensor_copy(entry[:, :, 0], offf[0:P]).then_inc(s("entry_ready"), 1)
                v.wait_ge(s("off_t"), 1)
                v.tensor_copy(offT, bank[7][0:NT, 0:P + 1]).then_inc(s("offT"), 1)
                v.wait_ge(s("offT"), 1)
                v.tensor_tensor(degT, offT[:, 1:P + 1], offT[:, 0:P], ALU.subtract).then_inc(s("degT"), 1)
                v.wait_ge(s("deg_t"), 1)
                v.tensor_copy(entry[:, :, 1].bitcast(F32), bank[6][0:P, 0:NT]).then_inc(s("entry_ready"), 1)
                v.tensor_scalar(bucket, bank[6][0:P, 0:NT], float(NBK - 1), None, ALU.min).then_inc(s("bucket_ready"), 1)
                v.wait_ge(s("sort_consts"), 6)
                v.wait_ge(s("bucket_ready"), 1)
                v.tensor_tensor(oh, bids[:, :, None].broadcast_to([P, NBK, NT]), bucket[:, None, :].broadcast_to([P, NBK, NT]), ALU.is_equal).then_inc(s("oh_ready"), 1)
                v.wait_ge(s("tot_ready"), NSB)
                flat = tot.rearrange("p b t -> p (b t)")
                v.tensor_tensor_scan(flat, flat, flat, 0.0, ALU.add, ALU.bypass).then_inc(s("sorting"), 1)
                v.wait_ge(s("sorting"), 1)
                v.wait_ge(s("below_ps"), NSB)
                for c in range(NSB):
                    n = min(512, NBK * NT - 512 * c)
                    v.tensor_tensor(flat[:, 512 * c:512 * c + n], flat[:, 512 * c:512 * c + n], bank[c][0:P, 0:n], ALU.add).then_inc(s("sorting"), 1)
                v.wait_ge(s("sorting"), 1 + NSB)
                v.tensor_tensor(tot, tot, oh, ALU.mult).then_inc(s("sorting"), 1)
                v.wait_ge(s("sorting"), 2 + NSB)
                v.tensor_reduce(bucket, tot.rearrange("p b t -> p t b"), AX.X, ALU.add).then_inc(s("sorting"), 1)
                v.wait_ge(s("sorting"), 3 + NSB)
                v.tensor_scalar(rank[:, :], bucket, -1.0, None, ALU.add).then_inc(s("rank_ready"), 1)
                v.wait_ge(s("rank_ready"), 1)
                v.wait_ge(s("att_in"), 32)
                with v.Fori(0, NT // CH) as i:
                    t = i * CH
                    v.wait_ge(s("h_ready"), t + CH)
                    v.wait_ge(s("scored"), t)
                    ht = acc[:, ds(t, CH), :]
                    v.scalar_tensor_tensor(lk, ht, 0.2, ht, ALU.mult, ALU.max).then_inc(s("leaky"), CH)
                    v.wait_ge(s("leaky"), t + CH)
                    t4 = tat.rearrange("p (c s) d -> p c s d", s=2)
                    v.tensor_tensor(t4, lk[:, :, None, :].broadcast_to([P, CH, 2, D]), attb[:, None, :, :].broadcast_to([P, CH, 2, D]), ALU.mult).then_inc(s("tat_ready"), CH)
                    v.wait_ge(s("tat_ready"), t + CH)
                    v.tensor_reduce(wf[:, ds(t, CH), :].rearrange("p t h -> p (t h)"), tat.rearrange("p c (h d) -> p (c h) d", d=GD), AX.X, ALU.add).then_inc(s("scored"), CH)
                v.wait_ge(s("scored"), NT)
                v.tensor_reduce(mx, wf[:, :, :].rearrange("p t h -> p h t"), AX.X, ALU.max).then_inc(s("mx_ready"), 1)
                v.wait_ge(s("mxa_ready"), 1)
                v.tensor_tensor(wf[:, :, :], wf[:, :, :], mxa[:, None, :].broadcast_to([P, NT, 2 * GH]), ALU.subtract).then_inc(s("score_shifted"), 1)
                v.wait_ge(s("w_ready"), 1)
                with steps(v, NT, CH) as t:
                    g4 = acc[:, ds(t, CH), :].rearrange("p t (h d) -> p t h d", d=GD)
                    v.tensor_tensor(g4, g4, wf[:, ds(t, CH), 0:GH].rearrange("p t (h o) -> p t h o", o=1).broadcast_to([P, CH, GH, GD]), ALU.mult).then_inc(s("g_ready"), CH)
                v.wait_ge(s("sorted_t"), 1)
                v.tensor_reduce(mxd[:, 0:1], bank[5][0:NT, 0:P], AX.X, ALU.max).then_inc(s("mxd"), 1)
                v.wait_ge(s("mxd"), 1)
                v.tensor_scalar(mxi[:, 0:1], mxd[:, 0:1], 1.0, float(BLK - 1), ALU.max, ALU.add).then_inc(s("mxd"), 1)
                v.tensor_scalar(mxi[:, 1:2], mxd[:, 0:1], 1.0, -1.0, ALU.max, ALU.add).then_inc(s("mxd"), 1)
                v.wait_ge(s("mxd"), 3)
                v.tensor_scalar(mxi[:, 0:1], mxi[:, 0:1], 2, None, ALU.arith_shift_right).then_inc(s("mxd"), 1)
                v.tensor_scalar(mxi[:, 1:2], mxi[:, 1:2], 6, None, ALU.arith_shift_right).then_inc(s("mxd"), 1)
                v.wait_ge(s("mxd"), 5)
                v.tensor_scalar(mxd[:, 0:1], mxi[:, 0:1], float(WB), None, ALU.min).then_inc(s("mxd"), 1)
                v.tensor_copy(mxd[:, 1:2], mxi[:, 1:2]).then_inc(s("mxd"), 1)
                v.wait_ge(s("mxd"), 7)
                v.tensor_scalar(mxd[:, 3:4], mxd[:, 1:2], float(WB), None, ALU.mult).then_inc(s("mxd"), 1)
                v.wait_ge(s("mxd"), 8)
                v.tensor_tensor(mxd[:, 2:3], mxd[:, 3:4], mxd[:, 0:1], ALU.add).then_inc(s("mxd"), 1)
                v.wait_ge(s("nblk_t"), 1)
                v.tensor_copy(nrow, bank[4][0:1, 0:4 * NT].rearrange("p (a b) -> p a b", b=NT)).then_inc(s("nrow"), 1)
                v.wait_ge(s("nrow"), 1)
                for k, what in ((0, 2), (1, 1)):
                    v.tensor_tensor_scan(nsum[:, k, :], nrow[:, what, :], nrow[:, what, :], 0.0, ALU.add, ALU.bypass).then_inc(s("nrow"), 1)
                v.wait_ge(s("nrow"), 3)
                for k, what in ((0, 2), (1, 1)):
                    v.tensor_tensor(nblk[:, 2 + k, :], nsum[:, k, :], nrow[:, what, :], ALU.subtract).then_inc(s("nrow"), 1)
                v.tensor_copy(nblk[:, 0:2, :], nrow[:, 0:2, :]).then_inc(s("nrow"), 1)

            @block.scalar
            def _(a):
                a.wait_ge(s("var_ready"), 1)
                a.activation(stt[7], stt[3], ACT.Sqrt).then_inc(s("sqrt_ready"), 1)
                a.wait_ge(s("eps_ready"), 2)
                a.activation(stt[8][:, 0:1], shf, ACT.Exp, scale=0.0).then_inc(s("exp_table"), 1)
                a.wait_ge(s("nmr_ready"), 1)

                def normed(k, i, t):
                    at = acc[:, ds(t, 1), :].rearrange("p t d -> p (t d)")
                    a.activation(at, at, ACT.Identity, bias=nmr[:, ds(t, 1)], scale=rstd[:, ds(t, 1)]).then_inc(s("xn"), 1)

                def turned_x(k, i, t):
                    a.wait_ge(s("xt_ps"), t + 1)
                    a.activation(xt[:, ds(t, 1), :, 0:P].rearrange("p t j n -> p (t j) n"),
                                 bank[k][:, 0:256].bitcast(F16).rearrange("p (j n) -> p j n", j=4)[:, :, 0:P], ACT.Copy).then_inc(s("xt_ready"), 1)

                def h_out(k, i, t):
                    a.wait_ge(s("h_ps"), t + 1)
                    a.activation(acc[:, ds(t, 1), :].rearrange("p t d -> p (t d)"), bank[4 + k][0:P, 0:D], ACT.Copy).then_inc(s("h_ready"), 1)
                pipeline(a, [(0, normed), (12, turned_x), (14, h_out)], NT, 4)
                for c in range(NSB):
                    n = min(512, NBK * NT - 512 * c)
                    a.wait_ge(s("tot_ps"), c + 1)
                    a.activation(tot.rearrange("p b t -> p (b t)")[:, 512 * c:512 * c + n], bank[c][0:P, 0:n], ACT.Copy).then_inc(s("tot_ready"), 1)
                a.wait_ge(s("score_shifted"), 1)
                a.activation(wf[:, :, :], wf[:, :, :], ACT.Exp, bias=shf).then_inc(s("w_ready"), 1)
                for c in (0, 1):
                    a.wait_ge(s(f"entries_out{c}"), 16 * NT // 2)
                a.dma_start(perm[:, :, :], by_degree.rearrange("(t p) a -> p t a", p=P)).then_inc(s("perm_in"), 16)
                a.wait_ge(s("perm_in"), 16)
                a.activation(degs, perm[:, :, 1].bitcast(F32), ACT.Copy).then_inc(s("degs_ready"), 1)

            @block.tensor
            def _(pe):
                pe.wait_ge(s("first1f_ready"), 1)
                pe.wait_ge(s("ones_ready"), 2)
                pe.matmul(bank[7][0:P + 1, 0:NS], ones[0:1, 0:P + 1], first1f, start=True, stop=True).then_inc(s("firsts_bcast"), 1)
                pe.wait_ge(s("gw_in"), 16)
                for k in (0, 1):
                    mm = pe.matmul(bank[6][:, 0:D], ones[:, :], gwf[:, k, :], start=(k == 0), stop=(k == 1))
                mm.then_inc(s("colsum"), 1)
                pe.wait_ge(s("identh_ready"), 1)
                pe.wait_ge(s("gw_ready"), 1)

                def transpose_x(k, i, t):
                    pe.wait_ge(s("xa_ready"), t + 1)
                    pe.wait_ge(s("xt_ready"), less(t, 3))
                    for j in range(4):
                        mm = pe.transpose(bank[k][:, 0:256].bitcast(F16).rearrange("p (j n) -> p j n", j=4)[:, j, 0:P],
                                          xa[j // 2][:, ds(t, 1), 128 * (j % 2):128 * (j % 2) + 128].rearrange("p t d -> p (t d)"), identh[0:P, 0:P])
                    mm.then_inc(s("xt_ps"), 1)

                def h_of(k, i, t):
                    pe.wait_ge(s("xt_ready"), t + 1)
                    pe.wait_ge(s("h_ready"), less(t, 3))
                    n = 0
                    for xh, wh in ((0, 0), (0, 1), (1, 0)):
                        for dh in (0, 1):
                            mm = pe.matmul(bank[4 + k][0:P, 0:D], xt[:, ds(t, 1), 2 * xh + dh, 0:P].rearrange("p t n -> p (t n)"), gw[:, wh, dh, :],
                                           start=(n == 0), stop=(n == 5))
                            n += 1
                    mm.then_inc(s("h_ps"), 1)
                pe.wait_ge(s("firsts_ready"), 1)
                pipeline(pe, [(0, transpose_x), (2, h_of)], NT, 4)
                pe.wait_ge(s("h_ready"), NT)
                pe.wait_ge(s("off_ready"), 1)
                pe.wait_ge(s("ident_ready"), 1)
                pe.wait_ge(s("firsts_ready"), 1)
                pe.transpose(bank[7][0:NT, 0:P + 1], offf, ident[0:P + 1, 0:P + 1]).then_inc(s("off_t"), 1)
                pe.wait_ge(s("degT"), 1)
                pe.wait_ge(s("gwc"), 1)
                pe.transpose(bank[6][0:P, 0:NT], degT, ident[0:NT, 0:NT]).then_inc(s("deg_t"), 1)
                pe.wait_ge(s("oh_ready"), 1)
                pe.wait_ge(s("h_ready"), NT)
                ohf = oh.rearrange("p b t -> p (b t)")
                for w, done in ((onesh, "tot_ps"), (trih, "below_ps")):
                    for c in range(NSB):
                        if done == "below_ps":
                            pe.wait_ge(s("tot_ready"), c + 1)
                        n = min(512, NBK * NT - 512 * c)
                        pe.matmul(bank[c][0:P, 0:n], w, ohf[:, 512 * c:512 * c + n], start=True, stop=True).then_inc(s(done), 1)
                pe.wait_ge(s("degs_ready"), 1)
                pe.wait_ge(s("rank_ready"), 1)
                pe.transpose(bank[5][0:NT, 0:P], degs, ident[0:P, 0:P]).then_inc(s("sorted_t"), 1)
                pe.wait_ge(s("mxd"), 9)
                for k in range(4):
                    mm = pe.transpose(bank[4][0:1, k * NT:(k + 1) * NT], mxd[:, k:k + 1], ident[0:NT, 0:NT])
                mm.then_inc(s("nblk_t"), 1)


        next_part()

        with nc.Block() as block:
            @block.sync
            def _(sp):
                def start_sums(k):
                    sp.dma_start(gacc[:, k].rearrange("p a b -> p (a b)"), table[0:1, :].rearrange("o (a b) -> o a b", a=1).broadcast_to([P, BLK, ROWW])).then_inc(s(f"sum_start{k}"), 16)

                def store_sums(t, k, n):
                    sp.wait_ge(s("sum_ready"), t + 1)
                    sp.dma_start(sums[ds(t * P, P), :], gacc[:, k, 0, :]).then_inc(s(f"sum_stored{k}"), 16)
                    sp.wait_ge(s(f"sum_stored{k}"), n * 16 + 16)
                for k in (0, 1):
                    start_sums(k)
                with sp.Fori(0, NT // 2 - 1) as i:
                    for k in (0, 1):
                        store_sums(i * 2 + k, k, i)
                        start_sums(k)
                for k in (0, 1):
                    store_sums(NT - 2 + k, k, NT // 2 - 1)
                sp.wait_ge(s("k_kv"), H * NT)
                tv = table[1:N + 1, :].rearrange("(t p) d -> p t d", p=P)

                def load_own(k, i, c):
                    sp.wait_ge(s("gs_used"), less(c, 1))
                    sp.dma_start(own[k], tv[:, ds(c * LCH, LCH), :]).then_inc(s(f"own_in{k}"), 16)
                pipeline(sp, [(0, load_own)], NT // LCH)
                sp.wait_ge(s("acc_sum"), GH)
                for c in (0, 1):
                    w1s, w2s = ws[c]
                    sp.dma_start(w1s, w1[ds(c, 1)].rearrange("e (a p) f -> p (e a) f", p=128)).then_inc(s(f"first_w_in"), 16)
                    sp.dma_start(w2s, w2[ds(c, 1)].rearrange("e (a p) d -> p (e a) d", p=128)).then_inc(s(f"first_w_in"), 16)

            @block.gpsimd
            def _(pool):
                def index_ops(k, name, n):
                    pool.tensor_scalar(wmask[:, :], kpos[:, :], wrem[k][:, 0:1], None, ALU.is_lt).then_inc(s(name), 1)
                    hold(pool, name, n + 1)
                    pool.tensor_tensor(gidx[k][:, :], widx[k][:, :], wmask[:, :], ALU.mult).then_inc(s(name), 1)
                    hold(pool, name, n + 2)

                def fetch_window(k, name):
                    pool.indirect_dma_start(out=widx[k][:, :], out_offset=None, in_=srcpad.rearrange("(n o) -> n o", o=1),
                                            in_offset=bass.IndirectOffsetOnAxis(ap=woff[k][:, 0:1], axis=0)).then_inc(s(name), 16)

                def fetch_first(t, k):
                    pool.tensor_copy(woff[k][:, :], perm[:, ds(t, 1), 0:1].rearrange("p t a -> p (t a)")).then_inc(s("wcopies"), 1)
                    pool.tensor_copy(wrem[k][:, :], perm[:, ds(t, 1), 1:2].rearrange("p t a -> p (t a)").bitcast(F32)).then_inc(s("wcopies"), 1)
                    hold(pool, "wcopies", t * 2 + 2)
                    fetch_window(k, "widx_in")

                def gathers(k, b, n):
                    for j in range(BLK):
                        hold(pool, f"added{j}", n * 16)
                        pool.indirect_dma_start(out=gacc[:, k, j, :], out_offset=None, in_=table,
                                                in_offset=bass.IndirectOffsetOnAxis(ap=gidx[k][:, BLK * b + j:BLK * b + j + 1], axis=0),
                                                compute_op=ALU.add).then_inc(s(f"added{j}"), 16)

                def finish(k, t):
                    pool.tensor_tensor(gacc[:, k, 0:2, :], gacc[:, k, 0:2, :], gacc[:, k, 2:4, :], ALU.add).then_inc(s("halved"), 1)
                    hold(pool, "halved", t + 1)
                    pool.tensor_tensor(gacc[:, k, 0, :], gacc[:, k, 0, :], gacc[:, k, 1, :], ALU.add).then_inc(s("sum_ready"), 1)

                def tile(t, k, n, first=False, last=False):
                    nb = pool.value_load(nblk[0:1, 0, ds(t, 1)], min_val=1, max_val=WB)
                    more = pool.value_load(nblk[0:1, 1, ds(t, 1)], min_val=0, max_val=E // WIN)
                    before = pool.value_load(nblk[0:1, 2, ds(t, 1)], min_val=0, max_val=E)
                    mbefore = pool.value_load(nblk[0:1, 3, ds(t, 1)], min_val=0, max_val=E)
                    hold(pool, f"sum_start{k}", n * 16 + 16)
                    gathers(k, 0, before)
                    if not first:
                        finish(1 - k, t - 1 if isinstance(t, int) else t + -1)
                    if not last:
                        fetch_first(t + 1, 1 - k)
                    for b in range(1, WB):
                        with pool.If(nb > b):
                            gathers(k, b, before + b)
                    with pool.If(more > 0):
                        with pool.Fori(0, more) as w:
                            for j in range(BLK):
                                hold(pool, f"added{j}", (before + w * WB + WB) * 16)
                            pool.tensor_scalar(woff[k][:, :], woff[k][:, :], float(WIN), float(E), ALU.add, ALU.min).then_inc(s("more_ops"), 1)
                            pool.tensor_scalar(wrem[k][:, :], wrem[k][:, :], float(-WIN), None, ALU.add).then_inc(s("more_ops"), 1)
                            hold(pool, "more_ops", (mbefore + w) * 4 + 2)
                            fetch_window(k, "more_in")
                            hold(pool, "more_in", (mbefore + w) * 16 + 16)
                            index_ops(k, "more_ops", (mbefore + w) * 4 + 2)
                            for b in range(WB):
                                gathers(k, b, before + (w * WB + (WB + b)))
                    if not last:
                        hold(pool, "widx_in", t * 16 + 32)
                        index_ops(1 - k, "index_ops", t * 2 + 2)
                    else:
                        for j in range(BLK):
                            hold(pool, f"added{j}", (before + nb + more * WB) * 16)
                        finish(k, t)

                fetch_first(0, 0)
                hold(pool, "widx_in", 16)
                index_ops(0, "index_ops", 0)
                tile(0, 0, 0, first=True)
                with pool.Fori(0, NT // 2 - 1) as i:
                    tile(i * 2 + 1, 1, i)
                    tile(i * 2 + 2, 0, i + 1)
                tile(NT - 1, 1, NT // 2 - 1, last=True)

                for k in (0, 1):
                    pool.wait_ge(s(f"sum_stored{k}"), 16 * (NT // 2))
                pool.wait_ge(s("k_kv"), H * NT)

                def sums_by_node(k, i, c):
                    hold(pool, "gs_used", less(c, 1))
                    pool.tensor_copy(gslot[k], rank[:, ds(c * LCH, LCH)]).then_inc(s("gslot"), 1)
                    hold(pool, "gslot", c + 1)
                    for j in range(LCH):
                        pool.indirect_dma_start(out=gs[k][:, j, :], out_offset=None, in_=sums,
                                                in_offset=bass.IndirectOffsetOnAxis(ap=gslot[k][:, j:j + 1], axis=0)).then_inc(s(f"gs_in{k}"), 16)
                pool.wait_ge(s("stats2"), NT)
                pipeline(pool, [(0, sums_by_node)], NT // LCH)
                pool.memset(upper, 1.0).then_inc(s("rt"), 1)
                pool.iota(downi, pattern=[[-1, NE]], base=NE, channel_multiplier=0).then_inc(s("rt"), 1)
                pool.iota(node, pattern=[[P, NT]], base=NE * CB, channel_multiplier=1).then_inc(s("rt"), 1)
                pool.wait_ge(s("rt"), 3)
                pool.affine_select(out=upper, in_=upper, compare_op=ALU.is_ge, fill=0.0, base=0, pattern=[[1, P]], channel_multiplier=-1).then_inc(s("rt"), 1)
                pool.tensor_copy(down, downi).then_inc(s("rt"), 1)
                pool.tensor_copy(rdump, node).then_inc(s("rt"), 1)
                pool.wait_ge(s("zpart"), 1)
                pool.partition_all_reduce(zall, zpart, P, bass.bass_isa.ReduceOp.add).then_inc(s("zall"), 1)
                pool.wait_ge(s("first_w_in"), 64)
                for c in (0, 1):
                    for m in (0, 1):
                        split_weights(pool, c, m, "first_w", 2 * c + m)

            @block.vector
            def _(v):
                with v.Fori(0, H) as h:
                    for m in range(3):
                        v.wait_ge(s("wsum_ps"), h * 3 + (m + 1))
                        v.scalar_tensor_tensor(wraw[:, m], bank[m][:, None, 0:D].broadcast_to([128, 2, D]), -1.0 / D, wraw[:, m], ALU.mult, ALU.add).then_inc(s("wcen"), 1)
                    v.wait_ge(s("wc_out"), h * 48)
                    v.wait_ge(s("wcen"), h * 3 + 3)
                    for m in (0, 1):
                        v.tensor_scalar(wc[m][:, 0, :, 0:D], wraw[:, m], 0.25, None, ALU.mult).then_inc(s("whi"), 1)
                    v.wait_ge(s("whi"), h * 4 + 2)
                    for m in (0, 1):
                        v.scalar_tensor_tensor(wc[m][:, 1, :, 0:D], wraw[:, m], 0.25, wc[m][:, 0, :, 0:D], ALU.mult, ALU.subtract).then_inc(s("wlo"), 1)
                    for m in (0, 1):
                        v.wait_ge(s("prod_ps"), h * 3 + (m + 1))
                        v.tensor_scalar(wc[m][:, 0, :, D:2 * D], bank[4 + m][:, :].rearrange("p (a b) -> p a b", a=2), 0.25, None, ALU.mult).then_inc(s("whi"), 1)
                    v.wait_ge(s("whi"), h * 4 + 4)
                    v.wait_ge(s("wlo"), h * 2 + 2)
                    for m in (0, 1):
                        v.scalar_tensor_tensor(wc[m][:, 1, :, D:2 * D], bank[4 + m][:, :].rearrange("p (a b) -> p a b", a=2), 0.25, wc[m][:, 0, :, D:2 * D], ALU.mult, ALU.subtract).then_inc(s("prod_used"), 1)
                    v.wait_ge(s("prod_ps"), h * 3 + 3)
                    v.tensor_copy(bmat, bank[6][:, :].rearrange("p (a b) -> p a b", a=2)).then_inc(s("prod_used"), 1)
                v.memset(zero, 0.0).then_inc(s("zero_ready"), 1)
                v.wait_ge(s("bo_in"), 16)
                v.tensor_copy(acc[:, :, :], brow_bo[:, None, :].broadcast_to([P, NT, D])).then_inc(s("acc_ready"), 1)
                v.wait_ge(s("acc_ready"), 1)
                with v.Fori(0, H) as h:
                    def negate(ph_):
                        def step(k, i, t):
                            v.wait_ge(s(f"{ph_}_sq"), h * NT + (t + 1))
                            v.tensor_scalar(nsq[k], sq[k], -1.0, LOG16, ALU.mult, ALU.subtract).then_inc(s(f"{ph_}_nsq"), 1)
                        return step

                    def k_hi(k, i, t):
                        v.wait_ge(s("k_exp"), h * NT + (t + 1))
                        v.wait_ge(s("k_kv"), h * NT + less(t, 3))
                        v.tensor_scalar(ph[k][:, 0, :], ex[k], PHI_EPS, None, ALU.add).then_inc(s("k_hi"), 1)

                    def k_lo(k, i, t):
                        v.wait_ge(s("k_hi"), h * NT + (t + 1))
                        v.scalar_tensor_tensor(ph[k][:, 1, :], ex[k], PHI_EPS, ph[k][:, 0, :], ALU.add, ALU.subtract).then_inc(s("k_ph"), 1)

                    pipeline(v, [(2, k_hi), (0, negate("k")), (2, k_lo)], NT, 4)
                    v.wait_ge(s("kvo_ps"), h + 1)
                    v.wait_ge(s("q_att"), h * NT)
                    kvp = bank[5][:, :].rearrange("p (a b) -> p a b", a=2)
                    v.tensor_copy(kvo[:, 0, :, 0:D], kvp).then_inc(s("kvo_hi"), 1)
                    v.tensor_copy(kvo[:, 0, :, D:D + 1], kvs[:, :, D:D + 1]).then_inc(s("kvo_hi"), 1)
                    v.wait_ge(s("kvo_hi"), h * 2 + 2)
                    v.tensor_tensor(kvo[:, 1, :, 0:D], kvp, kvo[:, 0, :, 0:D], ALU.subtract).then_inc(s("kvo_lo"), 1)
                    v.wait_ge(s("kvo_lo"), h + 1)
                    v.tensor_tensor(kvo[:, 1, :, D:D + 1], kvs[:, :, D:D + 1], kvo[:, 0, :, D:D + 1], ALU.subtract).then_inc(s("kvo_ready"), 1)

                    def turned(k):
                        return bank[4 + k % 2][:, 0:256].rearrange("p (a b) -> p a b", a=2)[:, :, 0:P]

                    def q_hi(k, i, t):
                        v.wait_ge(s("q_turned"), h * NT + (t + 1))
                        v.wait_ge(s("q_att"), h * NT + less(t, 3))
                        v.tensor_scalar(qt[k][:, 0, :, 0:P], turned(k), PHI_EPS, None, ALU.add).then_inc(s("q_hi"), 1)

                    def q_lo(k, i, t):
                        v.wait_ge(s("q_hi"), h * NT + (t + 1))
                        v.scalar_tensor_tensor(qt[k][:, 1, :, 0:P], turned(k), PHI_EPS, qt[k][:, 0, :, 0:P], ALU.add, ALU.subtract).then_inc(s("q_ph"), 1)

                    def over_z(k, i, t):
                        v.wait_ge(s("q_att"), h * NT + (t + 1))
                        v.wait_ge(s("q_acc"), h * NT + less(t, 3))
                        v.reciprocal(rz[k], bank[6 + k % 2][0:P, D:D + 1]).then_inc(s("q_rz"), 1)

                    def add_head(k, i, t):
                        v.wait_ge(s("q_rz"), h * NT + (t + 1))
                        at = acc[:, ds(t, 1), :].rearrange("p t d -> p (t d)")
                        v.scalar_tensor_tensor(at, bank[6 + k % 2][0:P, 0:D], rz[k], at, ALU.mult, ALU.add).then_inc(s("q_acc"), 1)

                    pipeline(v, [(3, q_hi), (0, negate("q")), (5, over_z), (3, q_lo), (5, add_head)], NT, 4)
                    v.wait_ge(s("q_acc"), (h + 1) * NT)


                def per_row(col, t, n=CH):
                    return col[:, ds(t, n)].rearrange("p (t o) -> p t o", o=1).broadcast_to([P, n, D])

                def norm_stats(n, eps_):
                    me, ve, mo, vo = tst[:, :, 1], tst[:, :, 2], tst[:, :, 4], tst[:, :, 5]
                    q, dm, vs, ve_, va, r0, r2, r3 = tln
                    ln = s("ln")
                    b = 10 * n
                    v.tensor_tensor(q, me, mo, ALU.add).then_inc(ln, 1)
                    v.tensor_tensor(dm, me, mo, ALU.subtract).then_inc(ln, 1)
                    v.tensor_tensor(vs, ve, vo, ALU.add).then_inc(ln, 1)
                    v.wait_ge(ln, b + 3)
                    v.tensor_scalar(mean[:, :], q, 0.5, None, ALU.mult).then_inc(ln, 1)
                    v.scalar_tensor_tensor(r0, dm, 0.25, dm, ALU.mult, ALU.mult).then_inc(ln, 1)
                    v.wait_ge(ln, b + 5)
                    v.scalar_tensor_tensor(va, vs, 1.0 / D, r0, ALU.mult, ALU.add).then_inc(ln, 1)
                    v.wait_ge(ln, b + 6)
                    v.tensor_scalar(ve_, va, eps_, None, ALU.add).then_inc(s("var_ready"), 1)
                    v.wait_ge(s("sqrt_ready"), n + 1)
                    v.reciprocal(r2, r3).then_inc(ln, 1)
                    v.wait_ge(ln, b + 7)
                    v.tensor_tensor(q, r2, r2, ALU.mult).then_inc(ln, 1)
                    v.wait_ge(ln, b + 8)
                    v.scalar_tensor_tensor(dm, q, -0.5, ve_, ALU.mult, ALU.mult).then_inc(ln, 1)
                    v.wait_ge(ln, b + 9)
                    v.scalar_tensor_tensor(rstd[:, :], dm, 1.5, r2, ALU.add, ALU.mult).then_inc(ln, 1)
                    v.wait_ge(ln, b + 10)
                    v.scalar_tensor_tensor(nmr[:, :], mean[:, :], -1.0, rstd[:, :], ALU.mult, ALU.mult).then_inc(s("nmr_ready"), 1)

                def stats_of(tile, done):
                    v.bn_stats(tst[:, ds(tile, 1), :].rearrange("p t a -> p (t a)"), acc[:, ds(tile, 1), :].rearrange("p t d -> p (t d)")).then_inc(s(done), 1)

                v.scalar_tensor_tensor(nmr[:, :], mean[:, :], -1.0, rstd[:, :], ALU.mult, ALU.mult).then_inc(s("nmr_ready"), 1)

                def add_xn(k, i, c):
                    v.wait_ge(s("xn_again"), c * CH + CH)
                    at = acc[:, ds(c * CH, CH), :]
                    v.tensor_tensor(at, at, xr[k], ALU.add).then_inc(s("resid"), 1)
                    v.wait_ge(s("resid"), c + 1)
                    for j in range(CH):
                        stats_of(c * CH + j, "stats1")
                pipeline(v, [(0, add_xn)], NT // CH, 3)
                v.wait_ge(s("stats1"), NT)
                norm_stats(0, MIX_EPS)
                v.wait_ge(s("tail_in"), 16 * 11)

                def out1(k, i, g):
                    v.wait_ge(s("out1_norm"), g * 2 + 2)
                    at = acc[:, ds(g * 2, 2), :]
                    v.tensor_tensor(at, at, g1b[:, None, :].broadcast_to([P, 2, D]), ALU.mult).then_inc(s("out1_g"), 1)
                    v.wait_ge(s("out1_g"), g + 1)
                    v.wait_ge(s("out1_turned"), less(g, 3))
                    v.tensor_tensor(o1[k], at, beta1b[:, None, :].broadcast_to([P, 2, D]), ALU.add).then_inc(s("out1_ready"), 1)

                def add_ffn(k, i, g):
                    v.wait_ge(s("ffn_ps"), g + 1)
                    at = acc[:, ds(g * 2, 2), :]
                    v.tensor_tensor(at, o1[k], bank[4 + k % 2][0:P, :].rearrange("p (a b) -> p a b", a=2), ALU.add).then_inc(s("ffn_added"), 1)
                    v.wait_ge(s("ffn_added"), g + 1)
                    v.tensor_tensor(at, at, bias2b[:, None, :].broadcast_to([P, 2, D]), ALU.add).then_inc(s("ffn_bias"), 1)

                def stats2(k, i, g):
                    v.wait_ge(s("ffn_bias"), g + 1)
                    for j in (0, 1):
                        stats_of(g * 2 + j, "stats2")
                pipeline(v, [(0, out1), (3, add_ffn), (4, stats2)], NT // 2, 4)
                v.wait_ge(s("stats2"), NT)
                norm_stats(1, MIX_EPS)
                v.tensor_tensor(beta2b, beta2b, gnnb, ALU.add).then_inc(s("beta2_gnn"), 1)
                v.wait_ge(s("beta2_gnn"), 1)
                with v.Fori(0, NT // CH // 2) as i:
                    for k in (0, 1):
                        t, c = i * 2 * CH + k * CH, i * 2 + k
                        at = acc[:, ds(t, CH), :]
                        v.wait_ge(s("mix_norm"), t + CH)
                        v.tensor_tensor(at, at, g2b[:, None, :].broadcast_to([P, CH, D]), ALU.mult).then_inc(s("mix_g"), 1)
                        v.wait_ge(s(f"xc2_in{k}"), i * 16 + 16)
                        v.tensor_tensor(xc[k], xc[k], beta2b[:, None, :].broadcast_to([P, CH, D]), ALU.add).then_inc(s("mix_g"), 1)
                        v.wait_ge(s("mix_g"), c * 2 + 2)
                        v.tensor_tensor(at, at, xc[k], ALU.add).then_inc(s(f"xc2_used{k}"), 1)
                for k in (0, 1):
                    v.wait_ge(s(f"xc2_used{k}"), NT // CH // 2)
                f4 = wf[:, :, GH:2 * GH]

                def scale_sums(k, i, c):
                    t = c * LCH
                    v.wait_ge(s(f"own_in{k}"), i * 16 + 16)
                    v.wait_ge(s(f"gs_in{k}"), i * 16 * LCH + 16 * LCH)
                    v.tensor_tensor(gs[k], gs[k], own[k], ALU.add).then_inc(s("own_added"), 1)
                    v.wait_ge(s("own_added"), c + 1)
                    v.tensor_tensor(zw[:, ds(t, LCH), :], gs[k][:, :, D:ROWW], f4[:, ds(t, LCH), :], ALU.mult).then_inc(s("scaled"), 1)
                    v.tensor_tensor(scaled[:, ds(t, LCH), :].rearrange("p t (h d) -> p t h d", d=GD), gs[k][:, :, 0:D].rearrange("p t (h d) -> p t h d", d=GD),
                                    f4[:, ds(t, LCH), :, None].broadcast_to([P, LCH, GH, GD]), ALU.mult).then_inc(s("scaled"), 1)
                    v.wait_ge(s("scaled"), c * 2 + 2)
                    v.sem_inc(s("gs_used"), 1)
                pipeline(v, [(0, scale_sums)], NT // LCH)
                v.tensor_reduce(zpart, zw.rearrange("p t h -> p h t"), AX.X, ALU.add).then_inc(s("zpart"), 1)
                v.wait_ge(s("zpart"), 1)
                v.wait_ge(s("zall"), 1)
                v.reciprocal(zpart, zall).then_inc(s("z"), 1)
                v.wait_ge(s("z"), 1)
                for h in range(GH):
                    v.scalar_tensor_tensor(acc[:, :, GD * h:GD * h + GD], scaled[:, :, GD * h:GD * h + GD], zpart[:, h:h + 1], acc[:, :, GD * h:GD * h + GD], ALU.mult, ALU.add).then_inc(s("acc_sum"), 1)
                v.wait_ge(s("acc_sum"), GH)
                with v.Fori(0, NT) as t:
                    stats_of(t, "acc_new")
                v.wait_ge(s("acc_new"), NT)
                norm_stats(2, LN_EPS)

                def gate_norm(k, i, c):
                    v.wait_ge(s("xf_turned"), less(c, 1) * CH)
                    v.tensor_tensor(xfs[k], acc[:, ds(c * CH, CH), :], per_row(mean, c * CH), ALU.subtract).then_inc(s("xf_centred"), 1)
                    v.wait_ge(s("xf_centred"), c + 1)
                    v.tensor_tensor(xfs[k], xfs[k], per_row(rstd, c * CH), ALU.mult).then_inc(s("xf_ready"), 1)

                def logits(k, i, c):
                    v.wait_ge(s("lg_ps"), c * CH + CH)
                    v.tensor_tensor(lg[:, ds(c * CH, CH), :], bank[5 + k][0:P, 0:CH * NE].rearrange("p (t e) -> p t e", e=NE),
                                    gateb[:, None, :].broadcast_to([P, CH, NE]), ALU.add).then_inc(s("logits"), 1)
                pipeline(v, [(0, gate_norm), (2, logits)], NT // CH)
                v.wait_ge(s("logits"), NT // CH)
                v.wait_ge(s("rt"), 6)

                def over_experts(col):
                    return col[:, :, None].broadcast_to([P, NT, NE])
                v.tensor_reduce(rmax, lg, AX.X, ALU.max).then_inc(s("route"), 1)
                v.wait_ge(s("route"), 1)
                v.tensor_tensor(lg, lg, over_experts(rmax), ALU.subtract).then_inc(s("route"), 1)
                v.wait_ge(s("rexp"), 1)
                v.tensor_reduce(rsum, rex, AX.X, ALU.add).then_inc(s("route"), 1)
                v.tensor_reduce(rmax, rex, AX.X, ALU.max).then_inc(s("route"), 1)
                v.wait_ge(s("route"), 4)
                v.reciprocal(rinv, rsum).then_inc(s("route"), 1)
                v.tensor_tensor(rex, rex, over_experts(rmax), ALU.is_equal).then_inc(s("route"), 1)
                v.wait_ge(s("route"), 6)
                v.tensor_tensor(rex, rex, down[:, None, :].broadcast_to([P, NT, NE]), ALU.mult).then_inc(s("route"), 1)
                v.tensor_tensor(rinv, rinv, rmax, ALU.mult).then_inc(s("route"), 1)
                v.wait_ge(s("route"), 8)
                v.tensor_reduce(ridx, rex, AX.X, ALU.max).then_inc(s("route"), 1)
                v.wait_ge(s("route"), 9)
                v.tensor_tensor(roh, rex, over_experts(ridx), ALU.is_equal).then_inc(s("onehot_ready"), 1)
                v.wait_ge(s("counts_ps"), 1)
                v.tensor_copy(rtot, bank[1][0:P, 0:NT * NE].rearrange("p (t e) -> p t e", e=NE)).then_inc(s("route"), 1)
                v.wait_ge(s("route"), 10)
                for e in range(NE):
                    v.tensor_tensor_scan(rscan[:, :, e], rtot[:, :, e], rtot[:, :, e], 0.0, ALU.add, ALU.bypass).then_inc(s("route"), 1)
                v.wait_ge(s("route"), 18)
                for m in (0, 1):
                    v.tensor_scalar(rows_of[:, :, m], rscan[0:1, NT - 1, :], float(-4 * P * m), None, ALU.add).then_inc(s("rows_ready"), 1)
                v.wait_ge(s("rows_ready"), 2)
                v.tensor_tensor(rscan, rscan, rtot, ALU.subtract).then_inc(s("route"), 1)
                v.wait_ge(s("route"), 19)
                v.tensor_tensor(rscan, rscan, bank[0][0:P, 0:NT * NE].rearrange("p (t e) -> p t e", e=NE), ALU.add).then_inc(s("route"), 1)
                v.wait_ge(s("route"), 20)
                v.tensor_tensor(rscan, rscan, roh, ALU.mult).then_inc(s("route"), 1)
                v.wait_ge(s("route"), 21)
                v.tensor_reduce(rpos, rscan, AX.X, ALU.add).then_inc(s("route"), 1)
                v.wait_ge(s("route"), 22)
                v.tensor_scalar(rkept, rpos, float(CAP) + 0.5, None, ALU.is_lt).then_inc(s("route"), 1)
                v.tensor_scalar(rpos, rpos, float(CAP), -1.0, ALU.min, ALU.add).then_inc(s("route"), 1)
                v.tensor_scalar(rtmp, ridx, -float(CB), float(NE * CB), ALU.mult, ALU.add).then_inc(s("route"), 1)
                v.wait_ge(s("route"), 25)
                v.tensor_tensor(rtmp, rtmp, rpos, ALU.add).then_inc(s("route"), 1)
                v.tensor_tensor(pk, rinv, rkept, ALU.mult).then_inc(s("route"), 1)
                v.wait_ge(s("route"), 27)
                v.tensor_copy(slot_in, rtmp).then_inc(s("route"), 1)
                v.tensor_tensor(rtmp, rtmp, rdump, ALU.subtract).then_inc(s("route"), 1)
                v.wait_ge(s("route"), 29)
                v.tensor_tensor(rtmp, rtmp, rkept, ALU.mult).then_inc(s("route"), 1)
                v.wait_ge(s("route"), 30)
                v.tensor_tensor(slot_out, rtmp, rdump, ALU.add).then_inc(s("slots_ready"), 1)
                v.tensor_scalar(above, rows_of, float(P) + 0.5, 1.0, ALU.is_gt, ALU.add).then_inc(s("levels"), 1)
                v.wait_ge(s("levels"), 1)
                v.scalar_tensor_tensor(above, rows_of, 2.0 * P + 0.5, above, ALU.is_gt, ALU.add).then_inc(s("levels"), 1)
                v.wait_ge(s("levels"), 2)
                v.scalar_tensor_tensor(used, rows_of, 3.0 * P + 0.5, above, ALU.is_gt, ALU.add).then_inc(s("levels"), 1)

            @block.scalar
            def _(a):
                a.activation(spare[:, 0:1], ident[0:P, 0:1], ACT.Exp)
                a.dma_start(brow_bo, bo.rearrange("(o d) -> o d", o=1).broadcast_to([P, D])).then_inc(s("bo_in"), 16)
                a.dma_start(projr, proj.rearrange("(a p) n -> p a n", p=128)).then_inc(s("proj_in"), 16)
                a.wait_ge(s("projt_ps"), 1)
                a.activation(projt, bank[0][:, :].rearrange("p (a b) -> p a b", a=2), ACT.Copy).then_inc(s("projt_ready"), 1)
                with a.Fori(0, H) as h:
                    a.wait_ge(s("prod_ps"), h * 3)
                    for m, w in enumerate((Wq, Wk, Wv)):
                        a.dma_start(wraw[:, m], w[:, ds(h, 1), :].rearrange("(a p) h k -> p a (h k)", p=128)).then_inc(s("w_in"), 16)
                    a.dma_start(wo, Wo[ds(h, 1)].rearrange("h (a p) d -> p (h a) d", p=128)).then_inc(s("w_in"), 16)
                    for m, b in enumerate((bq, bk, bv)):
                        a.dma_start(brow[0:1, m, :], b[ds(h, 1), :]).then_inc(s("w_in"), 16)
                    for m in range(3):
                        a.wait_ge(s("wt_ps"), h * 3 + (m + 1))
                        a.activation(wt[:, m], bank[3][:, :].rearrange("p (a b) -> p a b", a=2), ACT.Copy).then_inc(s("wt_ready"), 1)
                    a.wait_ge(s("prod_used"), h * 3 + 3)
                    for m in (0, 1):
                        a.dma_start(wcat[ds(h, 1), m].rearrange("h p n -> p (h n)"), wc[m].rearrange("p a b c -> p (a b c)")).then_inc(s("wc_out"), 16)
                    a.dma_start(bdram[ds(h, 1)].rearrange("h p n -> p (h n)"), bmat.rearrange("p a b -> p (a b)")).then_inc(s("wc_out"), 16)
                a.wait_ge(s("wc_out"), H * 48)
                def load_head(m, h, name):
                    a.dma_start(wc[m].rearrange("p a b c -> p (a b c)"), wcat[ds(h, 1), m].rearrange("h p n -> p (h n)")).then_inc(s(name), 16)
                with a.Fori(0, H) as h:
                    a.wait_ge(s("k_u"), h * NT)
                    load_head(1, h, "wk_in")
                    a.wait_ge(s("kvo_ps"), h)
                    a.dma_start(bmat.rearrange("p a b -> p (a b)"), bdram[ds(h, 1)].rearrange("h p n -> p (h n)")).then_inc(s("bmat_in"), 16)
                    a.wait_ge(s("q_u"), h * NT)
                    load_head(0, h, "wq_in")

                    def square(ph_):
                        def step(k, i, t):
                            a.wait_ge(s(f"{ph_}_u"), h * NT + (t + 1))
                            a.wait_ge(s(f"{ph_}_exp"), h * NT + less(t, 3))
                            a.activation(sqj[k], fbank[ph_][k][0:P, 0:D], ACT.Square, scale=0.5 ** 0.5, accum_out=sq[k]).then_inc(s(f"{ph_}_sq"), 1)
                        return step

                    def expo(ph_, used):
                        def step(k, i, t):
                            a.wait_ge(s(f"{ph_}_nsq"), h * NT + (t + 1))
                            a.wait_ge(s(used), h * NT + less(t, 3))
                            a.activation(ex[k], fbank[ph_][k][0:P, D:2 * D], ACT.Exp, bias=nsq[k]).then_inc(s(f"{ph_}_exp"), 1)
                        return step

                    a.wait_ge(s("q_turned"), h * NT)
                    pipeline(a, [(0, square("k")), (1, expo("k", "k_ph"))], NT, 4)
                    a.wait_ge(s("k_kv"), (h + 1) * NT)
                    for m in (0, 1):
                        ins = a.activation(kvs[:, m, 0:D + 1], bank[2 + m][:, 0:D + 1], ACT.Copy)
                    ins.then_inc(s("kvs_ready"), 1)
                    a.wait_ge(s("kvt_ps"), h + 1)
                    a.activation(kvt, bank[4][:, :].rearrange("p (a b) -> p a b", a=2), ACT.Copy).then_inc(s("kvt_ready"), 1)
                    a.wait_ge(s("k_ph"), (h + 1) * NT)
                    pipeline(a, [(0, square("q")), (1, expo("q", "q_turned"))], NT, 4)


                a.wait_ge(s("q_acc"), H * NT)
                for to, fro in ((g1b, g1), (beta1b, beta1), (g2b, g2), (beta2b, beta2), (bias2b, bias2), (gnnb, gb), (gateb, gate_b)):
                    a.dma_start(to, fro.rearrange("(o d) -> o d", o=1).broadcast_to([P, to.shape[-1]])).then_inc(s("tail_in"), 16)
                for to, fro in ((W1s, W1), (W2s, W2), (gate, gate_w)):
                    a.dma_start(to, fro.rearrange("(a p) n -> p a n", p=128)).then_inc(s("tail_in"), 16)
                a.dma_start(b1r, bias1.rearrange("(a p) -> a p", p=128)).then_inc(s("tail_in"), 16)

                def load_x(k, i, c):
                    a.wait_ge(s("resid"), less(c, 2))
                    a.dma_start(xr[k], xv[:, ds(c * CH, CH), :]).then_inc(s(f"xr_in{k}"), 16)

                def again(k, i, c):
                    a.wait_ge(s(f"xr_in{k}"), i * 16 + 16)
                    for j in range(CH):
                        t = c * CH + j
                        a.activation(xr[k][:, j, :], xr[k][:, j, :], ACT.Identity, bias=nmr[:, ds(t, 1)], scale=rstd[:, ds(t, 1)]).then_inc(s("xn_again"), 1)
                a.wait_ge(s("nmr_ready"), 1)
                pipeline(a, [(0, load_x), (1, again)], NT // CH, 3)

                def root(n):
                    a.wait_ge(s("var_ready"), n + 1)
                    a.activation(tln[7], tln[3], ACT.Sqrt).then_inc(s("sqrt_ready"), 1)
                root(0)
                a.wait_ge(s("bias1_ps"), 1)
                a.activation(bias1t, bank[6][:, 0:2], ACT.Copy).then_inc(s("bias1_ready"), 1)
                a.activation(spare[:, 1:2], ident[0:P, 0:1], ACT.Relu)

                def out1_norm(k, i, g):
                    for j in (0, 1):
                        at = acc[:, ds(g * 2 + j, 1), :].rearrange("p t d -> p (t d)")
                        a.activation(at, at, ACT.Identity, bias=nmr[:, ds(g * 2 + j, 1)], scale=rstd[:, ds(g * 2 + j, 1)]).then_inc(s("out1_norm"), 1)

                def out1_t(k, i, g):
                    a.wait_ge(s("out1_turned"), g + 1)
                    a.wait_ge(s("hidden_ps"), less(g, 1))
                    a.activation(ot[k % 2], bank[k % 2][:, 0:4 * P].rearrange("p (a b) -> p a b", a=2), ACT.Copy).then_inc(s("ot_ready"), 1)

                def relu(k, i, g):
                    a.wait_ge(s("hidden_ps"), g + 1)
                    a.wait_ge(s("ffn_ps"), less(g, 1))
                    for fh in (0, 1):
                        a.activation(ht[k % 2][:, fh, :], bank[2 + k % 2][:, fh * 2 * P:fh * 2 * P + 2 * P], ACT.Relu, bias=bias1t[:, fh:fh + 1]).then_inc(s("ht_ready"), 1)
                a.wait_ge(s("bias1_ready"), 1)
                a.wait_ge(s("nmr_ready"), 2)
                pipeline(a, [(0, out1_norm), (2, out1_t), (3, relu)], NT // 2, 4)
                root(1)
                a.wait_ge(s("nmr_ready"), 3)
                with a.Fori(0, NT // CH // 2) as i:
                    for k in (0, 1):
                        a.wait_ge(s(f"xc2_used{k}"), i)
                        a.dma_start(xc[k], xv[:, ds(i * 2 * CH + k * CH, CH), :]).then_inc(s(f"xc2_in{k}"), 16)
                        for j in range(CH):
                            t = i * 2 * CH + (k * CH + j)
                            at = acc[:, ds(t, 1), :].rearrange("p t d -> p (t d)")
                            a.activation(at, at, ACT.Identity, bias=nmr[:, ds(t, 1)], scale=rstd[:, ds(t, 1)]).then_inc(s("mix_norm"), 1)
                root(2)

                def xf_t(k, i, c):
                    for j in range(CH):
                        a.wait_ge(s("xf_turned"), c * CH + (j + 1))
                        a.wait_ge(s("lg_ps"), less(c, 1) * CH + (j + 1) if not isinstance(c, int) or c > 0 else 0)
                        a.activation(xft[j], bank[j][:, 0:2 * P].rearrange("p (a b) -> p a b", a=2), ACT.Copy).then_inc(s("xft_ready"), 1)
                pipeline(a, [(0, xf_t)], NT // CH)
                a.wait_ge(s("route"), 2)
                a.activation(rex, lg, ACT.Exp).then_inc(s("rexp"), 1)

            @block.tensor
            def _(pe):
                for m in (0, 1):
                    pe.wait_ge(s("proj_in"), 16)
                    for kh in (0, 1):
                        mm = pe.transpose(bank[0][:, kh * M + m * 128:kh * M + m * 128 + 128], projr[:, m, kh * 128:kh * 128 + 128], ident[:, :])
                mm.then_inc(s("projt_ps"), 1)
                pe.wait_ge(s("projt_ready"), 1)
                with pe.Fori(0, H) as h:
                    pe.wait_ge(s("w_in"), h * 112 + 112)
                    for m in range(3):
                        pe.wait_ge(s("wcen"), h * 3)
                        for dh in (0, 1):
                            pe.matmul(bank[m][:, 0:D], ones[:, :], wraw[:, m, dh, :], start=(dh == 0), stop=False)
                        pe.matmul(bank[m][:, 0:D], nones[0:1, :], brow[0:1, m, :], start=False, stop=True).then_inc(s("wsum_ps"), 1)
                    for m in range(3):
                        pe.wait_ge(s("wcen"), h * 3 + (m + 1))
                        pe.wait_ge(s("wt_ready"), h * 3 + m)
                        for kh in (0, 1):
                            for dh in (0, 1):
                                mm = pe.transpose(bank[3][:, kh * D + dh * 128:kh * D + dh * 128 + 128], wraw[:, m, dh, kh * 128:kh * 128 + 128], ident[:, :])
                        mm.then_inc(s("wt_ps"), 1)
                    for m in range(3):
                        pe.wait_ge(s("wt_ready"), h * 3 + (m + 1))
                        pe.wait_ge(s("prod_used"), h * 3)
                        rhs = projt if m < 2 else wo
                        for dh in (0, 1):
                            for kh in (0, 1):
                                mm = pe.matmul(bank[4 + m][:, dh * D:dh * D + D], wt[:, m, kh, dh * 128:dh * 128 + 128], rhs[:, kh, :], start=(kh == 0), stop=(kh == 1))
                        mm.then_inc(s("prod_ps"), 1)
                pe.wait_ge(s("prod_used"), H * 3)
                with pe.Fori(0, H) as h:
                    def features(w, ph_):
                        def step(k, i, t):
                            pe.wait_ge(s(f"{ph_}_exp"), h * NT + less(t, 3))
                            if ph_ == "k" and isinstance(t, int) and t == 2:
                                pe.wait_ge(s("q_acc"), h * NT)
                            n = 0
                            for xh, wh in ((0, 0), (0, 1), (1, 0)):
                                for dh in (0, 1):
                                    mm = pe.matmul(fbank[ph_][k][0:P, :], xt[:, ds(t, 1), 2 * xh + dh, 0:P].rearrange("p t n -> p (t n)"), w[:, wh, dh, :], start=(n == 0), stop=(n == 5))
                                    n += 1
                            mm.then_inc(s(f"{ph_}_u"), 1)
                        return step

                    def kv(k, i, t):
                        pe.wait_ge(s("k_ph"), h * NT + (t + 1))
                        for m in (0, 1):
                            for a, b in ((0, 0), (0, 1), (1, 0)):
                                mm = pe.matmul(bank[2 + m][:, 0:D + 1], ph[k][:, a, m * 128:m * 128 + 128], xa[b][:, ds(t, 1), 0:D + 1].rearrange("p t n -> p (t n)"),
                                               start=False, stop=False, skip_group_check=True)
                        mm.then_inc(s("k_kv"), 1)

                    pe.wait_ge(s("wk_in"), h * 16 + 16)
                    pe.wait_ge(s("zero_ready"), 1)
                    pe.wait_ge(s("kvs_ready"), h)
                    pe.wait_ge(s("q_exp"), h * NT)
                    for m in (0, 1):
                        pe.matmul(bank[2 + m][:, 0:D + 1], zero, xa[0][:, 0, 0:D + 1], start=True, stop=False, skip_group_check=True)
                    pipeline(pe, [(0, features(wc[1], "k")), (3, kv)], NT, 4)
                    pe.wait_ge(s("q_ph"), h * NT)
                    pe.wait_ge(s("kvs_ready"), h + 1)
                    for dh in (0, 1):
                        for m in (0, 1):
                            mm = pe.transpose(bank[4][:, dh * M + m * 128:dh * M + m * 128 + 128], kvs[:, m, dh * 128:dh * 128 + 128], ident[:, :])
                    mm.then_inc(s("kvt_ps"), 1)
                    pe.wait_ge(s("kvt_ready"), h + 1)
                    pe.wait_ge(s("bmat_in"), h * 16 + 16)
                    for m in (0, 1):
                        for dh in (0, 1):
                            mm = pe.matmul(bank[5][:, m * D:m * D + D], kvt[:, dh, m * 128:m * 128 + 128], bmat[:, dh, :], start=(dh == 0), stop=(dh == 1))
                    mm.then_inc(s("kvo_ps"), 1)
                    pe.wait_ge(s("wq_in"), h * 16 + 16)
                    pe.wait_ge(s("k_exp"), (h + 1) * NT)
                    pe.wait_ge(s("kvo_ready"), h + 1)

                    def turn(k, i, t):
                        pe.wait_ge(s("q_exp"), h * NT + (t + 1))
                        pe.wait_ge(s("q_ph"), h * NT + less(t, 1))
                        for m in (0, 1):
                            mm = pe.transpose(bank[4 + k % 2][:, m * 128:m * 128 + P], ex[k][:, m * 128:m * 128 + 128], ident[0:P, 0:P])
                        mm.then_inc(s("q_turned"), 1)

                    def attend(k, i, t):
                        pe.wait_ge(s("q_ph"), h * NT + (t + 1))
                        pe.wait_ge(s("q_acc"), h * NT + less(t, 1))
                        n = 0
                        for a, b in ((0, 0), (0, 1), (1, 0)):
                            for m in (0, 1):
                                mm = pe.matmul(bank[6 + k % 2][0:P, 0:D + 1], qt[k][:, a, m, 0:P], kvo[:, b, m, 0:D + 1], start=(n == 0), stop=(n == 5))
                                n += 1
                        mm.then_inc(s("q_att"), 1)

                    pipeline(pe, [(0, features(wc[0], "q")), (2, turn), (4, attend)], NT, 4)

                pe.wait_ge(s("tail_in"), 16 * 11)
                pe.wait_ge(s("q_acc"), H * NT)
                pe.transpose(bank[6][:, 0:2], b1r, ident[0:2, 0:2]).then_inc(s("bias1_ps"), 1)

                def turn_out1(k, i, g):
                    pe.wait_ge(s("out1_ready"), g + 1)
                    pe.wait_ge(s("ot_ready"), less(g, 1))
                    for dh in (0, 1):
                        for j in (0, 1):
                            mm = pe.transpose(bank[k % 2][:, dh * 2 * P + j * P:dh * 2 * P + j * P + P],
                                              o1[k][:, j, dh * 128:dh * 128 + 128], ident[0:P, 0:P])
                    mm.then_inc(s("out1_turned"), 1)

                def ffn1(k, i, g):
                    pe.wait_ge(s("ot_ready"), g + 1)
                    pe.wait_ge(s("ht_ready"), less(g, 1) * 2)
                    for fh in (0, 1):
                        for dh in (0, 1):
                            mm = pe.matmul(bank[2 + k % 2][:, fh * 2 * P:fh * 2 * P + 2 * P], W1s[:, dh, fh * 128:fh * 128 + 128], ot[k % 2][:, dh, :], start=(dh == 0), stop=(dh == 1))
                    mm.then_inc(s("hidden_ps"), 1)

                def ffn2(k, i, g):
                    pe.wait_ge(s("ht_ready"), g * 2 + 2)
                    pe.wait_ge(s("ffn_added"), less(g, 1))
                    for j in (0, 1):
                        for fh in (0, 1):
                            mm = pe.matmul(bank[4 + k % 2][0:P, j * D:j * D + D], ht[k % 2][:, fh, j * P:j * P + P], W2s[:, fh, :], start=(fh == 0), stop=(fh == 1))
                    mm.then_inc(s("ffn_ps"), 1)
                pipeline(pe, [(0, turn_out1), (1, ffn1), (2, ffn2)], NT // 2, 4)

                def turn_xf(k, i, c):
                    pe.wait_ge(s("xf_ready"), c + 1)
                    pe.wait_ge(s("xft_ready"), c * CH)
                    for j in range(CH):
                        for dh in (0, 1):
                            mm = pe.transpose(bank[j][:, dh * P:dh * P + P], xfs[k][:, j, dh * 128:dh * 128 + 128], ident[0:P, 0:P])
                        mm.then_inc(s("xf_turned"), 1)

                def gate_logits(k, i, c):
                    pe.wait_ge(s("logits"), less(c, 1))
                    for j in range(CH):
                        pe.wait_ge(s("xft_ready"), c * CH + (j + 1))
                        for dh in (0, 1):
                            mm = pe.matmul(bank[5 + k][0:P, j * NE:j * NE + NE], xft[j][:, dh, :], gate[:, dh, :], start=(dh == 0), stop=(dh == 1))
                        mm.then_inc(s("lg_ps"), 1)
                pipeline(pe, [(0, turn_xf), (0, gate_logits)], NT // CH)
                pe.wait_ge(s("onehot_ready"), 1)
                one_hot = roh.rearrange("p t e -> p (t e)")
                pe.matmul(bank[0][0:P, 0:NT * NE], upper, one_hot, start=True, stop=True)
                pe.matmul(bank[1][0:P, 0:NT * NE], ones[0:P, 0:P], one_hot, start=True, stop=True).then_inc(s("counts_ps"), 1)


        next_part()

        with nc.Block() as block:
            @block.sync
            def _(sp):
                for k in range(CH):
                    sp.wait_ge(s(f"scattered{k}"), 16 * (NT // CH))

                def load_rows(k, i, t):
                    e, half = (i * 2 + k // 2), k % 2
                    if half == 0:
                        if not isinstance(t, int) or 2 <= t < 2 * NE - 2:
                            sp.wait_ge(s("w2_split"), max(e - 2, 0) if isinstance(t, int) else i * 2 + (k // 2 - 2))
                            w1s, w2s = ws[(k // 2 + 1) % 2]
                            for to, w in ((w1s, w1), (w2s, w2)):
                                sp.dma_start(to, w[ds(e + 1, 1)].rearrange("e (a p) f -> p (e a) f", p=128)).then_inc(s(f"we_in{(k // 2 + 1) % 2}"), 16)
                        sp.wait_ge(s("ye_ready"), less(t, 2) * 2)
                        sp.dma_start(b2b[k // 2], b2[ds(e, 1), :].broadcast_to([P, D])).then_inc(s(f"b2_in{k // 2}"), 16)
                    sp.wait_ge(s("xe_turned"), less(t, 1))
                    sp.dma_start(xe[k % 2], ebuf[0:NE * CB].rearrange("(u j p) d -> u p j d", p=P, j=4)[ds(t, 1)].rearrange("u p j d -> p (u j) d")).then_inc(s(f"xe_in{k % 2}"), 16)

                def store_rows(k, i, t):
                    sp.wait_ge(s("flagged"), t + 1)
                    sp.dma_start(ybuf.rearrange("(u j p) d -> u p j d", p=P, j=4)[ds(t, 1)].rearrange("u p j d -> p (u j) d"), ye).then_inc(s("ye_out"), 16)
                pipeline(sp, [(0, load_rows), (3, store_rows)], 2 * NE, 4)
                ov = out.rearrange("(t p) d -> p t d", p=P)
                with sp.Fori(0, NT // CH) as i:
                    sp.wait_ge(s("out_ready"), i + 1)
                    sp.dma_start(ov[:, ds(i * CH, CH), :], acc[:, ds(i * CH, CH), :]).then_inc(s("out_stored"), 16)
                sp.wait_ge(s("out_stored"), 16 * (NT // CH))

            @block.gpsimd
            def _(pool):
                with pool.Fori(0, NT // CH) as i:
                    for k in range(CH):
                        hold(pool, f"scattered{k}", i * 16)
                        pool.tensor_copy(oslot[k], slot_out[:, ds(i * CH + k, 1)]).then_inc(s("oslot"), 1)
                        hold(pool, "oslot", i * CH + (k + 1))
                        hold(pool, f"xs_ready{k}", i + 1)
                        pool.indirect_dma_start(out=ebuf, out_offset=bass.IndirectOffsetOnAxis(ap=oslot[k], axis=0), in_=xs[k], in_offset=None).then_inc(s(f"scattered{k}"), 16)
                with pool.Fori(1, NE // 2) as i:
                    for c in (0, 1):
                        hold(pool, f"we_in{c}", i * 32)
                        hold(pool, "hid_block", i * 4 * (F // 128) + (2 * c - 2) * (F // 128))
                        split_weights(pool, c, 0, "w1_split", i * 2 + (c - 2))
                        hold(pool, "ye_ps", i * 4 + (2 * c - 2))
                        split_weights(pool, c, 1, "w2_split", i * 2 + (c - 2))
                pool.wait_ge(s("finite"), 2)
                pool.partition_all_reduce(bad[:, 1:2], bad[:, 0:1], P, bass.bass_isa.ReduceOp.add).then_inc(s("bad_all"), 1)
                pool.wait_ge(s("ye_out"), 16 * 2 * NE)
                with pool.Fori(0, NT // CH // 2) as i:
                    for c in (0, 1):
                        hold(pool, f"yg_used{c}", i)
                        for k in range(CH):
                            pool.tensor_copy(islot[c * CH + k], slot_in[:, ds(i * 2 * CH + (c * CH + k), 1)]).then_inc(s("islot"), 1)
                            hold(pool, "islot", i * 2 * CH + (c * CH + k + 1))
                            pool.indirect_dma_start(out=yg[c][:, k, :], out_offset=None, in_=ybuf,
                                                    in_offset=bass.IndirectOffsetOnAxis(ap=islot[c * CH + k], axis=0)).then_inc(s(f"yg_in{c}"), 16)

            @block.vector
            def _(v):
                def per_row(col, t, n=CH):
                    return col[:, ds(t, n)].rearrange("p (t o) -> p t o", o=1).broadcast_to([P, n, D])


                with v.Fori(0, NT // CH) as i:
                    for k in range(CH):
                        v.wait_ge(s(f"scattered{k}"), i * 16)
                        t = i * CH + k
                        v.tensor_scalar(xs[k], acc[:, ds(t, 1), :].rearrange("p t d -> p (t d)"), mean[:, ds(t, 1)], rstd[:, ds(t, 1)], ALU.subtract, ALU.mult).then_inc(s(f"xs_ready{k}"), 1)

                v.wait_ge(s("b1t_ps"), 1)
                v.tensor_copy(b1t.rearrange("p a b -> p (a b)"), bank[7][:, 0:NE * F // 128]).then_inc(s("b1t_ready"), 1)
                def copy_rows(k, i, t):
                    v.wait_ge(s("xe_turned"), t + 1)
                    v.wait_ge(s("hid_block"), less(t, 1) * (F // 128))
                    for dh in (0, 1):
                        v.tensor_copy(xet[k % 2][:, 0, dh, :], bank[dh][:, 0:4 * P]).then_inc(s("xet_hi"), 1)
                    v.wait_ge(s("xet_hi"), t * 2 + 2)
                    for dh in (0, 1):
                        v.tensor_tensor(xet[k % 2][:, 1, dh, :], bank[dh][:, 0:4 * P], xet[k % 2][:, 0, dh, :], ALU.subtract).then_inc(s("xet_ready"), 1)

                def hidden_lo(k, i, t):
                    for fb in range(F // 128):
                        v.wait_ge(s("relu_ready"), t * (F // 128) + (fb + 1))
                        v.tensor_tensor(hid[k % 2][:, 1, fb, :], relus[fb % 2], hid[k % 2][:, 0, fb, :], ALU.subtract).then_inc(s("hid_ready"), 1)

                def add_b2(k, i, t):
                    v.wait_ge(s("ye_ps"), t + 1)
                    v.wait_ge(s(f"b2_in{k // 2}"), i * 16 + 16)
                    v.wait_ge(s("ye_out"), t * 16)
                    for j in (0, 1):
                        v.tensor_tensor(ye[:, 2 * j:2 * j + 2, :], bank[5 + j][0:P, :].rearrange("p (a b) -> p a b", a=2), b2b[k // 2][:, None, :].broadcast_to([P, 2, D]), ALU.add).then_inc(s("ye_ready"), 1)
                    v.wait_ge(s("ye_ready"), t * 2 + 2)
                    v.wait_ge(s("flagged"), t)
                    v.tensor_scalar(junk_y, ye, 0.0, 0.0, ALU.mult, ALU.add, accum_out=flags[:, ds(t, 1)]).then_inc(s("flagged"), 1)
                pipeline(v, [(0, copy_rows), (1, hidden_lo), (2, add_b2)], 2 * NE, 4)
                v.wait_ge(s("flagged"), 2 * NE)
                v.tensor_scalar(flags, flags, 0.0, None, ALU.not_equal).then_inc(s("finite"), 1)
                v.wait_ge(s("finite"), 1)
                v.tensor_reduce(bad[:, 0:1], flags, AX.X, ALU.add).then_inc(s("finite"), 1)
                v.wait_ge(s("bad_all"), 1)
                v.tensor_copy(badi, bad[:, 1:2]).then_inc(s("finite"), 1)
                v.wait_ge(s("finite"), 3)

                v.memset(fill[0], 0.0).then_inc(s("fills"), 1)
                v.memset(fill[1], 10000.0).then_inc(s("fills"), 1)
                v.memset(fill[2], -10000.0).then_inc(s("fills"), 1)
                v.wait_ge(s("fills"), 3)
                any_bad = v.value_load(badi[0:1, 0:1], min_val=0, max_val=2 * NE * P)
                with v.If(any_bad > 0):
                    with v.Fori(0, NT // CH // 2) as i:
                        for k in (0, 1):
                            t, n = i * 2 * CH + k * CH, i * 12 + k * 6
                            v.wait_ge(s(f"yg_in{k}"), i * 16 * CH + 16 * CH)
                            v.tensor_tensor(yg[k], yg[k], per_row(pk, t), ALU.mult).then_inc(s("fin"), 1)
                            v.wait_ge(s("fin"), n + 1)
                            v.tensor_tensor(msk[0], yg[k], yg[k], ALU.not_equal).then_inc(s("fin"), 1)
                            v.tensor_scalar(msk[1], yg[k], 3.4028234e38, None, ALU.is_gt).then_inc(s("fin"), 1)
                            hold(v, "fin", n + 3, "dve")
                            v.copy_predicated(yg[k], msk[1], fill[1][:, None, :].broadcast_to([P, CH, D])).then_inc(s("fin"), 1)
                            hold(v, "fin", n + 4, "dve")
                            v.copy_predicated(yg[k], msk[0], fill[0][:, None, :].broadcast_to([P, CH, D])).then_inc(s("fin"), 1)
                            v.wait_ge(s("fin"), n + 5)
                            v.tensor_scalar(msk[1], yg[k], -3.4028234e38, None, ALU.is_lt).then_inc(s("fin"), 1)
                            hold(v, "fin", n + 6, "dve")
                            v.copy_predicated(yg[k], msk[1], fill[2][:, None, :].broadcast_to([P, CH, D])).then_inc(s("fin2"), 1)
                            v.wait_ge(s("fin2"), i * 2 + (k + 1))
                            at = acc[:, ds(t, CH), :]
                            v.tensor_tensor(at, at, yg[k], ALU.add).then_inc(s(f"yg_used{k}"), 1)
                            v.wait_ge(s(f"yg_used{k}"), i + 1)
                            v.sem_inc(s("out_ready"), 1)
                with v.If(any_bad < 1):
                    with v.Fori(0, NT // CH // 2) as i:
                        for k in (0, 1):
                            t = i * 2 * CH + k * CH
                            v.wait_ge(s(f"yg_in{k}"), i * 16 * CH + 16 * CH)
                            for j in range(CH):
                                at = acc[:, ds(t + j, 1), :].rearrange("p t d -> p (t d)")
                                v.scalar_tensor_tensor(at, yg[k][:, j, :], pk[:, ds(t + j, 1)], at, ALU.mult, ALU.add).then_inc(s("added_up"), 1)
                            v.wait_ge(s("added_up"), t + CH)
                            v.sem_inc(s(f"yg_used{k}"), 1)
                            v.sem_inc(s("out_ready"), 1)

            @block.scalar
            def _(a):
                for k in range(CH):
                    a.wait_ge(s(f"scattered{k}"), 16 * (NT // CH))
                a.dma_start(b1rows, b1.rearrange("e (a p) -> (e a) p", p=128)).then_inc(s("b1_in"), 16)
                a.wait_ge(s("b1t_ready"), 1)

                def hidden(k, i, t):
                    a.wait_ge(s("ye_ps"), less(t, 1))
                    for fb in range(F // 128):
                        hold(a, "hid_block", t * (F // 128) + (fb + 1), "act")
                        b1c = b1t[:, ds(i * 2 + k // 2, 1), fb:fb + 1].rearrange("p a b -> p (a b)")
                        a.activation(hid[k % 2][:, 0, fb, :], bank[2 + fb % 3][:, 0:4 * P], ACT.Relu, bias=b1c).then_inc(s("relu_hi"), 1)
                        if fb >= 2:
                            hold(a, "hid_ready", t * (F // 128) + (fb - 1), "act")
                        else:
                            hold(a, "hid_ready", less(t, 1) * (F // 128) + (F // 128 - 1 + fb if not isinstance(t, int) or t > 0 else 0), "act")
                        a.activation(relus[fb % 2], bank[2 + fb % 3][:, 0:4 * P], ACT.Relu, bias=b1c).then_inc(s("relu_ready"), 1)
                pipeline(a, [(0, hidden)], 2 * NE, 4)

            @block.tensor
            def _(pe):
                pe.wait_ge(s("b1_in"), 16)
                pe.transpose(bank[7][:, 0:NE * F // 128], b1rows, ident[0:NE * F // 128, 0:NE * F // 128]).then_inc(s("b1t_ps"), 1)

                def turn_rows(k, i, t):
                    pe.wait_ge(s(f"xe_in{k % 2}"), i * 32 + (k // 2 * 16 + 16))
                    pe.wait_ge(s("xet_ready"), 2 * t)
                    for dh in (0, 1):
                        for j in range(4):
                            mm = pe.transpose(bank[dh][:, j * P:j * P + P], xe[k % 2][:, j, dh * 128:dh * 128 + 128], ident[0:P, 0:P])
                    mm.then_inc(s("xe_turned"), 1)

                def expert1(k, i, t):
                    n_used = pe.value_load(used[0:1, ds(i * 2 + k // 2, 1), k % 2:k % 2 + 1], min_val=1, max_val=4)
                    pe.wait_ge(s("xet_ready"), 2 * t + 2)
                    if not isinstance(t, int) or t >= 4:
                        pe.wait_ge(s("w1_split"), i * 2 + (k // 2 - 1))
                    def blocks(cols):
                        for fb in range(F // 128):
                            if fb >= 3:
                                pe.wait_ge(s("relu_ready"), t * (F // 128) + (fb - 2))
                            else:
                                pe.wait_ge(s("relu_ready"), t * (F // 128))
                            n = 0
                            for xh, wh in ((0, 0), (1, 0), (0, 1)):
                                for dh in (0, 1):
                                    mm = pe.matmul(bank[2 + fb % 3][:, 0:cols], we[k // 2][0][:, wh, dh, fb * 128:fb * 128 + 128], xet[k % 2][:, xh, dh, 0:cols], start=(n == 0), stop=(n == 5))
                                    n += 1
                            mm.then_inc(s("hid_block"), 1)
                    with pe.If(n_used > 3):
                        blocks(4 * P)
                    with pe.If(n_used == 3):
                        blocks(3 * P)
                    with pe.If(n_used < 3):
                        blocks(2 * P)

                def expert2(k, i, t):
                    n_used = pe.value_load(used[0:1, ds(i * 2 + k // 2, 1), k % 2:k % 2 + 1], min_val=1, max_val=4)
                    if not isinstance(t, int) or t >= 4:
                        pe.wait_ge(s("w2_split"), i * 2 + (k // 2 - 1))
                    pe.wait_ge(s("hid_ready"), (t + 1) * (F // 128))
                    pe.wait_ge(s("ye_ready"), 2 * t)
                    def out_tile(j):
                        n = 0
                        for fb in range(F // 128):
                            for hh, wh in ((0, 0), (0, 1), (1, 0)):
                                mm = pe.matmul(bank[5 + j // 2][0:P, j % 2 * D:j % 2 * D + D], hid[k % 2][:, hh, fb, j * P:j * P + P], we[k // 2][1][:, wh, fb, :],
                                               start=(n == 0), stop=(n == 3 * F // 128 - 1))
                                n += 1
                        return mm
                    for j in (3, 2, 1):
                        with pe.If(n_used > j):
                            out_tile(j)
                    out_tile(0).then_inc(s("ye_ps"), 1)
                pipeline(pe, [(0, turn_rows), (1, expert1), (2, expert2)], 2 * NE, 4)


_INS = ["x", "src", "dst", "L0_gnn_W", "L0_gnn_att", "L0_gnn_b", "L0_mix_Wq", "L0_mix_bq", "L0_mix_Wk", "L0_mix_bk",
        "L0_mix_Wv", "L0_mix_bv", "L0_mix_Wo", "L0_mix_bo", "L0_mix_proj", "L0_mix_W1", "L0_mix_bias1", "L0_mix_W2",
        "L0_mix_bias2", "L0_mix_g1", "L0_mix_beta1", "L0_mix_g2", "L0_mix_beta2", "L0_ffn_gate_w", "L0_ffn_gate_b",
        "L0_ffn_w1", "L0_ffn_b1", "L0_ffn_w2", "L0_ffn_b2"]


def kernel(**inputs):
    import numpy as _np
    import concourse.bacc as _bacc
    from concourse import mybir as _mybir
    from concourse.bass_utils import run_bass_kernel_spmd as _run

    nc = _bacc.Bacc("TRN2", target_bir_lowering=False, num_devices=1)
    arrays, args = {}, []
    for name in _INS:
        a = _np.ascontiguousarray(inputs[name])
        arrays[f"in_{name}_dram"] = a
        args.append(nc.dram_tensor(f"in_{name}_dram", a.shape, _mybir.dt.from_np(a.dtype), kind="ExternalInput").ap())
    args.append(nc.dram_tensor("out_0_dram", (N, D), F32, kind="ExternalOutput").ap())
    gps_layer(nc, *args)
    r = _run(nc, [arrays], core_ids=[0])
    return r.results[0]["out_0_dram"]
```
